# Optimizing a Trainium2 kernel written in Bass

```python
import numpy as np
import jax
import jax.numpy as jnp

def _softmax(x, axis=-1):
    return jax.nn.softmax(x, axis=axis)

def _gelu(x):
    return jax.nn.gelu(x, approximate=True)

def _silu(x):
    return jax.nn.silu(x)

def _sigmoid(x):
    return jax.nn.sigmoid(x)

def _layernorm(x, axis=-1, eps=1e-05):
    m = jnp.mean(x, axis=axis, keepdims=True)
    v = jnp.var(x, axis=axis, keepdims=True)
    return (x - m) / jnp.sqrt(v + eps)

def _scatter_add(tgt, idx, src, axis=0):
    return tgt.at[idx].add(src)

def _segment_sum(src, seg, n):
    return jax.ops.segment_sum(src, seg, n)
kernel_name = 'mk_flamingo_gated_d4_seqx_r8_df3f8c'

def setup_inputs(seed: int=0):
    np.random.seed(seed)
    _w = jnp.asarray

    def _rec_inputs():
        import jax
        import jax.numpy as jnp
        _rk = jax.random.key(seed)
        x = -0.0003929 + 0.9999 * jax.random.normal(jax.random.fold_in(_rk, 1), (4, 256, 128), jnp.float32)
        _lenS = 256 - jax.random.randint(jax.random.fold_in(_rk, 7), (4,), 0, max(1, 256 // 4) + 1, jnp.int32)
        _lenS2 = 64 - jax.random.randint(jax.random.fold_in(_rk, 8), (4,), 0, max(1, 64 // 4) + 1, jnp.int32)
        _ctx_1024P = jax.random.normal(jax.random.fold_in(_rk, 11), (4, 16, 128), jnp.float32)
        _ctx_1024c = jax.random.dirichlet(jax.random.fold_in(_rk, 511), 0.3 * jnp.ones((16,), jnp.float32), (4, 64))
        _ctx_1024t = jnp.einsum('bsk,bkd->bsd', _ctx_1024c, _ctx_1024P)
        _ctx_1024t = _ctx_1024t * jax.lax.rsqrt(jnp.mean(jnp.square(_ctx_1024t)) + 1e-12) * 0.953939
        ctx_1024 = 2.81802e-05 + 1.00001 * (_ctx_1024t + 0.3 * jax.random.normal(jax.random.fold_in(_rk, 611), (4, 64, 128), jnp.float32))
        _validS = jnp.arange(256)[None, :] < _lenS[:, None]
        _validS2 = jnp.arange(64)[None, :] < _lenS2[:, None]
        _causal = jnp.tril(jnp.ones((256, 256), dtype=bool))
        mask_BxS2_ik0 = jnp.where(jnp.broadcast_to(_validS2[:, :], (4, 64)), 0, 1).astype(jnp.int32)
        _g = jax.random.normal(jax.random.fold_in(_rk, 9001), (2, 4), jnp.float32)
        _g = jnp.sign(_g) * jnp.maximum(jnp.abs(_g), 1.0) + (_g == 0) * 1.0
        g_xattn = _g[0]
        g_ffn = _g[1]
        return (x, ctx_1024, mask_BxS2_ik0, g_xattn, g_ffn)
    x, ctx_1024, mask_BxS2_ik0, g_xattn, g_ffn = _rec_inputs()

    def _L0_xattn_setup():
        import jax, jax.numpy as jnp
        import numpy as np
        B, T, C, H = (4, 512, 128, 16)
        D = C // H

        def _heads(t):
            b, n, c = t.shape
            return t.reshape(b, n, H, D).transpose(0, 2, 1, 3)
        key = jax.random.key(seed)
        ks = jax.random.split(key, 10)
        s = 1.0 / np.sqrt(C)
        return {'x': jax.random.normal(ks[0], (B, T, C), jnp.float32), 'y': jax.random.normal(ks[1], (B, T, C), jnp.float32), 'Wq': jax.random.normal(ks[2], (C, C), jnp.float32) * s, 'bq': jnp.zeros((C,), jnp.float32), 'Wk': jax.random.normal(ks[3], (C, C), jnp.float32) * s, 'bk': jnp.zeros((C,), jnp.float32), 'Wv': jax.random.normal(ks[4], (C, C), jnp.float32) * s, 'bv': jnp.zeros((C,), jnp.float32), 'Wp': jax.random.normal(ks[5], (C, C), jnp.float32) * s, 'bp': jnp.zeros((C,), jnp.float32)}
    _L0_xattn_all = _L0_xattn_setup()
    _L0_xattn_in = {k: v for k, v in _L0_xattn_all.items() if k in ('Wq', 'bq', 'Wk', 'bk', 'Wv', 'bv', 'Wp', 'bp')}
    del _L0_xattn_all

    def _L0_ffn_setup():
        import jax, jax.numpy as jnp
        import numpy as np
        E, K, H, F = (64, 6, 128, 64)
        SHARED_F = 256
        B, S = (1, 256)
        T = B * S
        CAP = 2 * ((T * K + E - 1) // E)
        key = jax.random.key(seed)
        ks = jax.random.split(key, 6)
        s = 0.05
        return {'hidden_states': jax.random.normal(ks[0], (B, S, H), jnp.float32), 'router_weight': jax.random.normal(ks[1], (E, H), jnp.float32) * s, 'expert_bias': jnp.zeros((E,), jnp.float32), 'w1': jax.random.normal(ks[2], (E, H, F), jnp.float32) * s, 'w2': jax.random.normal(ks[3], (E, F, H), jnp.float32) * s, 'sw1': jax.random.normal(ks[4], (SHARED_F, H), jnp.float32) * s, 'sw2': jax.random.normal(ks[5], (H, SHARED_F), jnp.float32) * s}
    _L0_ffn_all = _L0_ffn_setup()
    _L0_ffn_in = {k: v for k, v in _L0_ffn_all.items() if k in ('router_weight', 'expert_bias', 'w1', 'w2', 'sw1', 'sw2')}
    del _L0_ffn_all

    def _L1_xattn_setup():
        import jax, jax.numpy as jnp
        import numpy as np
        D_MODEL = 128
        N_HEADS = 16
        HEAD_DIM = D_MODEL // N_HEADS
        key = jax.random.key(seed)
        k1, k2, k3, k4, k5, k6 = jax.random.split(key, 6)
        B, T_q, T_kv = (4, 128, 512)
        s = 1.0 / np.sqrt(D_MODEL)
        return {'query': jax.random.normal(k1, (B, T_q, D_MODEL), dtype=jnp.float32), 'kv_source': jax.random.normal(k2, (B, T_kv, D_MODEL), dtype=jnp.float32), 'w_q': jax.random.normal(k3, (D_MODEL, D_MODEL), dtype=jnp.float32) * s, 'w_k': jax.random.normal(k4, (D_MODEL, D_MODEL), dtype=jnp.float32) * s, 'w_v': jax.random.normal(k5, (D_MODEL, D_MODEL), dtype=jnp.float32) * s, 'w_o': jax.random.normal(k6, (D_MODEL, D_MODEL), dtype=jnp.float32) * s}
    _L1_xattn_all = _L1_xattn_setup()
    _L1_xattn_in = {k: v for k, v in _L1_xattn_all.items() if k in ('w_q', 'w_k', 'w_v', 'w_o')}
    del _L1_xattn_all

    def _L1_ffn_setup():
        import jax, jax.numpy as jnp
        import numpy as np
        HIDDEN = 128
        HEAD_DIM = 64
        N_EXPERTS = 16
        MIN_EXPERTS = 2
        B, T = (4, 256)

        def _normalize(x, axis):
            n = jnp.sqrt(jnp.sum(x * x, axis=axis, keepdims=True))
            return x / jnp.maximum(n, 1e-12)

        def _ste(x):
            hard = jax.lax.stop_gradient((x > 0).astype(x.dtype))
            return hard + x - jax.lax.stop_gradient(x)

        def _gating(hidden_states, sim_matrix, gates):
            b, t, c = hidden_states.shape
            flat = hidden_states.reshape(b * t, c)
            logits = _normalize(flat, -1) @ _normalize(sim_matrix, 0) - jax.nn.sigmoid(gates)
            gated = jax.nn.relu(logits)
            mask = _ste(gated)
            inactive = jnp.sum(mask, axis=1) == 0
            _, fb_idx = jax.lax.top_k(logits, MIN_EXPERTS)
            fb = jnp.zeros_like(mask).at[jnp.arange(b * t)[:, None], fb_idx].set(1.0)
            fb_applied = inactive[:, None] & (fb > 0)
            mask = jnp.where(fb_applied, 1.0, mask)
            masked_logits = jnp.where(mask > 0, gated, -jnp.inf)
            return jax.nn.softmax(masked_logits, axis=-1).reshape(b, t, -1)
        key = jax.random.key(seed)
        ks = jax.random.split(key, 6)
        xav_qkv = float(np.sqrt(6.0 / (HIDDEN + HEAD_DIM)))
        return {'hidden_states': jax.random.normal(ks[0], (B, T, HIDDEN), dtype=jnp.float32), 'sim_matrix': jax.random.normal(ks[1], (HIDDEN, N_EXPERTS), dtype=jnp.float32), 'gates': jnp.zeros((N_EXPERTS,), dtype=jnp.float32), 'q_proj': jax.random.uniform(ks[2], (N_EXPERTS, HIDDEN, HEAD_DIM), jnp.float32, -xav_qkv, xav_qkv), 'k_proj': jax.random.uniform(ks[3], (N_EXPERTS, HIDDEN, HEAD_DIM), jnp.float32, -xav_qkv, xav_qkv), 'v_proj': jax.random.uniform(ks[4], (N_EXPERTS, HIDDEN, HEAD_DIM), jnp.float32, -xav_qkv, xav_qkv), 'o_proj': jax.random.uniform(ks[5], (N_EXPERTS, HEAD_DIM, HIDDEN), jnp.float32, -xav_qkv, xav_qkv)}
    _L1_ffn_all = _L1_ffn_setup()
    _L1_ffn_in = {k: v for k, v in _L1_ffn_all.items() if k in ('sim_matrix', 'gates', 'q_proj', 'k_proj', 'v_proj', 'o_proj')}
    del _L1_ffn_all

    def _L2_xattn_setup():
        import jax, jax.numpy as jnp
        import numpy as np
        HEADS = 16
        DIM_Q = 128
        DIM_KV = 128
        INNER = 128
        key = jax.random.key(seed)
        k1, k2, k3, k4, k5, k6, k7 = jax.random.split(key, 7)
        B, Lq, Lkv = (2, 256, 512)
        H = jax.random.normal(k1, (B, Lq, DIM_Q), dtype=jnp.float32)
        T = jax.random.normal(k2, (B, Lkv, DIM_KV), dtype=jnp.float32)
        mask = jax.random.randint(k3, (B, Lkv), 0, 2, dtype=jnp.int32)
        s = 0.02
        Wq = jax.random.normal(k4, (DIM_Q, INNER), dtype=jnp.float32) * s
        Wk = jax.random.normal(k5, (DIM_KV, INNER), dtype=jnp.float32) * s
        Wv = jax.random.normal(k6, (DIM_KV, INNER), dtype=jnp.float32) * s
        Wo = jax.random.normal(k7, (INNER, DIM_Q), dtype=jnp.float32) * s
        return {'H': H, 'T': T, 'mask': mask, 'Wq': Wq, 'Wk': Wk, 'Wv': Wv, 'Wo': Wo}
    _L2_xattn_all = _L2_xattn_setup()
    _L2_xattn_in = {k: v for k, v in _L2_xattn_all.items() if k in ('Wq', 'Wk', 'Wv', 'Wo')}
    del _L2_xattn_all

    def _L2_ffn_setup():
        import jax, jax.numpy as jnp
        import numpy as np
        E = 8
        K = 2
        CAPACITY_FACTOR = 1.25
        key = jax.random.key(seed)
        ks = jax.random.split(key, 4)
        B, T, C, H = (8, 256, 128, 512)
        x = jax.random.normal(ks[0], (B, T, C), jnp.float32)
        Wr = jax.random.normal(ks[1], (C, E), jnp.float32) * 0.02
        br = jnp.zeros((E,), jnp.float32)
        W1 = jax.random.normal(ks[2], (E, C, H), jnp.float32) * 0.02
        b1 = jnp.zeros((E, H), jnp.float32)
        W2 = jax.random.normal(ks[3], (E, H, C), jnp.float32) * 0.02
        b2 = jnp.zeros((E, C), jnp.float32)
        return {'x': x, 'Wr': Wr, 'br': br, 'W1': W1, 'b1': b1, 'W2': W2, 'b2': b2}
    _L2_ffn_all = _L2_ffn_setup()
    _L2_ffn_in = {k: v for k, v in _L2_ffn_all.items() if k in ('Wr', 'br', 'W1', 'b1', 'W2', 'b2')}
    del _L2_ffn_all

    def _L3_xattn_setup():
        import jax, jax.numpy as jnp
        import numpy as np
        D_MODEL = 128
        N_HEADS = 16
        N_KV_HEADS = 4
        HEAD_DIM = 64
        key = jax.random.key(seed)
        ks = jax.random.split(key, 6)
        B, Tq, Tkv = (2, 256, 256)
        query = jax.random.normal(ks[0], (B, Tq, D_MODEL), dtype=jnp.float32)
        context = jax.random.normal(ks[1], (B, Tkv, D_MODEL), dtype=jnp.float32)
        s = 1.0 / np.sqrt(D_MODEL)
        Wq = jax.random.normal(ks[2], (N_HEADS * HEAD_DIM, D_MODEL), dtype=jnp.float32) * s
        Wk = jax.random.normal(ks[3], (N_KV_HEADS * HEAD_DIM, D_MODEL), dtype=jnp.float32) * s
        Wv = jax.random.normal(ks[4], (N_KV_HEADS * HEAD_DIM, D_MODEL), dtype=jnp.float32) * s
        Wo = jax.random.normal(ks[5], (D_MODEL, N_HEADS * HEAD_DIM), dtype=jnp.float32) * s
        return {'query': query, 'context': context, 'Wq': Wq, 'Wk': Wk, 'Wv': Wv, 'Wo': Wo}
    _L3_xattn_all = _L3_xattn_setup()
    _L3_xattn_in = {k: v for k, v in _L3_xattn_all.items() if k in ('Wq', 'Wk', 'Wv', 'Wo')}
    del _L3_xattn_all

    def _L3_ffn_setup():
        import jax, jax.numpy as jnp
        import numpy as np
        DIM = 128
        HIDDEN = 384
        SCALE = 1.0 / 127.0

        def _dequant(w_int, dtype):
            return w_int.astype(dtype) * jnp.asarray(SCALE, dtype)
        key = jax.random.key(seed)
        k_x, k_g, k_u, k_d = jax.random.split(key, 4)
        x = jax.random.normal(k_x, (4, 256, DIM), dtype=jnp.float32)
        w_gate = jax.random.randint(k_g, (HIDDEN, DIM), -127, 128, dtype=jnp.int32)
        w_up = jax.random.randint(k_u, (HIDDEN, DIM), -127, 128, dtype=jnp.int32)
        w_down = jax.random.randint(k_d, (DIM, HIDDEN), -127, 128, dtype=jnp.int32)
        return {'x': x, 'w_gate': w_gate, 'w_up': w_up, 'w_down': w_down}
    _L3_ffn_all = _L3_ffn_setup()
    _L3_ffn_in = {k: v for k, v in _L3_ffn_all.items() if k in ('w_gate', 'w_up', 'w_down')}
    del _L3_ffn_all
    return {'x': x, 'ctx_1024': ctx_1024, 'mask_BxS2_ik0': mask_BxS2_ik0, 'g_xattn': g_xattn, 'g_ffn': g_ffn, 'L0_xattn_Wq': _L0_xattn_in['Wq'], 'L0_xattn_bq': _L0_xattn_in['bq'], 'L0_xattn_Wk': _L0_xattn_in['Wk'], 'L0_xattn_bk': _L0_xattn_in['bk'], 'L0_xattn_Wv': _L0_xattn_in['Wv'], 'L0_xattn_bv': _L0_xattn_in['bv'], 'L0_xattn_Wp': _L0_xattn_in['Wp'], 'L0_xattn_bp': _L0_xattn_in['bp'], 'L0_ffn_router_weight': _L0_ffn_in['router_weight'], 'L0_ffn_expert_bias': _L0_ffn_in['expert_bias'], 'L0_ffn_w1': _L0_ffn_in['w1'], 'L0_ffn_w2': _L0_ffn_in['w2'], 'L0_ffn_sw1': _L0_ffn_in['sw1'], 'L0_ffn_sw2': _L0_ffn_in['sw2'], 'L1_xattn_w_q': _L1_xattn_in['w_q'], 'L1_xattn_w_k': _L1_xattn_in['w_k'], 'L1_xattn_w_v': _L1_xattn_in['w_v'], 'L1_xattn_w_o': _L1_xattn_in['w_o'], 'L1_ffn_sim_matrix': _L1_ffn_in['sim_matrix'], 'L1_ffn_gates': _L1_ffn_in['gates'], 'L1_ffn_q_proj': _L1_ffn_in['q_proj'], 'L1_ffn_k_proj': _L1_ffn_in['k_proj'], 'L1_ffn_v_proj': _L1_ffn_in['v_proj'], 'L1_ffn_o_proj': _L1_ffn_in['o_proj'], 'L2_xattn_Wq': _L2_xattn_in['Wq'], 'L2_xattn_Wk': _L2_xattn_in['Wk'], 'L2_xattn_Wv': _L2_xattn_in['Wv'], 'L2_xattn_Wo': _L2_xattn_in['Wo'], 'L2_ffn_Wr': _L2_ffn_in['Wr'], 'L2_ffn_br': _L2_ffn_in['br'], 'L2_ffn_W1': _L2_ffn_in['W1'], 'L2_ffn_b1': _L2_ffn_in['b1'], 'L2_ffn_W2': _L2_ffn_in['W2'], 'L2_ffn_b2': _L2_ffn_in['b2'], 'L3_xattn_Wq': _L3_xattn_in['Wq'], 'L3_xattn_Wk': _L3_xattn_in['Wk'], 'L3_xattn_Wv': _L3_xattn_in['Wv'], 'L3_xattn_Wo': _L3_xattn_in['Wo'], 'L3_ffn_w_gate': _L3_ffn_in['w_gate'], 'L3_ffn_w_up': _L3_ffn_in['w_up'], 'L3_ffn_w_down': _L3_ffn_in['w_down']}

def reference(x, ctx_1024, mask_BxS2_ik0, g_xattn, g_ffn, L0_xattn_Wq, L0_xattn_bq, L0_xattn_Wk, L0_xattn_bk, L0_xattn_Wv, L0_xattn_bv, L0_xattn_Wp, L0_xattn_bp, L0_ffn_router_weight, L0_ffn_expert_bias, L0_ffn_w1, L0_ffn_w2, L0_ffn_sw1, L0_ffn_sw2, L1_xattn_w_q, L1_xattn_w_k, L1_xattn_w_v, L1_xattn_w_o, L1_ffn_sim_matrix, L1_ffn_gates, L1_ffn_q_proj, L1_ffn_k_proj, L1_ffn_v_proj, L1_ffn_o_proj, L2_xattn_Wq, L2_xattn_Wk, L2_xattn_Wv, L2_xattn_Wo, L2_ffn_Wr, L2_ffn_br, L2_ffn_W1, L2_ffn_b1, L2_ffn_W2, L2_ffn_b2, L3_xattn_Wq, L3_xattn_Wk, L3_xattn_Wv, L3_xattn_Wo, L3_ffn_w_gate, L3_ffn_w_up, L3_ffn_w_down):
    import jax
    import jax.numpy as jnp

    def _L0_xattn_ref(x, y, Wq, bq, Wk, bk, Wv, bv, Wp, bp):
        import jax, jax.numpy as jnp
        import numpy as np
        B, T, C, H = (4, 512, 128, 16)
        D = C // H

        def _heads(t):
            b, n, c = t.shape
            return t.reshape(b, n, H, D).transpose(0, 2, 1, 3)
        q = jax.nn.softmax(_heads(x @ Wq.T + bq), axis=-1)
        k = jax.nn.softmax(_heads(y @ Wk.T + bk), axis=-1)
        v = _heads(y @ Wv.T + bv)
        k_cumsum = jnp.sum(k, axis=-2, keepdims=True)
        D_inv = 1.0 / jnp.sum(q * k_cumsum, axis=-1, keepdims=True)
        kv = jnp.einsum('bhnd,bhne->bhde', k, v)
        out = q + jnp.einsum('bhnd,bhde->bhne', q, kv) * D_inv
        out = out.transpose(0, 2, 1, 3).reshape(x.shape[0], x.shape[1], C)
        return out @ Wp.T + bp

    def _L0_ffn_ref(hidden_states, router_weight, expert_bias, w1, w2, sw1, sw2):
        import jax, jax.numpy as jnp
        import numpy as np
        E, K, H, F = (64, 6, 128, 64)
        SHARED_F = 256
        B, S = (1, 256)
        T = B * S
        CAP = 2 * ((T * K + E - 1) // E)
        b, s, h = hidden_states.shape
        x = hidden_states.reshape(-1, h)
        t = x.shape[0]
        logits = x @ router_weight.T
        scores = jax.nn.sigmoid(logits)
        _, top_idx = jax.lax.top_k(scores + expert_bias[None, :], K)
        top_scores = jnp.take_along_axis(scores, top_idx, axis=1)
        probs = top_scores / (jnp.sum(top_scores, axis=-1, keepdims=True) + 1e-20)
        flat_e = top_idx.reshape(-1)
        order = jnp.argsort(flat_e)
        sorted_e = flat_e[order]
        token_of = order // K
        counts = jnp.bincount(flat_e, length=E)
        offsets = jnp.cumsum(counts) - counts
        pos = jnp.arange(t * K) - offsets[sorted_e]
        valid = pos < CAP
        slot = jnp.where(valid, sorted_e * CAP + pos, E * CAP)
        xs = jnp.zeros((E * CAP + 1, h), x.dtype).at[slot].set(x[token_of])
        xs = xs[:-1].reshape(E, CAP, h)
        hmid = jax.nn.gelu(jnp.einsum('ech,ehf->ecf', xs, w1), approximate=True)
        y = jnp.einsum('ecf,efh->ech', hmid, w2).reshape(E * CAP, h)
        pair_w = jnp.where(valid, probs.reshape(-1)[order], 0.0)
        y_pair = y[jnp.minimum(slot, E * CAP - 1)] * pair_w[:, None]
        out = jnp.zeros((t, h), x.dtype).at[token_of].add(y_pair)
        shared = jax.nn.gelu(x @ sw1.T, approximate=True) @ sw2.T
        return (out + shared).reshape(b, s, h)

    def _L1_xattn_ref(query, kv_source, w_q, w_k, w_v, w_o):
        import jax, jax.numpy as jnp
        import numpy as np
        D_MODEL = 128
        N_HEADS = 16
        HEAD_DIM = D_MODEL // N_HEADS
        B, T_q, _ = query.shape
        T_kv = kv_source.shape[1]
        q = (query @ w_q.T).reshape(B, T_q, N_HEADS, HEAD_DIM)
        k = (kv_source @ w_k.T).reshape(B, T_kv, N_HEADS, HEAD_DIM)
        v = (kv_source @ w_v.T).reshape(B, T_kv, N_HEADS, HEAD_DIM)
        scale = HEAD_DIM ** (-0.5)
        attn = jax.nn.softmax(jnp.einsum('bqhd,bkhd->bhqk', q, k) * scale, axis=-1)
        out = jnp.einsum('bhqk,bkhd->bqhd', attn, v).reshape(B, T_q, D_MODEL)
        return out @ w_o.T

    def _L1_ffn_ref(hidden_states, sim_matrix, gates, q_proj, k_proj, v_proj, o_proj):
        import jax, jax.numpy as jnp
        import numpy as np
        HIDDEN = 128
        HEAD_DIM = 64
        N_EXPERTS = 16
        MIN_EXPERTS = 2
        B, T = (4, 256)

        def _normalize(x, axis):
            n = jnp.sqrt(jnp.sum(x * x, axis=axis, keepdims=True))
            return x / jnp.maximum(n, 1e-12)

        def _ste(x):
            hard = jax.lax.stop_gradient((x > 0).astype(x.dtype))
            return hard + x - jax.lax.stop_gradient(x)

        def _gating(hidden_states, sim_matrix, gates):
            b, t, c = hidden_states.shape
            flat = hidden_states.reshape(b * t, c)
            logits = _normalize(flat, -1) @ _normalize(sim_matrix, 0) - jax.nn.sigmoid(gates)
            gated = jax.nn.relu(logits)
            mask = _ste(gated)
            inactive = jnp.sum(mask, axis=1) == 0
            _, fb_idx = jax.lax.top_k(logits, MIN_EXPERTS)
            fb = jnp.zeros_like(mask).at[jnp.arange(b * t)[:, None], fb_idx].set(1.0)
            fb_applied = inactive[:, None] & (fb > 0)
            mask = jnp.where(fb_applied, 1.0, mask)
            masked_logits = jnp.where(mask > 0, gated, -jnp.inf)
            return jax.nn.softmax(masked_logits, axis=-1).reshape(b, t, -1)
        b, t, c = hidden_states.shape
        rw = _gating(hidden_states, sim_matrix, gates)
        q = jnp.einsum('bte,bted->btd', rw, jnp.einsum('btc,ecd->bted', hidden_states, q_proj))
        k = jnp.einsum('bte,bted->btd', rw, jnp.einsum('btc,ecd->bted', hidden_states, k_proj))
        v = jnp.einsum('bte,bted->btd', rw, jnp.einsum('btc,ecd->bted', hidden_states, v_proj))
        scale = 1.0 / jnp.sqrt(jnp.asarray(HEAD_DIM, dtype=q.dtype))
        scores = jnp.einsum('bqd,bkd->bqk', q, k) * scale
        causal = jnp.tril(jnp.ones((t, t), dtype=bool))
        scores = jnp.where(causal, scores, -jnp.inf)
        attn = jnp.einsum('bqk,bkd->bqd', jax.nn.softmax(scores, axis=-1), v)
        mixed = attn[:, :, None, :] * rw[..., None]
        return jnp.einsum('bted,edc->btc', mixed, o_proj)

    def _L2_xattn_ref(H, T, mask, Wq, Wk, Wv, Wo):
        import jax, jax.numpy as jnp
        import numpy as np
        HEADS = 16
        DIM_Q = 128
        DIM_KV = 128
        INNER = 128
        B, Lq, _ = H.shape
        Lkv = T.shape[1]
        dph = INNER // HEADS

        def shape(x, L):
            return x.reshape(B, L, HEADS, dph).transpose(0, 2, 1, 3)
        q = shape(H @ Wq, Lq) * dph ** (-0.5)
        k = shape(T @ Wk, Lkv)
        v = shape(T @ Wv, Lkv)
        scores = jnp.einsum('bhqd,bhkd->bhqk', q, k)
        ext = (1.0 - mask.astype(scores.dtype))[:, None, None, :] * jnp.finfo(scores.dtype).min
        scores = scores + ext
        attn = jax.nn.softmax(scores.astype(jnp.float32), axis=-1).astype(scores.dtype)
        out = jnp.einsum('bhqk,bhkd->bhqd', attn, v)
        out = out.transpose(0, 2, 1, 3).reshape(B, Lq, INNER)
        return out @ Wo

    def _L2_ffn_ref(x, Wr, br, W1, b1, W2, b2):
        import jax, jax.numpy as jnp
        import numpy as np
        E = 8
        K = 2
        CAPACITY_FACTOR = 1.25
        B, T, C = x.shape
        cap = max(1, int(T / E * CAPACITY_FACTOR))
        probs = jax.nn.softmax(x @ Wr + br, axis=-1)
        topk_p, topk_e = jax.lax.top_k(probs, K)
        e_flat = topk_e.reshape(B, T * K)
        p_flat = topk_p.reshape(B, T * K)
        oh = jax.nn.one_hot(e_flat, E, dtype=jnp.int32)
        pos_all = jnp.cumsum(oh, axis=1) - oh
        pos = jnp.take_along_axis(pos_all, e_flat[:, :, None], axis=2)[:, :, 0]
        keep = pos < cap
        b_idx = jnp.arange(B)[:, None]
        flat_idx = (e_flat * B + b_idx) * cap + jnp.minimum(pos, cap - 1)
        x_rep = jnp.broadcast_to(x[:, :, None, :], (B, T, K, C)).reshape(B, T * K, C)
        buf = jnp.zeros((E * B * cap, C), x.dtype).at[flat_idx.reshape(-1)].add((x_rep * keep[:, :, None].astype(x.dtype)).reshape(-1, C))
        buf = buf.reshape(E, B * cap, C)
        h = jax.nn.relu(jnp.einsum('enc,ech->enh', buf, W1) + b1[:, None, :])
        y = jnp.einsum('enh,ehc->enc', h, W2) + b2[:, None, :]
        y_tok = y.reshape(E * B * cap, C)[flat_idx.reshape(-1)].reshape(B, T * K, C)
        y_tok = y_tok * (p_flat * keep.astype(x.dtype))[:, :, None]
        return y_tok.reshape(B, T, K, C).sum(axis=2)

    def _L3_xattn_ref(query, context, Wq, Wk, Wv, Wo):
        import jax, jax.numpy as jnp
        import numpy as np
        D_MODEL = 128
        N_HEADS = 16
        N_KV_HEADS = 4
        HEAD_DIM = 64
        B, Tq, _ = query.shape
        Tkv = context.shape[1]
        q = (query @ Wq.T).reshape(B, Tq, N_HEADS, HEAD_DIM).transpose(0, 2, 1, 3)
        k = (context @ Wk.T).reshape(B, Tkv, N_KV_HEADS, HEAD_DIM).transpose(0, 2, 1, 3)
        v = (context @ Wv.T).reshape(B, Tkv, N_KV_HEADS, HEAD_DIM).transpose(0, 2, 1, 3)
        groups = N_HEADS // N_KV_HEADS
        k = jnp.repeat(k, groups, axis=1)
        v = jnp.repeat(v, groups, axis=1)
        scale = jnp.sqrt(jnp.float32(HEAD_DIM))
        scores = jnp.einsum('bhqd,bhkd->bhqk', q, k) / scale
        attn = jax.nn.softmax(scores, axis=-1)
        out = jnp.einsum('bhqk,bhkd->bhqd', attn, v)
        out = out.transpose(0, 2, 1, 3).reshape(B, Tq, N_HEADS * HEAD_DIM)
        return out @ Wo.T

    def _L3_ffn_ref(x, w_gate, w_up, w_down):
        import jax, jax.numpy as jnp
        import numpy as np
        DIM = 128
        HIDDEN = 384
        SCALE = 1.0 / 127.0

        def _dequant(w_int, dtype):
            return w_int.astype(dtype) * jnp.asarray(SCALE, dtype)
        wg = _dequant(w_gate, x.dtype)
        wu = _dequant(w_up, x.dtype)
        wd = _dequant(w_down, x.dtype)
        gate = jnp.einsum('bsd,hd->bsh', x, wg)
        up = jnp.einsum('bsd,hd->bsh', x, wu)
        h = jax.nn.silu(gate) * up
        return jnp.einsum('bsh,dh->bsd', h, wd)
    x = x + jnp.tanh(g_xattn[0]) * _L0_xattn_ref(_layernorm(x, axis=-1), ctx_1024, L0_xattn_Wq, L0_xattn_bq, L0_xattn_Wk, L0_xattn_bk, L0_xattn_Wv, L0_xattn_bv, L0_xattn_Wp, L0_xattn_bp)
    x = x + jnp.tanh(g_ffn[0]) * _L0_ffn_ref(_layernorm(x, axis=-1), L0_ffn_router_weight, L0_ffn_expert_bias, L0_ffn_w1, L0_ffn_w2, L0_ffn_sw1, L0_ffn_sw2)
    x = x + jnp.tanh(g_xattn[1]) * _L1_xattn_ref(_layernorm(x, axis=-1), ctx_1024, L1_xattn_w_q, L1_xattn_w_k, L1_xattn_w_v, L1_xattn_w_o)
    x = x + jnp.tanh(g_ffn[1]) * _L1_ffn_ref(_layernorm(x, axis=-1), L1_ffn_sim_matrix, L1_ffn_gates, L1_ffn_q_proj, L1_ffn_k_proj, L1_ffn_v_proj, L1_ffn_o_proj)
    x = x + jnp.tanh(g_xattn[2]) * _L2_xattn_ref(_layernorm(x, axis=-1), ctx_1024, mask_BxS2_ik0, L2_xattn_Wq, L2_xattn_Wk, L2_xattn_Wv, L2_xattn_Wo)
    x = x + jnp.tanh(g_ffn[2]) * _L2_ffn_ref(_layernorm(x, axis=-1), L2_ffn_Wr, L2_ffn_br, L2_ffn_W1, L2_ffn_b1, L2_ffn_W2, L2_ffn_b2)
    x = x + jnp.tanh(g_xattn[3]) * _L3_xattn_ref(_layernorm(x, axis=-1), ctx_1024, L3_xattn_Wq, L3_xattn_Wk, L3_xattn_Wv, L3_xattn_Wo)
    x = x + jnp.tanh(g_ffn[3]) * _L3_ffn_ref(_layernorm(x, axis=-1), L3_ffn_w_gate, L3_ffn_w_up, L3_ffn_w_down)
    return x

_drawn_inputs = setup_inputs


def setup_inputs(seed=0):
    import zlib

    import numpy as np

    out = dict(_drawn_inputs(seed))
    spreads = {'L0_xattn_bq': (0.0, 0.432),
     'L0_xattn_bk': (0.0, 0.8),
     'L0_xattn_bv': (0.0, 0.1),
     'L0_xattn_bp': (0.0, 0.1),
     'L0_ffn_expert_bias': (0.0, 0.1),
     'L1_ffn_gates': (0.0, 0.1),
     'L2_ffn_br': (0.0, 0.604),
     'L2_ffn_b1': (0.0, 0.8),
     'L2_ffn_b2': (0.0, 0.607)}
    factors = {'L2_xattn_Wq': 8.0,
     'L2_xattn_Wk': 8.0,
     'L2_xattn_Wv': 2.759,
     'L2_ffn_Wr': 3.967,
     'L2_ffn_W1': 7.335,
     'L2_ffn_W2': 5.767}
    for name, (base, spread) in spreads.items():
        noise = np.random.default_rng([zlib.crc32(name.encode()), seed]).standard_normal(out[name].shape)
        drawn = base * np.exp(spread * noise) if base else spread * noise
        out[name] = jnp.asarray(drawn.astype(out[name].dtype))
    for name, factor in factors.items():
        out[name] = (out[name] * factor).astype(out[name].dtype)
    return out
```

```python
from contextlib import ExitStack

import numpy as np
import concourse.bass as bass
from concourse import mybir

F32 = mybir.dt.float32
F32R = mybir.dt.float32r
I32 = mybir.dt.int32
ALU = mybir.AluOpType
ACT = mybir.ActivationFunctionType
AX = mybir.AxisListType

P = 128
B, T, C = 4, 256, 128
NT = B * T // P
KEYS = 64
H, D = 16, 8
EPS = 1e-5
BIG = 1e30

E0, K0, HID0, CAP0 = 64, 6, 64, 48
SH0 = 256
E1, D1 = 16, 64
E2, K2, HID2 = 8, 2, 512
CAP2 = int(T / E2 * 1.25)
HK3, D3, R3 = 4, 64, 4
M3 = 3
FMIN = float(np.finfo(np.float32).min)

PACKS = {
    "first": [("x", NT * C), ("ctxT", B * KEYS), ("wq0", C), ("wkv0", 2 * C), ("rows0", 5 * C), ("ident", P),
              ("headmask", H), ("gain", 8)],
    "attn": [("wp0", C), ("router0", E0), ("ebias0", E0), ("earlier", P), ("half64", E0), ("ctx2", B * 2 * KEYS),
             ("wq2", C), ("wk2", C), ("wv2", C), ("wo2", C), ("wq4", C), ("wk4", C), ("wv4", C), ("wo4", C),
             ("parity", 2)],
    "moe0a": [("w1_0", (E0 * HID0 + SH0))],
    "moe0b": [("w2_0", (E0 * HID0 + SH0) // P * C)],
    "mix": [("half32", E1), ("sim", E1), ("gates", E1), ("qk3", E1 * P), ("v3", E1 * D1), ("o3", E1 * D1 // P * C),
            ("causal", T)],
    "moe2": [("router2", E2), ("b1_2", E2 * HID2 // P), ("b2_2", C)],
}
GQA = [("wq6", HK3 // 2 * R3 * C), ("wk6", HK3 * D3), ("wv6", HK3 * 2 * D3), ("wo6", H * D3 // P * C)]
LATER = {"moe2a": ("w1_0", E2 * HID2), "moe2b": ("w2_0", E2 * HID2 // P * C)}
IPACK = [("mask", B * KEYS), ("wg", M3 * P), ("wu", M3 * P), ("wd", M3 * C)]


def spans(fields):
    at, out = 0, {}
    for name, n in fields:
        out[name] = (at, at + n)
        at += n
    return out, at


def flamingo_blocks(nc, packed, ints, out):
    ctx = ExitStack()
    with ctx:
        def sb(name, shape, dt=F32):
            return ctx.enter_context(nc.sbuf_tensor(name, shape, dt))

        where, ctx_in = {}, {}
        for pk, fields in PACKS.items():
            sp, n = spans(fields)
            t = sb("in_" + pk, [P, n])
            ctx_in[pk] = t
            for name, (a, z) in sp.items():
                where[name] = t[:, a:z]
        for name, (a, z) in spans(GQA)[0].items():
            o = spans(PACKS["mix"])[0]["qk3"][0]
            where[name] = ctx_in["mix"][:, o + a:o + z]
        sp, n = spans(IPACK)
        ipk = sb("in_ints", [P, n], I32)
        fpk = ipk[:].bitcast(F32)
        for name, (a, z) in sp.items():
            where[name] = fpk[:, a:z]

        def w(name):
            return where[name]

        X = w("x").rearrange("p (t c) -> p t c", c=C)
        ident = w("ident")
        row0 = w("rows0").rearrange("p (k c) -> p k c", c=C)
        ones = sb("ones", [P, P])
        half_neg = sb("half_neg", [P, 2])
        hm = w("headmask")

        st = sb("ln_stats", [P, 2, 6])
        mv = sb("ln_mean_var", [P, 2, 2])
        vareps = sb("ln_var_eps", [P, 2])
        rstd = sb("ln_rstd", [P, 2])
        hN = sb("ln_h", [P, NT, C])
        hT = sb("hT", [P, B * T])

        kk = sb("k_soft", [P, 2, C])
        vv = sb("v_ones", [P, 2, C + 1])
        red = sb("red", [P, 2, H])
        red2 = sb("red2", [P, 2, H])
        with nc.sbuf_tensor("spread64", [P, E0 * HID0], F32R) as early:
            spread64 = early
        S = sb("scores", [P, 4, H * KEYS])
        tail = sb("tail", [P, 3 * M3 * T])
        q0 = tail[:, 0:4 * C].rearrange("p (k j c) -> p k j c", k=2, c=C)
        q0T = tail[:, 4 * C:6 * C]
        kvb = tail[:, 6 * C:6 * C + B * (C + H)].rearrange("p (b n) -> p b n", b=B)
        o0 = sb("o_tok", [P, 2, C])
        oT = sb("oT", [P, 2 * P])
        gain = sb("tanh_gain", [P, 8])

        kT = sb("kT", [P, 2, B * KEYS])
        kblk = {2: sb("kblk2", [P, B, H * KEYS]), 4: sb("kblk4", [P, B, H * KEYS])}
        A6 = kblk[2]
        v18 = {2: sb("v18_2", [P, B, H // 2 * 2 * (D + 1)]), 4: sb("v18_4", [P, B, H // 2 * 2 * (D + 1)])}
        kT6 = sb("kT6", [P, 2, B * KEYS])
        VO6 = kblk[4][:].rearrange("p b (k c) -> p b k c", c=C)
        qT = sb("qT", [P, 2, 2 * P])
        smax = sb("smax", [P, 2, H])
        ssum = sb("ssum", [P, 2, H])
        PT = sb("probsT", [P, 2, H * KEYS])
        rden = sb("rden", [P, 2, H])

        sc = sb("scores_r", [P, 2, E0])
        topin = sb("topin", [P, 2, 2 + E0])
        topin2 = sb("topin2", [P, 2, 6 + E1])
        rep = sb("replaced", [P, 2, 2 + E0])
        top8 = sb("top8", [P, 2, 8])
        sel = sb("chosen", [P, NT, E0])
        wts = sb("weights", [P, 2, E0])
        rs = sb("rsum", [P, 2, 1])
        GG = sb("gates_tok", [P, 2, 2 * E0])
        G16 = sb("gates16_tok", [P, 2, 64])
        gT = sb("gateT", [P, B * T], F32R)
        gT3 = gT5 = gT[0:64, :]
        pair16 = sb("pair16", [64, E1 * D1], F32R)
        rows32 = sb("rows32", [64, E1], F32R)
        shared = sb("hidden_or_mixed", [P, 6 * 512 + 1024])
        H1 = shared[:, 0:1024].rearrange("p (k n) -> p k n", k=2)
        Hg = shared[:, 1024:2560].rearrange("p (k n) -> p k n", k=3)
        accS = shared[:, 2560:3072]
        vT6 = shared[:, 0:HK3 * B * 2 * KEYS].rearrange("p (g n) -> p g n", g=HK3)
        xeT = shared[:].rearrange("p (e t) -> p e t", e=E1)

        simn = sb("sim_n", [P, E1])
        simss = sb("sim_sumsq", [P, E1])
        siminv = sb("sim_inv", [P, E1])
        sgate = sb("sgate", [P, E1])
        ss = sb("sumsq", [P, 2])
        junk = sb("junk", [P, C])
        rn = sb("rnorm", [P, B, 2])
        lg = sb("logits3", [P, 2, E1])
        act1 = sb("active", [P, 2, E1])
        cnt = sb("cnt3", [P, 2, 1])
        qT3 = sb("qT3", [D1, 2, T])
        kT3 = sb("kT3", [D1, 2, T])
        v3d = sb("v3d", [P, 2, 2, 2 * D1])
        S3 = sb("S3", [P, 2, T])
        m3 = sb("m3", [P, 2, 1])
        s3 = sb("s3", [P, 2, 1])
        PT3 = sb("PT3", [P, 2, T])
        aT3 = sb("aT3", [P, T])
        mixT = tail[:, 0:E1 // 2 * T].rearrange("p (e t) -> p e t", t=T)

        sg7 = tail[:, 0:M3 * T].rearrange("p (m t) -> p m t", t=T)
        H7 = tail[:, M3 * T:].rearrange("p (k m t) -> p k m t", k=2, t=T)

        PS = ctx.enter_context(nc.psum_tensor("banks", [P, 8, 512], F32))

        def sem(name):
            return ctx.enter_context(nc.semaphore(name))

        load = {pk: sem("load_" + pk) for pk in list(PACKS) + list(LATER) + ["gqa"]}
        load_ints = sem("load_ints")
        stored = sem("stored")
        names = """consts ln_var ln_rstd ln_h ln_T hT resid out_ready dve_step act_step pool_step
            ints_cast gain_set kvb_set spread_set sc_pool qkv_mm2 kT6_set pe_k0 k0_sub k0_exp k0_soft pe_kv0 q0_mm q0_sub q0_exp q0_soft q0_T q0T_set kvo o0_tok
            oT_mm oT_set kT_mm kT_set kblk_set v_mm v18_set q_mm q_set sc_mm sc_sub sc_exp sc_norm PT_mm PT_set pv_mm o_tok
            r1_mm r1_exp sel_set pos_mm gg_set ggT_mm gT_set mA mG h1 hg hg_used acc_evac
            sim_sq sim_mm sim_ss sim_pw sim_set sg_exp ss_set ss_pw l3_mm l3_sub l3_exp g3_set g3T_mm g3T_set bc_mm xe_set
            qkv_mm qkv_set qkv_v s3_mm s3_sub s3_exp s3_norm PT3_mm PT3_set a3_mm a3_set bp_mm mix_set
            r5_mm r5_sub r5_exp sel5 pos5 g5_set g5T_mm g5T_set vT6_mm vT6_set A6_mm A6_set vo_mm vo_set
            gu_mm silu7 h7_set""".split()
        sig = {n: sem(n) for n in names}

        block = ctx.enter_context(nc.Block())

        order = []
        for b in range(B):
            order.append(("F", 0, b))
            if b:
                order.append(("B", 0, b - 1))
        order.append(("F", 1, 0))
        order.append(("B", 0, B - 1))
        order += [("F", 1, 1), ("F", 1, 2), ("F", 1, 3), ("S", 2, 0), ("M", 1, 0), ("M", 1, 1)]

        def pipe(subs, after):
            fs = [("F", s, b) for s in subs for b in range(B)]
            bs = [("B", s, b) for s in subs for b in range(B)]
            o = [fs[0]]
            for i in range(1, len(fs)):
                o += [fs[i], bs[i - 1]]
            return o + after[:1] + [bs[-1]] + after[1:]

        order += pipe([2, 3, 4], [("F", 5, 0), ("F", 5, 1), ("F", 5, 2), ("F", 5, 3)])
        order += [("S", 6, 0), ("M", 5, 0), ("M", 5, 1)]
        order += pipe([6, 7], [])
        LN = [(s, b) for s in range(8) for b in range(B)]
        STEPS = {1: (E0 * HID0 + SH0) // P, 5: E2 * HID2 // P}
        BASE = {1: 0, 5: 2 * STEPS[1]}
        GBASE = {1: 0, 5: 2 * (E0 * HID0 // P)}

        ATT = [0, 2, 4]
        KV0 = [3, 4, 5, 7]

        def heads(ap, d=D):
            return ap.rearrange("p (h d) -> p h d", d=d)


        @block.sync
        def _(sp):
            for pk in ["first", "attn", "moe0a", "moe0b", "mix", "moe2"]:
                sp.dma_start(ctx_in[pk][:], packed[pk]).then_inc(load[pk], 16)
            sp.dma_start(ipk[:], ints).then_inc(load_ints, 16)
            sp.wait_ge(sig["hg_used"], BASE[5])
            for pk, (name, n) in LATER.items():
                sp.dma_start(w(name)[:, 0:n], packed[pk]).then_inc(load[pk], 16)
            sp.wait_ge(sig["out_ready"], 4 * B)
            o, n = spans(PACKS["mix"])[0]["qk3"][0], spans(GQA)[1]
            sp.dma_start(ctx_in["mix"][:, o:o + n], packed["gqa"]).then_inc(load["gqa"], 16)
            for b in range(B):
                sp.wait_ge(sig["resid"], 7 * B + b + 1)
                sp.dma_start(out[:, 2 * b * C:(2 * b + 2) * C],
                             w("x")[:, 2 * b * C:(2 * b + 2) * C]).then_inc(stored, 16)
            sp.wait_ge(stored, 16 * B)

        @block.gpsimd
        def _(pool):
            nc.gpsimd.memset(half_neg[:], -0.5).then_inc(sig["pool_step"], 1)
            pool.wait_ge(sig["pool_step"], 1)

            def rsqrt(n):
                pool.wait_ge(sig["ln_var"], n + 1)
                if n:
                    pool.wait_ge(sig["ln_h"], 2 * n)
                nc.gpsimd.tensor_tensor(rstd[:], vareps[:], half_neg[:], ALU.pow).then_inc(sig["ln_rstd"], 1)

            def key_blocks(s):
                k = s // 4
                pool.wait_ge(sig["kT_set"], k + 1)
                for b in range(B):
                    a = kT[:, k, b * KEYS:(b + 1) * KEYS].unsqueeze(1).broadcast_to([P, H, KEYS])
                    nc.gpsimd.tensor_tensor(heads(kblk[s][:, b, :], KEYS), a,
                                            hm.unsqueeze(2).broadcast_to([P, H, KEYS]), ALU.mult)\
                        .then_inc(sig["kblk_set"], 1)

            def cast_ints():
                pool.wait_ge(load_ints, 16)
                nc.gpsimd.tensor_copy(fpk, ipk[:]).then_inc(sig["pool_step"], 1)
                pool.wait_ge(sig["pool_step"], 2)
                a = B * KEYS
                nc.gpsimd.tensor_scalar(fpk[:, a:], fpk[:, a:], 1.0 / 127.0, None, ALU.mult)
                nc.gpsimd.tensor_scalar(fpk[:, 0:a], fpk[:, 0:a], -1.0, 1.0, ALU.mult, ALU.add)\
                    .then_inc(sig["pool_step"], 1)
                pool.wait_ge(sig["pool_step"], 3)
                nc.gpsimd.tensor_scalar(fpk[:, 0:a], fpk[:, 0:a], FMIN, None, ALU.mult).then_inc(sig["ints_cast"], 1)

            def sim_norms():
                pool.wait_ge(sig["sim_ss"], 1)
                nc.gpsimd.tensor_tensor(siminv[:], simss[:], half_neg[:, 0:1].broadcast_to([P, E1]), ALU.pow)\
                    .then_inc(sig["sim_pw"], 1)

            for kind, s, b in order:
                if kind == "F" and s == 0 and b == 0:
                    for k in range(B):
                        rsqrt(k)
                    continue
                if kind == "F" and s == 1 and b == 0:
                    pool.wait_ge(load["attn"], 16)
                    nc.gpsimd.tensor_copy(spread64[:].rearrange("p (e d) -> p e d", d=HID0),
                                          w("half64").unsqueeze(2).broadcast_to([P, E0, HID0]))\
                        .then_inc(sig["spread_set"], 1)
                if kind == "S" and s == 2:
                    key_blocks(2)
                    sim_norms()
                    key_blocks(4)
                    cast_ints()
                if kind == "B" and s + 1 < 8:
                    rsqrt((s + 1) * B + b)
                    if s + 1 == 3:
                        pool.wait_ge(sig["ss_set"], 2 * b + 2)
                        nc.gpsimd.tensor_tensor(rn[:, b, :], ss[:], half_neg[:], ALU.pow)\
                            .then_inc(sig["ss_pw"], 1)
                if kind == "M":
                    rsqrt((s + 1) * B + 2 * b)
                    rsqrt((s + 1) * B + 2 * b + 1)
                if kind == "F" and s == 6:
                    for j in range(2):
                        n = 2 * b + j
                        pool.wait_ge(sig["sc_norm"], n + 1)
                        nc.gpsimd.tensor_tensor(heads(S[:, n % 4, :], KEYS), heads(S[:, n % 4, :], KEYS),
                                                rden[:, j, :].unsqueeze(2).broadcast_to([P, H, KEYS]), ALU.mult)\
                            .then_inc(sig["sc_pool"], 1)

        @block.tensor
        def _(pe):
            mm = nc.tensor.matmul

            def bank(k):
                return PS[:, k, :]

            def ln_T(n):
                pe.wait_ge(sig["ln_h"], 2 * n + 2)
                if n:
                    pe.wait_ge(sig["hT"], n)
                for j in range(2):
                    last = nc.tensor.transpose(bank(0)[:, j * P:(j + 1) * P], hN[:, 2 * (n % B) + j, :], ident)
                last.then_inc(sig["ln_T"], 1)
                pe.wait_ge(sig["hT"], n + 1)

            def h(b, j=None):
                a = 2 * b * P
                return hT[:, a:a + 2 * P] if j is None else hT[:, a + j * P:a + (j + 1) * P]

            def out_free(n):
                if n:
                    pe.wait_ge(sig["resid"], n)

            def setup0():
                pe.wait_ge(load["first"], 16)
                pe.wait_ge(sig["consts"], 1)
                for j in range(2):
                    o = bank(6 + j)[:, 0:2 * C]
                    mm(o, ones[0:1, :], row0[0:1, 1:3, :], start=True, stop=False)
                    mm(o, w("ctxT")[:, j * P:(j + 1) * P], w("wkv0"), start=False, stop=True).then_inc(sig["pe_k0"], 1)
                for b in range(B):
                    pe.wait_ge(sig["k0_soft"], b // 2 + 1)
                    r = slice((b % 2) * KEYS, (b % 2 + 1) * KEYS)
                    mm(bank(KV0[b])[:, 0:C + 1], kk[r, b // 2, :], vv[r, b // 2, :],
                       start=True, stop=True).then_inc(sig["pe_kv0"], 1)

            def F0(b):
                ln_T(b)
                if b:
                    pe.wait_ge(sig["q0_sub"], b)
                for j in range(2):
                    o = bank(2)[:, j * C:(j + 1) * C]
                    mm(o, ones[0:1, :], row0[0:1, 0, :], start=True, stop=False)
                    m = mm(o, h(b, j), w("wq0"), start=False, stop=True)
                m.then_inc(sig["q0_mm"], 1)

            def B0(b):
                pe.wait_ge(sig["q0_soft"], b + 1)
                if b:
                    pe.wait_ge(sig["oT_set"], b)
                for j in range(2):
                    m = nc.tensor.transpose(bank(6)[:, j * P:(j + 1) * P], q0[:, b % 2, j, :], ident)
                m.then_inc(sig["q0_T"], 1)
                pe.wait_ge(sig["q0T_set"], b + 1)
                pe.wait_ge(sig["kvb_set"], b + 1)
                for j in range(2):
                    m = mm(bank(7)[:, j * 144:(j + 1) * 144], q0T[:, j * P:(j + 1) * P], kvb[:, b, :],
                           start=True, stop=True)
                m.then_inc(sig["kvo"], 1)
                pe.wait_ge(load["attn"], 16)
                project(0, b, w("wp0"), row0[0:1, 3, :])

            def project(s, b, wo, bias=None):
                n = s * B + b
                k = ATT.index(s) * B + b
                pe.wait_ge(sig["o_tok"], k + 1)
                for j in range(2):
                    m = nc.tensor.transpose(bank(3)[:, j * P:(j + 1) * P], o0[:, j, :], ident)
                m.then_inc(sig["oT_mm"], 1)
                pe.wait_ge(sig["oT_set"], k + 1)
                out_free(n)
                for j in range(2):
                    o = bank(1)[:, j * C:(j + 1) * C]
                    if bias is not None:
                        mm(o, ones[0:1, :], bias, start=True, stop=False)
                    m = mm(o, oT[:, j * P:(j + 1) * P], wo, start=bias is None, stop=True)
                m.then_inc(sig["out_ready"], 1)

            def F1(b):
                ln_T(B + b)
                if b:
                    pe.wait_ge(sig["gT_set"], b)
                else:
                    pe.wait_ge(load["attn"], 16)
                    pe.wait_ge(sig["q0_sub"], B)
                for j in range(2):
                    m = mm(bank(2)[:, j * E0:(j + 1) * E0], h(b, j), w("router0"), start=True, stop=True)
                m.then_inc(sig["r1_mm"], 1)
                pe.wait_ge(sig["sel_set"], b + 1)
                for j in range(2):
                    i = 2 * b + j
                    o = bank(2)[:, 256 + j * E0:256 + (j + 1) * E0]
                    for k in range(i):
                        mm(o, ones[:], sel[:, k, :], start=(k == 0), stop=False)
                    m = mm(o, w("earlier"), sel[:, i, :], start=(i == 0), stop=True)
                m.then_inc(sig["pos_mm"], 1)
                pe.wait_ge(sig["gg_set"], b + 1)
                for j in range(2):
                    m = nc.tensor.transpose(bank(2)[:, j * P:(j + 1) * P], GG[:, j, :], ident)
                m.then_inc(sig["ggT_mm"], 1)

            def S2():
                for k, s in enumerate((2, 4)):
                    if k == 0:
                        pe.wait_ge(sig["gT_set"], B)
                    else:
                        pe.wait_ge(sig["kT_set"], k)
                    mm(bank(2)[:, 0:256], w(f"wk{s}"), w("ctxT"), start=True, stop=True).then_inc(sig["kT_mm"], 1)
                for k, s in enumerate((2, 4)):
                    if k:
                        pe.wait_ge(sig["v18_set"], k * B)
                    for b in range(B):
                        m = mm(bank(3)[:, b * C:(b + 1) * C], w("ctx2")[:, b * P:(b + 1) * P], w(f"wv{s}"),
                               start=True, stop=True)
                    m.then_inc(sig["v_mm"], 1)

            def M(s, half):
                steps = STEPS[s]
                base = BASE[s] + half * steps
                gbase = GBASE[s] + half * (32)
                lo = half * 512
                w1 = w("w1_0").rearrange("p (m k) -> p m k", k=P)
                w2 = w("w2_0").rearrange("p (m k) -> p m k", k=C)
                acc = bank(3)
                if half == 0:
                    if s == 1:
                        pe.wait_ge(sig["spread_set"], 1)
                    if s == 5:
                        pe.wait_ge(sig["A6_set"], H // 2)
                        pe.wait_ge(sig["vo_set"], B * HK3)
                    for pk in (("moe0a", "moe0b") if s == 1 else ("moe2a", "moe2b")):
                        pe.wait_ge(load[pk], 16)

                def second(m):
                    g = base + m
                    pe.wait_ge(sig["hg"], g + 1)
                    if m == 0 and (s, half) != (1, 0):
                        pe.wait_ge(sig["acc_evac"], (s // 4) * 2 + half)
                    first = m == 0
                    if first and s == 1 and half == 0:
                        pe.wait_ge(sig["v18_set"], 2 * B)
                    if first and s == 5:
                        mm(acc, w("b2_2")[0:64, :], gT5[:, lo:lo + 512].bitcast(F32), start=True, stop=False)
                        first = False
                    i = mm(acc, w2[:, m, :], Hg[:, g % 3, :], start=first, stop=(m == steps - 1))
                    i.then_inc(sig["hg_used"], 1)
                    if m == steps - 1:
                        return i

                for m in range(steps + 2):
                    g = base + m
                    if m < steps:
                        if g >= 2:
                            pe.wait_ge(sig["h1"], g - 1)
                        mm(bank(6 + g % 2), w1[:, m, :], hT[:, lo:lo + 512], start=True, stop=True)\
                            .then_inc(sig["mA"], 1)
                        if m < 32:
                            if g >= 2:
                                pe.wait_ge(sig["hg"], g - 1)
                            if s == 1:
                                lh = spread64[:, m * P:(m + 1) * P]
                                rh = gT[:, lo:lo + 512]
                            else:
                                lh = rows32[:, m // 4:m // 4 + 1].broadcast_to([64, P])
                                rh = gT5[:, lo:lo + 512]
                            mm(bank(4 + g % 2), lh, rh, start=True, stop=True).then_inc(sig["mG"], 1)
                    if m >= 2:
                        second(m - 2)
                k = (s // 4) * 2 + half
                pe.wait_ge(sig["acc_evac"], k + 1)
                out_free(s * B + 2 * half)
                for j in range(4):
                    m = nc.tensor.transpose(bank(1)[:, j * P:(j + 1) * P], accS[:, j * P:(j + 1) * P], ident)
                m.then_inc(sig["out_ready"], 2)

            def scores(s, b, mat):
                for j in range(2):
                    n = (ATT.index(s) - 1) * 2 * B + 2 * b + j if s < 6 else 4 * B + 2 * b + j
                    if n:
                        pe.wait_ge(sig["sc_sub"], n)
                    lh = qT[:, b % 2, j * P:(j + 1) * P] if s < 6 else h(b, j)
                    for k in range(2):
                        m = mm(bank(4 + k), lh, mat[:, b, k * 512:(k + 1) * 512], start=True, stop=True)
                    m.then_inc(sig["sc_mm"], 1)

            def Fx(s, b):
                ln_T(s * B + b)
                k = (s // 4) * B + b
                if k:
                    pe.wait_ge(sig["q_set"], k)
                if k == B:
                    pe.wait_ge(sig["qkv_v"], B)
                mm(bank(2)[:, 0:256], w(f"wq{s}"), h(b), start=True, stop=True).then_inc(sig["q_mm"], 1)
                pe.wait_ge(sig["q_set"], k + 1)
                pe.wait_ge(sig["kblk_set"], (s // 4) * B + b + 1)
                scores(s, b, kblk[s])

            def probs_T(n, j):
                for k in range(2):
                    if n:
                        pe.wait_ge(sig["PT_set"], 2 * (n - 1) + k + 1)
                    for i in range(4):
                        a = (4 * k + i) * P
                        m = nc.tensor.transpose(bank(6 + k)[:, i * P:(i + 1) * P], S[:, n % 4, a:a + P], ident)
                    m.then_inc(sig["PT_mm"], 1)

            def Bx(s, b):
                for j in range(2):
                    n = (s // 4) * 2 * B + 2 * b + j
                    pe.wait_ge(sig["sc_exp"], n + 1)
                    probs_T(n, j)
                    pe.wait_ge(sig["PT_set"], 2 * n + 2)
                    if j == 0:
                        k = ATT.index(s) * B + b
                        pe.wait_ge(sig["oT_set"], k)
                    for k in range(8):
                        m = mm(bank(3)[:, j * 144 + k * 18:j * 144 + (k + 1) * 18],
                               PT[:, j, k * P:(k + 1) * P], v18[s][:, b, k * 18:(k + 1) * 18], start=True, stop=True)
                    m.then_inc(sig["pv_mm"], 1)
                project(s, b, w(f"wo{s}"))

            def setup3():
                pe.wait_ge(sig["sim_sq"], 1)
                pe.wait_ge(sig["v18_set"], 2 * B)
                mm(bank(3)[:, 0:E1], ones[:], junk[:, 0:E1], start=True, stop=True).then_inc(sig["sim_mm"], 1)

            def spread(o, lh, rh):
                return mm(o, lh, rh, start=True, stop=True)

            def F3(b):
                ln_T(3 * B + b)
                if b == 0:
                    pe.wait_ge(sig["sim_set"], 1)
                    pe.wait_ge(sig["sc_sub"], 2 * B)
                if b:
                    pe.wait_ge(sig["qkv_v"], b)
                for j in range(2):
                    m = mm(bank(2)[:, j * E1:(j + 1) * E1], h(b, j), simn[:], start=True, stop=True)
                m.then_inc(sig["l3_mm"], 1)
                pe.wait_ge(sig["g3_set"], b + 1)
                for j in range(2):
                    m = nc.tensor.transpose(bank(2)[0:64, 256 + j * P - 0:256 + (j + 1) * P], G16[:, j, :], ident)
                m.then_inc(sig["g3T_mm"], 1)
                pe.wait_ge(sig["g3T_set"], b + 1)
                for k in range(8):
                    n = b * 8 + k
                    if n >= 2:
                        pe.wait_ge(sig["xe_set"], n - 1)
                    for i in range(2):
                        e = 2 * k + i
                        m = spread(bank(4 + k % 2)[:, i * T:(i + 1) * T], rows32[:, e:e + 1].broadcast_to([64, P]),
                                   gT3[:, b * T:(b + 1) * T])
                    m.then_inc(sig["bc_mm"], 1)
                pe.wait_ge(sig["xe_set"], 8 * b + 8)
                for e in range(E1):
                    m = mm(bank(2)[:, 0:T], w("qk3")[:, e * P:(e + 1) * P], xeT[:, e, :], start=(e == 0),
                           stop=(e == E1 - 1))
                m.then_inc(sig["qkv_mm"], 1)
                pe.wait_ge(sig["qkv_set"], 2 * b + 2)
                for j in range(2):
                    for e in range(E1):
                        m = mm(bank(2)[:, 256 + j * D1:256 + (j + 1) * D1], xeT[:, e, j * P:(j + 1) * P],
                               w("v3")[:, e * D1:(e + 1) * D1], start=(e == 0), stop=(e == E1 - 1))
                m.then_inc(sig["qkv_mm2"], 1)

            def B3(b):
                pe.wait_ge(sig["qkv_v"], b + 1)
                for j in range(2):
                    n = 2 * b + j
                    if n:
                        pe.wait_ge(sig["s3_sub"], n)
                    if j == 0 and b:
                        pe.wait_ge(sig["mix_set"], 4 * b)
                    keys = (j + 1) * P
                    mm(bank(6)[:, 0:keys], qT3[:, b % 2, j * P:(j + 1) * P], kT3[:, b % 2, 0:keys], start=True,
                       stop=True).then_inc(sig["s3_mm"], 1)
                for j in range(2):
                    n = 2 * b + j
                    pe.wait_ge(sig["s3_norm"], n + 1)
                    if n:
                        pe.wait_ge(sig["PT3_set"], n)
                    for i in range(j + 1):
                        m = nc.tensor.transpose(bank(7)[:, i * P:(i + 1) * P], S3[:, j, i * P:(i + 1) * P], ident)
                    m.then_inc(sig["PT3_mm"], 1)
                    pe.wait_ge(sig["PT3_set"], n + 1)
                    if j == 0 and b:
                        pe.wait_ge(sig["a3_set"], b)
                    for i in range(j + 1):
                        m = mm(bank(3)[:, j * P:(j + 1) * P], v3d[:, b % 2, i, :], PT3[:, i, 0:P],
                               start=(i == 0), stop=(i == j))
                    m.then_inc(sig["a3_mm"], 1)
                for k in range(4):
                    if k >= 2:
                        pe.wait_ge(sig["mix_set"], 4 * b + k - 1)
                    for i in range(2):
                        p = 2 * k + i
                        m = spread(bank(6 + k % 2)[:, i * T:(i + 1) * T],
                                   pair16[:, p * P:(p + 1) * P],
                                   gT3[:, b * T:(b + 1) * T])
                    m.then_inc(sig["bp_mm"], 1)
                pe.wait_ge(sig["mix_set"], 4 * b + 4)
                out_free(3 * B + b)
                for j in range(2):
                    for p in range(E1 // 2):
                        m = mm(bank(1)[:, j * C:(j + 1) * C], mixT[:, p, j * P:(j + 1) * P],
                               w("o3")[:, p * C:(p + 1) * C], start=(p == 0), stop=(p == E1 // 2 - 1))
                m.then_inc(sig["out_ready"], 1)

            def F5(b):
                ln_T(5 * B + b)
                if b:
                    pe.wait_ge(sig["g5T_set"], b)
                for j in range(2):
                    o = bank(2)[:, j * E2:(j + 1) * E2]
                    mm(o, ones[0:1, :], row0[0:1, 4, 0:E2], start=True, stop=False)
                    m = mm(o, h(b, j), w("router2"), start=False, stop=True)
                m.then_inc(sig["r5_mm"], 1)
                pe.wait_ge(sig["sel5"], b + 1)
                mm(bank(2)[:, 256:256 + E2], w("earlier"), sel[:, 0, 0:E2], start=True, stop=True)
                mm(bank(2)[:, 256 + E2:256 + 2 * E2], ones[:], sel[:, 0, 0:E2], start=True, stop=False)
                mm(bank(2)[:, 256 + E2:256 + 2 * E2], w("earlier"), sel[:, 1, 0:E2], start=False, stop=True)\
                    .then_inc(sig["pos5"], 1)
                pe.wait_ge(sig["g5_set"], b + 1)
                for j in range(2):
                    m = nc.tensor.transpose(bank(2)[0:64, j * P:(j + 1) * P], G16[:, j, :], ident)
                m.then_inc(sig["g5T_mm"], 1)

            def S6():
                pe.wait_ge(load["gqa"], 16)
                pe.wait_ge(sig["g5T_set"], B)
                for k in range(2):
                    m = mm(bank(2)[:, k * 256:(k + 1) * 256], w("wk6")[:, k * P:(k + 1) * P], w("ctxT"),
                           start=True, stop=True)
                m.then_inc(sig["kT_mm"], 1)
                pe.wait_ge(sig["oT_set"], 3 * B)
                for g in range(HK3):
                    if g:
                        pe.wait_ge(sig["vT6_set"], g)
                    mm(bank(3), w("wv6")[:, g * P:(g + 1) * P], w("ctx2"), start=True, stop=True)\
                        .then_inc(sig["vT6_mm"], 1)
                pe.wait_ge(sig["kT6_set"], 1)
                pe.wait_ge(sig["sc_sub"], 4 * B)
                for hh in range(H // 2):
                    if hh >= 2:
                        pe.wait_ge(sig["A6_set"], hh - 1)
                    for i in range(2):
                        q = 2 * hh + i
                        g, r = q // R3, q % R3
                        G, gp = g // 2, g % 2
                        rr = slice(gp * D3, (gp + 1) * D3)
                        a = (G * R3 + r) * C
                        m = mm(bank(4 + hh % 2)[:, i * 256:(i + 1) * 256], w("wq6")[rr, a:a + C], kT6[rr, G, :],
                               start=True, stop=True)
                    m.then_inc(sig["A6_mm"], 1)
                pe.wait_ge(sig["vT6_set"], HK3)
                for b in range(B):
                    for g in range(HK3):
                        n = b * HK3 + g
                        if n >= 2:
                            pe.wait_ge(sig["vo_set"], n - 1)
                        mm(bank(6 + n % 2)[:, 0:256], vT6[:, g, b * P:(b + 1) * P],
                           w("wo6")[:, 2 * g * C:(2 * g + 2) * C], start=True, stop=True).then_inc(sig["vo_mm"], 1)

            def F6(b):
                ln_T(6 * B + b)
                scores(6, b, A6)

            def B6(b):
                out_free(6 * B + b)
                for j in range(2):
                    n = 4 * B + 2 * b + j
                    pe.wait_ge(sig["sc_pool"], 2 * b + j + 1)
                    probs_T(n, j)
                    pe.wait_ge(sig["PT_set"], 2 * n + 2)
                    for k in range(8):
                        m = mm(bank(1)[:, j * C:(j + 1) * C], PT[:, j, k * P:(k + 1) * P], VO6[:, b, k, :],
                               start=(k == 0), stop=(k == 7))
                m.then_inc(sig["out_ready"], 1)

            def F7(b):
                ln_T(7 * B + b)
                if b == 0:
                    pe.wait_ge(sig["ints_cast"], 1)
                    pe.wait_ge(sig["sc_sub"], 6 * B)
                for m in range(M3):
                    n = b * M3 + m
                    k = (4, 5, 2)[m]
                    if b:
                        pe.wait_ge(sig["h7_set"], n - M3 + 1)
                    mm(bank(k)[:, 0:T], w("wg")[:, m * P:(m + 1) * P], h(b), start=True, stop=True)
                    mm(bank(k)[:, T:2 * T], w("wu")[:, m * P:(m + 1) * P], h(b), start=True, stop=True)\
                        .then_inc(sig["gu_mm"], 1)

            def B7(b):
                pe.wait_ge(sig["h7_set"], M3 * (b + 1))
                out_free(7 * B + b)
                for j in range(2):
                    for m in range(M3):
                        i = mm(bank(1)[:, j * C:(j + 1) * C], H7[:, b % 2, m, j * P:(j + 1) * P],
                               w("wd")[:, m * C:(m + 1) * C], start=(m == 0), stop=(m == M3 - 1))
                i.then_inc(sig["out_ready"], 1)

            setup0()
            for kind, s, b in order:
                if kind == "F":
                    if s in (3, 5) and b == 0:
                        pe.wait_ge(load["mix" if s == 3 else "moe2"], 16)
                    {0: F0, 1: F1, 3: F3, 5: F5, 6: F6, 7: F7}[s](b) if s not in (2, 4) else Fx(s, b)
                elif kind == "B":
                    {0: B0, 3: B3, 6: B6, 7: B7}[s](b) if s not in (2, 4) else Bx(s, b)
                elif kind == "S":
                    if s == 2:
                        pe.wait_ge(load["mix"], 16)
                        S2()
                        setup3()
                    else:
                        S6()
                else:
                    M(s, b)

        @block.scalar
        def _(act):
            A = nc.scalar.activation

            def copy(o, i):
                return nc.scalar.copy(o, i)

            def ln_out(n):
                b = n % B
                act.wait_ge(sig["ln_T"], n + 1)
                copy(hT[:, b * 256:(b + 1) * 256], PS[:, 0, 0:256]).then_inc(sig["hT"], 1)

            def o_T(s, b):
                k = ATT.index(s) * B + b
                act.wait_ge(sig["oT_mm"], k + 1)
                copy(oT[:], PS[:, 3, 0:256]).then_inc(sig["oT_set"], 1)

            def exp_tile(s, b):
                for j in range(2):
                    n = {2: 0, 4: 2 * B, 6: 4 * B}[s] + 2 * b + j
                    act.wait_ge(sig["sc_sub"], n + 1)
                    A(S[:, n % 4, :], S[:, n % 4, :], ACT.Exp, scale=(D ** -0.5 if s == 2 else 1.0 if s == 4 else D3 ** -0.5))\
                        .then_inc(sig["sc_exp"], 1)

            def probs_out(s, b):
                for j in range(2):
                    n = {2: 0, 4: 2 * B, 6: 4 * B}[s] + 2 * b + j
                    for k in range(2):
                        act.wait_ge(sig["PT_mm"], 2 * n + k + 1)
                        copy(PT[:, j, k * 512:(k + 1) * 512], PS[:, 6 + k, :]).then_inc(sig["PT_set"], 1)

            def M(s, half):
                steps, base = STEPS[s], BASE[s] + half * STEPS[s]
                for m in range(steps):
                    g = base + m
                    act.wait_ge(sig["mA"], g + 1)
                    if g >= 2:
                        act.wait_ge(sig["hg"], g - 1)
                    if s == 1:
                        A(H1[:, g % 2, :], PS[:, 6 + g % 2, :], ACT.Gelu_apprx_tanh).then_inc(sig["h1"], 1)
                    else:
                        A(H1[:, g % 2, :], PS[:, 6 + g % 2, :], ACT.Relu, bias=w("b1_2")[:, m:m + 1])\
                            .then_inc(sig["h1"], 1)
                k = (s // 4) * 2 + half
                act.wait_ge(sig["hg_used"], base + steps)
                if half:
                    act.wait_ge(sig["out_ready"], s * B + 2)
                copy(accS, PS[:, 3, :]).then_inc(sig["acc_evac"], 1)

            act.wait_ge(load["first"], 16)
            A(gain[:], w("gain"), ACT.Tanh).then_inc(sig["gain_set"], 1)
            for j in range(2):
                act.wait_ge(sig["k0_sub"], j + 1)
                A(kk[:, j, :], kk[:, j, :], ACT.Exp).then_inc(sig["k0_exp"], 1)
            for kind, s, b in order:
                if kind == "F":
                    ln_out(s * B + b)
                if (kind, s) == ("F", 0):
                    act.wait_ge(sig["q0_sub"], b + 1)
                    A(q0[:, b % 2], q0[:, b % 2], ACT.Exp).then_inc(sig["q0_exp"], 1)
                if (kind, s) == ("B", 0):
                    act.wait_ge(sig["q0_T"], b + 1)
                    copy(q0T, PS[:, 6, 0:256]).then_inc(sig["q0T_set"], 1)
                    o_T(0, b)
                if (kind, s) == ("F", 1):
                    act.wait_ge(sig["r1_mm"], b + 1)
                    A(sc[:], PS[:, 2, 0:2 * E0].rearrange("p (j e) -> p j e", j=2), ACT.Exp, scale=-1.0)\
                        .then_inc(sig["r1_exp"], 1)
                if (kind, s) == ("S", 2):
                    act.wait_ge(load["mix"], 16)
                    A(sgate[:], w("gates"), ACT.Exp, scale=-1.0).then_inc(sig["sg_exp"], 1)
                    for k in range(2):
                        act.wait_ge(sig["kT_mm"], k + 1)
                        copy(kT[:, k, :], PS[:, 2, 0:256]).then_inc(sig["kT_set"], 1)
                if kind == "M":
                    M(s, b)
                if kind == "F" and s in (2, 4):
                    act.wait_ge(sig["q_mm"], (s // 4) * B + b + 1)
                    copy(qT[:, b % 2, :], PS[:, 2, 0:256]).then_inc(sig["q_set"], 1)
                if kind == "F" and s in (2, 4, 6):
                    exp_tile(s, b)
                if kind == "B" and s in (2, 4, 6):
                    probs_out(s, b)
                    if s < 6:
                        o_T(s, b)
                if (kind, s) == ("F", 3):
                    act.wait_ge(sig["l3_sub"], b + 1)
                    A(lg[:], lg[:], ACT.Exp).then_inc(sig["l3_exp"], 1)
                    act.wait_ge(sig["qkv_mm"], b + 1)
                    copy(qT3[:, b % 2, :], PS[0:D1, 2, 0:T]).then_inc(sig["qkv_set"], 1)
                    copy(kT3[:, b % 2, :], PS[D1:2 * D1, 2, 0:T]).then_inc(sig["qkv_set"], 1)
                    act.wait_ge(sig["qkv_mm2"], b + 1)
                    v = PS[:, 2, 256:256 + 2 * D1].rearrange("p (j d) -> p j d", j=2)
                    copy(v3d[:, b % 2, :, 0:D1], v)
                    copy(v3d[:, b % 2, :, D1:2 * D1], v).then_inc(sig["qkv_v"], 1)
                if (kind, s) == ("B", 3):
                    for j in range(2):
                        n = 2 * b + j
                        act.wait_ge(sig["s3_sub"], n + 1)
                        A(S3[:, j, 0:(j + 1) * P], S3[:, j, 0:(j + 1) * P], ACT.Exp, scale=D1 ** -0.5,
                          accum_out=s3[:, j, :]).then_inc(sig["s3_exp"], 1)
                    for j in range(2):
                        n = 2 * b + j
                        act.wait_ge(sig["PT3_mm"], n + 1)
                        if n:
                            act.wait_ge(sig["a3_mm"], n)
                        copy(PT3[:, 0:j + 1, 0:P], PS[:, 7, 0:(j + 1) * P].rearrange("p (i k) -> p i k", k=P))\
                            .then_inc(sig["PT3_set"], 1)
                if (kind, s) == ("F", 5):
                    act.wait_ge(sig["r5_sub"], b + 1)
                    A(sc[:, :, 0:E2], sc[:, :, 0:E2], ACT.Exp).then_inc(sig["r5_exp"], 1)
                if (kind, s) == ("S", 6):
                    act.wait_ge(sig["kT_mm"], 3)
                    copy(kT6[:], PS[:, 2, :].rearrange("p (k n) -> p k n", k=2)).then_inc(sig["kT6_set"], 1)
                    for hh in range(H // 2):
                        act.wait_ge(sig["A6_mm"], hh + 1)
                        for i in range(2):
                            m = copy(A6[:, :, (2 * hh + i) * KEYS:(2 * hh + i + 1) * KEYS],
                                     PS[:, 4 + hh % 2, i * 256:(i + 1) * 256].rearrange("p (b k) -> p b k", b=B))
                        m.then_inc(sig["A6_set"], 1)
                    for n in range(B * HK3):
                        act.wait_ge(sig["vo_mm"], n + 1)
                        g = n % HK3
                        copy(VO6[:, n // HK3, 2 * g:2 * g + 2, :],
                             PS[:, 6 + n % 2, 0:256].rearrange("p (k c) -> p k c", k=2)).then_inc(sig["vo_set"], 1)
                if (kind, s) == ("F", 7):
                    for m in range(M3):
                        act.wait_ge(sig["gu_mm"], b * M3 + m + 1)
                        A(sg7[:, m, :], PS[:, (4, 5, 2)[m], 0:T], ACT.Silu).then_inc(sig["silu7"], 1)

        @block.vector
        def _(dve):
            tt, ts, stt = nc.vector.tensor_tensor, nc.vector.tensor_scalar, nc.vector.scalar_tensor_tensor
            cp, red_, rcp = nc.vector.tensor_copy, nc.vector.tensor_reduce, nc.vector.reciprocal
            chain = [0]

            def link(ins):
                chain[0] += 1
                ins.then_inc(sig["dve_step"], 1)
                dve.wait_ge(sig["dve_step"], chain[0])

            def over(a, k):
                return a.unsqueeze(len(a.shape)).broadcast_to(list(a.shape) + [k])

            def layer_norm(n):
                b = n % B
                for j in range(2):
                    m = nc.vector.bn_stats(st[:, j, :], X[:, 2 * b + j, :])
                link(m)
                for j in range(2):
                    m = nc.vector.bn_aggr(mv[:, j, :], st[:, j, :])
                link(m)
                ts(vareps[:], mv[:, :, 1], EPS, None, ALU.add).then_inc(sig["ln_var"], 1)
                dve.wait_ge(sig["ln_rstd"], n + 1)
                if n >= B:
                    dve.wait_ge(sig["ln_T"], n - B + 1)
                for j in range(2):
                    ts(hN[:, 2 * b + j, :], X[:, 2 * b + j, :], mv[:, j, 0:1], rstd[:, j:j + 1], ALU.subtract, ALU.mult)\
                        .then_inc(sig["ln_h"], 1)
                if n // B == 3:
                    dve.wait_ge(sig["ln_h"], 2 * n + 2)
                    if b:
                        dve.wait_ge(sig["ss_pw"], b)
                    for j in range(2):
                        link(nc.vector.tensor_tensor_reduce(junk[:], hN[:, 2 * b + j, :], hN[:, 2 * b + j, :], 1.0, 0.0, ALU.mult,
                                                            ALU.add, ss[:, j:j + 1]))
                    ts(ss[:], ss[:], 1e-24, None, ALU.max).then_inc(sig["ss_set"], 2)
                    return "ss_set", 2 * b + 2
                return "ln_h", 2 * n + 2

            def residual(s, b, o):
                if (s, b) == (0, 0):
                    dve.wait_ge(sig["gain_set"], 1)
                x = w("x")[:, 2 * b * C:(2 * b + 2) * C]
                k = s // 2 + (0 if s % 2 == 0 else 4)
                stt(x, o, gain[:, k:k + 1], x, ALU.mult, ALU.add).then_inc(sig["resid"], 1)
                if s < 7:
                    dve.wait_ge(sig["resid"], s * B + b + 1)
                    return layer_norm((s + 1) * B + b)
                return "resid", s * B + b + 1

            def group_softmax_front(o, i, bias_src=None):
                link(red_(red[:], i, AX.X, ALU.max))
                return tt(o, i, over(red[:], D), ALU.subtract)

            def setup0():
                for j in range(2):
                    dve.wait_ge(sig["pe_k0"], j + 1)
                    kps = PS[:, 6 + j, 0:C].rearrange("p (h d) -> p h d", d=D)
                    link(red_(red[:, j, :], kps, AX.X, ALU.max))
                    cp(vv[:, j, 0:C], PS[:, 6 + j, C:2 * C])
                    tt(heads(kk[:, j, :]), kps, over(red[:, j, :], D), ALU.subtract).then_inc(sig["k0_sub"], 1)
                for j in range(2):
                    dve.wait_ge(sig["k0_exp"], j + 1)
                    kv = heads(kk[:, j, :])
                    link(red_(red[:, j, :], kv, AX.X, ALU.add))
                    link(rcp(red2[:, j, :], red[:, j, :]))
                    tt(kv, kv, over(red2[:, j, :], D), ALU.mult).then_inc(sig["k0_soft"], 1)
                for b in range(B):
                    dve.wait_ge(sig["pe_kv0"], b + 1)
                    tt(heads(kvb[:, b, 0:C]), PS[:, KV0[b], 0:C].rearrange("p (h d) -> p h d", d=D),
                       over(hm, D), ALU.mult)
                    ts(kvb[:, b, C:C + H], hm, PS[:, KV0[b], C:C + 1], None, ALU.mult)\
                        .then_inc(sig["kvb_set"], 1)
                dve.wait_ge(sig["kvb_set"], B)

            def F0(b):
                dve.wait_ge(sig["q0_mm"], b + 1)
                qps = PS[:, 2, 0:256].rearrange("p (k d) -> p k d", d=D)
                r1 = red[:].rearrange("p j h -> p (j h)")
                r2 = red2[:].rearrange("p j h -> p (j h)")
                link(red_(r1, qps, AX.X, ALU.max))
                q = q0[:, b % 2].rearrange("p j (h d) -> p (j h) d", d=D)
                tt(q, qps, over(r1, D), ALU.subtract).then_inc(sig["q0_sub"], 1)
                dve.wait_ge(sig["q0_exp"], b + 1)
                link(red_(r1, q, AX.X, ALU.add))
                link(rcp(r2, r1))
                tt(q, q, over(r2, D), ALU.mult).then_inc(sig["q0_soft"], 1)
                return "q0_soft", b + 1

            def B0(b):
                dve.wait_ge(sig["kvo"], b + 1)
                kvo = PS[:, 7, 0:288].rearrange("p (j n) -> p j n", j=2)
                link(rcp(red2[:], kvo[:, :, C:C + H]))
                if b:
                    dve.wait_ge(sig["oT_mm"], b)
                for j in range(2):
                    tt(heads(o0[:, j, :]), heads(kvo[:, j, 0:C]), over(red2[:, j, :], D), ALU.mult)\
                        .then_inc(sig["dve_step"], 1)
                    chain[0] += 1
                dve.wait_ge(sig["dve_step"], chain[0])
                tt(o0[:], o0[:], q0[:, b % 2], ALU.add).then_inc(sig["o_tok"], 1)
                return finish(0, b)

            def finish(s, b):
                dve.wait_ge(sig["out_ready"], s * B + b + 1)
                return residual(s, b, PS[:, 1, 0:256])

            def F1(b):
                if b == 0:
                    dve.wait_ge(load["attn"], 16)
                dve.wait_ge(sig["r1_exp"], b + 1)
                link(ts(sc[:], sc[:], 1.0, None, ALU.add))
                link(rcp(sc[:], sc[:]))
                link(tt(topin[:, :, 2:], sc[:], w("ebias0").unsqueeze(1).broadcast_to([P, 2, E0]), ALU.add))
                for j in range(2):
                    m = nc.vector.max(top8[:, j, :], topin[:, j, :])
                link(m)
                for j in range(2):
                    m = nc.vector.match_replace(rep[:, j, :], top8[:, j, :], topin[:, j, :], -BIG)
                link(m)
                ts(sel[:, 2 * b:2 * b + 2, :], rep[:, :, 2:], -BIG, None, ALU.is_equal).then_inc(sig["sel_set"], 1)
                dve.wait_ge(sig["sel_set"], b + 1)
                link(tt(wts[:], sc[:], sel[:, 2 * b:2 * b + 2, :], ALU.mult))
                link(red_(rs[:], wts[:], AX.X, ALU.add))
                link(ts(rs[:], rs[:], 1e-20, None, ALU.add))
                link(rcp(rs[:], rs[:]))
                link(tt(wts[:], wts[:], rs[:].broadcast_to([P, 2, E0]), ALU.mult))
                dve.wait_ge(sig["pos_mm"], b + 1)
                for j in range(2):
                    pos = PS[:, 2, 256 + j * E0:256 + (j + 1) * E0].unsqueeze(1).broadcast_to([P, 2, E0])
                    m = stt(GG[:, j, :].rearrange("p (k e) -> p k e", k=2), pos, float(CAP0),
                            wts[:, j, :].unsqueeze(1).broadcast_to([P, 2, E0]), ALU.is_lt, ALU.mult)
                m.then_inc(sig["gg_set"], 1)
                dve.wait_ge(sig["ggT_mm"], b + 1)
                g = gT[:, b * 256:(b + 1) * 256]
                link(cp(g, PS[:, 2, 0:256]))
                tt(g[64:128, :], PS[64:128, 2, 0:256], g[64:128, :].bitcast(F32), ALU.subtract)\
                    .then_inc(sig["gT_set"], 1)
                return "gT_set", b + 1

            def S2():
                for k, s in enumerate((2, 4)):
                    dve.wait_ge(sig["v_mm"], k + 1)
                    for b in range(B):
                        o = v18[s][:, b, :].rearrange("p (k j d) -> p k j d", j=2, d=D + 1)
                        for j in range(2):
                            i = PS[:, 3, b * C:(b + 1) * C].rearrange("p (k j d) -> p k j d", j=2, d=D)[:, :, j, :]
                            ts(o[:, :, j, 0:D], i, w("parity")[:, j:j + 1], None, ALU.mult)
                            m = ts(o[:, :, j, D], ones[:, 0:H // 2], w("parity")[:, j:j + 1], None, ALU.mult)
                        m.then_inc(sig["v18_set"], 1)

            def M(s, half):
                steps, base = STEPS[s], BASE[s] + half * STEPS[s]
                gbase = GBASE[s] + half * 32
                for m in range(steps):
                    g = base + m
                    dve.wait_ge(sig["h1"], g + 1)
                    if g >= 3:
                        dve.wait_ge(sig["hg_used"], g - 2)
                    if m < 32:
                        dve.wait_ge(sig["mG"], gbase + m + 1)
                        tt(Hg[:, g % 3, :], H1[:, g % 2, :], PS[:, 4 + g % 2, :], ALU.mult).then_inc(sig["hg"], 1)
                    else:
                        cp(Hg[:, g % 3, :], H1[:, g % 2, :]).then_inc(sig["hg"], 1)
                for j in range(2):
                    b = 2 * half + j
                    dve.wait_ge(sig["out_ready"], s * B + 2 * half + 2)
                    if j:
                        dve.wait_ge(sig[ended[0]], ended[1])
                    ended = residual(s, b, PS[:, 1, j * 256:(j + 1) * 256])
                return ended

            def softmax_tile(s, b):
                for j in range(2):
                    n = {2: 0, 4: 2 * B, 6: 4 * B}[s] + 2 * b + j
                    dve.wait_ge(sig["sc_mm"], n + 1)
                    if n >= 4:
                        dve.wait_ge(sig["PT_mm"], 2 * (n - 4) + 2)
                    sp_ = PS[:, 4:6, :].rearrange("p k (h n) -> p (k h) n", n=KEYS)
                    so = heads(S[:, n % 4, :], KEYS)
                    if s == 4:
                        if b == 0:
                            dve.wait_ge(sig["ints_cast"], 1)
                        e = w("mask")[:, b * KEYS:(b + 1) * KEYS].unsqueeze(1).broadcast_to([P, H, KEYS])
                        link(stt(so, sp_, D ** -0.5, e, ALU.mult, ALU.add))
                        link(red_(smax[:, j, :], so, AX.X, ALU.max))
                        sp_ = so
                    else:
                        link(red_(smax[:, j, :], sp_, AX.X, ALU.max))
                    tt(so, sp_, over(smax[:, j, :], KEYS), ALU.subtract).then_inc(sig["sc_sub"], 1)
                    if s == 6:
                        dve.wait_ge(sig["sc_exp"], n + 1)
                        link(red_(ssum[:, j, :], so, AX.X, ALU.add))
                        if b:
                            dve.wait_ge(sig["sc_pool"], 2 * b + j - 1)
                        rcp(rden[:, j, :], ssum[:, j, :]).then_inc(sig["sc_norm"], 1)
                return ("sc_norm", 2 * b + 2) if s == 6 else ("sc_sub", n + 1)

            def Bx(s, b):
                k = ATT.index(s) * B + b
                dve.wait_ge(sig["pv_mm"], (s // 4) * 2 * B + 2 * b + 2)
                for j in range(2):
                    pv = PS[:, 3, j * 144:(j + 1) * 144].rearrange("p (h d) -> p h d", d=D + 1)
                    link(rcp(rden[:, j, :], pv[:, :, D]))
                    if j == 0:
                        dve.wait_ge(sig["oT_mm"], k)
                    m = tt(heads(o0[:, j, :]), pv[:, :, 0:D], over(rden[:, j, :], D), ALU.mult)
                m.then_inc(sig["o_tok"], 1)
                return finish(s, b)

            def setup3():
                tt(junk[:, 0:E1], w("sim"), w("sim"), ALU.mult).then_inc(sig["sim_sq"], 1)

            def setup3b():
                dve.wait_ge(sig["sim_mm"], 1)
                ts(simss[:], PS[:, 3, 0:E1], 1e-24, None, ALU.max).then_inc(sig["sim_ss"], 1)
                dve.wait_ge(sig["sg_exp"], 1)
                link(ts(sgate[:], sgate[:], 1.0, None, ALU.add))
                link(rcp(sgate[:], sgate[:]))
                dve.wait_ge(sig["sim_pw"], 1)
                tt(simn[:], w("sim"), siminv[:], ALU.mult).then_inc(sig["sim_set"], 1)
                return "sim_set", 1

            def F3(b):
                dve.wait_ge(sig["l3_mm"], b + 1)
                dve.wait_ge(sig["ss_pw"], b + 1)
                for j in range(2):
                    m = stt(lg[:, j, :], PS[:, 2, j * E1:(j + 1) * E1], rn[:, b, j:j + 1], sgate[:], ALU.mult,
                            ALU.subtract)
                link(m)
                link(cp(topin2[:, :, 6:], lg[:]))
                for j in range(2):
                    m = nc.vector.max(top8[:, j, :], topin2[:, j, :])
                link(m)
                for j in range(2):
                    m = nc.vector.match_replace(rep[:, j, 0:6 + E1], top8[:, j, :], topin2[:, j, :], -BIG)
                ts(act1[:], lg[:], 0.0, None, ALU.is_gt)
                link(m)
                link(ts(rep[:, :, 32:32 + E1], rep[:, :, 6:6 + E1], -BIG, None, ALU.is_equal))
                link(red_(cnt[:], act1[:], AX.X, ALU.max))
                link(ts(cnt[:], cnt[:], -1.0, 1.0, ALU.mult, ALU.add))
                link(tt(rep[:, :, 32:32 + E1], rep[:, :, 32:32 + E1], cnt[:].broadcast_to([P, 2, E1]), ALU.mult))
                link(tt(act1[:], act1[:], rep[:, :, 32:32 + E1], ALU.max))
                link(ts(lg[:], lg[:], 0.0, None, ALU.max))
                link(red_(cnt[:], lg[:], AX.X, ALU.max))
                tt(lg[:], lg[:], cnt[:].broadcast_to([P, 2, E1]), ALU.subtract).then_inc(sig["l3_sub"], 1)
                dve.wait_ge(sig["l3_exp"], b + 1)
                link(tt(lg[:], lg[:], act1[:], ALU.mult))
                link(red_(cnt[:], lg[:], AX.X, ALU.add))
                link(rcp(cnt[:], cnt[:]))
                for j in range(2):
                    m = ts(G16[:, j, :].rearrange("p (k e) -> p k e", k=2)[:, :, 0:E1],
                           lg[:, j, :].unsqueeze(1).broadcast_to([P, 2, E1]), cnt[:, j, :], None, ALU.mult)
                m.then_inc(sig["g3_set"], 1)
                dve.wait_ge(sig["g3T_mm"], b + 1)
                g = gT3[:, b * T:(b + 1) * T]
                link(cp(g, PS[0:64, 2, 256:512]))
                tt(g[32:64, :], PS[32:64, 2, 256:512], g[32:64, :].bitcast(F32), ALU.subtract)\
                    .then_inc(sig["g3T_set"], 1)
                for k in range(8):
                    dve.wait_ge(sig["bc_mm"], 8 * b + k + 1)
                    if k == 0 and b:
                        dve.wait_ge(sig["qkv_mm2"], b)
                    hb = hT[:, b * T:(b + 1) * T].unsqueeze(1).broadcast_to([P, 2, T])
                    tt(xeT[:, 2 * k:2 * k + 2, :], PS[:, 4 + k % 2, :].rearrange("p (e t) -> p e t", e=2), hb,
                       ALU.mult).then_inc(sig["xe_set"], 1)
                return "xe_set", 8 * b + 8

            def B3(b):
                for j in range(2):
                    n = 2 * b + j
                    ks = (j + 1) * P
                    dve.wait_ge(sig["s3_mm"], n + 1)
                    if b:
                        dve.wait_ge(sig["PT3_mm"], 2 * b)
                    a = P if j == 0 else 0
                    link(tt(S3[:, j, 0:ks], PS[:, 6, 0:ks], w("causal")[:, a:a + ks], ALU.add))
                    link(red_(m3[:, j, :], S3[:, j, 0:ks], AX.X, ALU.max))
                    ts(S3[:, j, 0:ks], S3[:, j, 0:ks], m3[:, j, :], None, ALU.subtract).then_inc(sig["s3_sub"], 1)
                for j in range(2):
                    n = 2 * b + j
                    ks = (j + 1) * P
                    dve.wait_ge(sig["s3_exp"], n + 1)
                    link(rcp(m3[:, j, :], s3[:, j, :]))
                    ts(S3[:, j, 0:ks], S3[:, j, 0:ks], m3[:, j, :], None, ALU.mult).then_inc(sig["s3_norm"], 1)
                dve.wait_ge(sig["a3_mm"], 2 * b + 2)
                cp(aT3[:], PS[:, 3, 0:T]).then_inc(sig["a3_set"], 1)
                dve.wait_ge(sig["a3_set"], b + 1)
                for k in range(4):
                    dve.wait_ge(sig["bp_mm"], 4 * b + k + 1)
                    if k == 0 and b:
                        dve.wait_ge(sig["out_ready"], 3 * B + b)
                    ab = aT3[:].unsqueeze(1).broadcast_to([P, 2, T])
                    tt(mixT[:, 2 * k:2 * k + 2, :], PS[:, 6 + k % 2, :].rearrange("p (e t) -> p e t", e=2), ab,
                       ALU.mult).then_inc(sig["mix_set"], 1)
                return finish(3, b)

            def F5(b):
                dve.wait_ge(sig["r5_mm"], b + 1)
                lps = PS[:, 2, 0:2 * E2].rearrange("p (j e) -> p j e", j=2)
                link(red_(rs[:], lps, AX.X, ALU.max))
                tt(sc[:, :, 0:E2], lps, rs[:].broadcast_to([P, 2, E2]), ALU.subtract).then_inc(sig["r5_sub"], 1)
                dve.wait_ge(sig["r5_exp"], b + 1)
                link(red_(rs[:], sc[:, :, 0:E2], AX.X, ALU.add))
                link(rcp(rs[:], rs[:]))
                link(tt(sc[:, :, 0:E2], sc[:, :, 0:E2], rs[:].broadcast_to([P, 2, E2]), ALU.mult))
                link(cp(topin2[:, :, 6:6 + E2], sc[:, :, 0:E2]))
                for j in range(2):
                    m = nc.vector.max(top8[:, j, :], topin2[:, j, 0:6 + E2])
                link(m)
                for j in range(2):
                    m = nc.vector.match_replace(rep[:, j, 0:6 + E2], top8[:, j, :], topin2[:, j, 0:6 + E2], -BIG)
                link(m)
                ts(sel[:, 0:2, 0:E2], rep[:, :, 6:6 + E2], -BIG, None, ALU.is_equal).then_inc(sig["sel5"], 1)
                dve.wait_ge(sig["sel5"], b + 1)
                link(tt(sc[:, :, 0:E2], sc[:, :, 0:E2], sel[:, 0:2, 0:E2], ALU.mult))
                dve.wait_ge(sig["pos5"], b + 1)
                for j in range(2):
                    pos = PS[:, 2, 256 + j * E2:256 + (j + 1) * E2].unsqueeze(1).broadcast_to([P, 2, E2])
                    m = stt(G16[:, j, :].rearrange("p (k e) -> p k e", k=2)[:, :, 0:E2], pos, float(CAP2),
                            sc[:, j, 0:E2].unsqueeze(1).broadcast_to([P, 2, E2]), ALU.is_lt, ALU.mult)
                m.then_inc(sig["g5_set"], 1)
                dve.wait_ge(sig["g5T_mm"], b + 1)
                g = gT5[:, b * T:(b + 1) * T]
                link(cp(g, PS[0:64, 2, 0:256]))
                tt(g[32:64, :], PS[32:64, 2, 0:256], g[32:64, :].bitcast(F32), ALU.subtract)\
                    .then_inc(sig["g5T_set"], 1)
                return "g5T_set", b + 1

            def S6():
                for g in range(HK3):
                    dve.wait_ge(sig["vT6_mm"], g + 1)
                    o = vT6[:, g, :].rearrange("p (b j k) -> p b j k", j=2, k=KEYS)
                    i = PS[:, 3, :].rearrange("p (b j k) -> p b j k", j=2, k=KEYS)
                    for j in range(2):
                        m = ts(o[:, :, j, :], i[:, :, j, :], w("parity")[:, j:j + 1], None, ALU.mult)
                    m.then_inc(sig["vT6_set"], 1)
                return "vT6_set", HK3

            def F7(b):
                for m in range(M3):
                    n = b * M3 + m
                    dve.wait_ge(sig["silu7"], n + 1)
                    if b >= 2 and m == 0:
                        dve.wait_ge(sig["out_ready"], 7 * B + b - 1)
                    tt(H7[:, b % 2, m, :], sg7[:, m, :], PS[:, (4, 5, 2)[m], T:2 * T], ALU.mult)\
                        .then_inc(sig["h7_set"], 1)
                return "h7_set", M3 * (b + 1)

            nc.vector.memset(ones[:], 1.0)
            nc.vector.memset(vv[:, :, C:C + 1], 1.0)
            nc.vector.memset(topin[:, :, 0:2], BIG)
            nc.vector.memset(topin2[:, :, 0:6], BIG)
            nc.vector.memset(G16[:], 0.0).then_inc(sig["consts"], 1)
            dve.wait_ge(sig["consts"], 1)
            dve.wait_ge(load["first"], 16)
            layer_norm(0)
            dve.wait_ge(sig["ln_h"], 2)
            setup0()
            ended = "kvb_set", B
            for n in range(1, B):
                dve.wait_ge(sig[ended[0]], ended[1])
                ended = layer_norm(n)
            for kind, s, b in order:
                dve.wait_ge(sig[ended[0]], ended[1])
                if kind == "F":
                    if s in (2, 4, 6):
                        ended = softmax_tile(s, b)
                    else:
                        ended = {0: F0, 1: F1, 3: F3, 5: F5, 7: F7}[s](b)
                elif kind == "B":
                    if s in (6, 7):
                        ended = finish(s, b)
                    elif s in (2, 4):
                        ended = Bx(s, b)
                    else:
                        ended = {0: B0, 3: B3}[s](b)
                elif kind == "S" and s == 2:
                    dve.wait_ge(load["mix"], 16)
                    cp(rows32[:], w("half32")[0:64, :])
                    cp(pair16[:].rearrange("p (e d) -> p e d", d=D1), over(w("half32")[0:64, :], D1))
                    setup3()
                    S2()
                    ended = setup3b()
                elif kind == "S":
                    ended = S6()
                else:
                    ended = M(s, b)


def layout(i):
    f = {k: np.asarray(v) for k, v in i.items()}

    def rows(a, n=P):
        return np.broadcast_to(a.reshape(1, -1), (n, a.size))

    def tiles(a):
        return a.reshape(-1, P, a.shape[-1]).transpose(1, 0, 2).reshape(P, -1)

    def first_rows(parts):
        a = np.zeros((P, len(parts) * C), np.float32)
        for k, v in enumerate(parts):
            a[0, k * C:k * C + v.size] = v
        return a

    p = np.arange(P)
    ctx = f["ctx_1024"].reshape(B * KEYS, C).T
    ctx2 = np.repeat(ctx.reshape(C, B, 1, KEYS), 2, axis=2).reshape(C, -1)
    b2 = np.zeros((P, C), np.float32)
    b2[0:E2] = b2[32:32 + E2] = f["L2_ffn_b2"]
    half32 = ((p[:, None] % 32 == np.arange(E1)) & (p[:, None] < 64)).astype(np.float32)
    cols = np.arange(T)
    wq6 = f["L3_xattn_Wq"].reshape(2, 2, R3, D3, C).transpose(1, 3, 0, 2, 4).reshape(P, -1)
    qk3 = np.concatenate([f["L1_ffn_q_proj"], f["L1_ffn_k_proj"]], axis=2)
    a = {
        "x": tiles(f["x"].reshape(B * T, C)), "ctxT": ctx, "ctx2": ctx2,
        "wq0": f["L0_xattn_Wq"].T, "wkv0": np.concatenate([f["L0_xattn_Wk"].T, f["L0_xattn_Wv"].T], axis=1),
        "wp0": f["L0_xattn_Wp"].T,
        "rows0": first_rows([f["L0_xattn_bq"], f["L0_xattn_bk"], f["L0_xattn_bv"], f["L0_xattn_bp"], f["L2_ffn_br"]]),
        "ident": np.eye(P, dtype=np.float32), "headmask": (p[:, None] // D == np.arange(H)).astype(np.float32),
        "gain": np.concatenate([rows(f["g_xattn"]), rows(f["g_ffn"])], axis=1),
        "router0": f["L0_ffn_router_weight"].T, "ebias0": rows(f["L0_ffn_expert_bias"]),
        "earlier": (p[:, None] < p).astype(np.float32), "half64": (p[:, None] % E0 == np.arange(E0)).astype(np.float32),
        "wq2": f["L1_xattn_w_q"].T, "wk2": f["L1_xattn_w_k"].T, "wv2": f["L1_xattn_w_v"].T, "wo2": f["L1_xattn_w_o"].T,
        "wq4": f["L2_xattn_Wq"], "wk4": f["L2_xattn_Wk"], "wv4": f["L2_xattn_Wv"], "wo4": f["L2_xattn_Wo"],
        "parity": (p[:, None] // KEYS == np.arange(2)).astype(np.float32),
        "w1_0": np.concatenate([f["L0_ffn_w1"].transpose(1, 0, 2).reshape(C, -1), f["L0_ffn_sw1"].T], axis=1),
        "w2_0": np.concatenate([tiles(f["L0_ffn_w2"].reshape(-1, C)), tiles(f["L0_ffn_sw2"].T)], axis=1),
        "half32": half32, "sim": f["L1_ffn_sim_matrix"], "gates": rows(f["L1_ffn_gates"]),
        "qk3": qk3.transpose(1, 0, 2).reshape(C, -1), "v3": f["L1_ffn_v_proj"].transpose(1, 0, 2).reshape(C, -1),
        "o3": tiles(f["L1_ffn_o_proj"].reshape(-1, C)),
        "causal": np.where(cols[None, :] <= P + p[:, None], 0.0, -BIG).astype(np.float32),
        "router2": f["L2_ffn_Wr"], "b1_2": f["L2_ffn_b1"].reshape(-1, P).T, "b2_2": b2,
        "moe2a": f["L2_ffn_W1"].transpose(1, 0, 2).reshape(C, -1), "moe2b": tiles(f["L2_ffn_W2"].reshape(-1, C)),
        "wq6": wq6, "wk6": f["L3_xattn_Wk"].T,
        "wv6": np.repeat(f["L3_xattn_Wv"].T.reshape(C, HK3, 1, D3), 2, axis=2).reshape(C, -1),
        "wo6": tiles(f["L3_xattn_Wo"].T),
        "mask": rows(f["mask_BxS2_ik0"]), "wg": f["L3_ffn_w_gate"].T, "wu": f["L3_ffn_w_up"].T,
        "wd": tiles(f["L3_ffn_w_down"].T),
    }
    packs = {"p_" + k: np.ascontiguousarray(np.concatenate([a[n] for n, _ in v], axis=1)) for k, v in PACKS.items()}
    for k in LATER:
        packs["p_" + k] = np.ascontiguousarray(a[k])
    packs["p_gqa"] = np.ascontiguousarray(np.concatenate([a[n] for n, _ in GQA], axis=1))
    packs["p_ints"] = np.ascontiguousarray(np.concatenate([a[n] for n, _ in IPACK], axis=1))
    return packs


def kernel(**inputs):
    import concourse.bacc as bacc
    from concourse.bass_utils import run_bass_kernel_spmd

    nc = bacc.Bacc("TRN2", target_bir_lowering=False, num_devices=1)
    arrays = layout(inputs)
    aps = {k: nc.dram_tensor(k, a.shape, mybir.dt.from_np(a.dtype), kind="ExternalInput").ap()
           for k, a in arrays.items()}
    out = nc.dram_tensor("out", (P, NT * C), F32, kind="ExternalOutput").ap()
    flamingo_blocks(nc, {k[2:]: v for k, v in aps.items()}, aps["p_ints"], out)
    r = run_bass_kernel_spmd(nc, [arrays], core_ids=[0])
    y = r.results[0]["out"]
    return y.reshape(P, NT, C).transpose(1, 0, 2).reshape(B, T, C)
```

```python
from contextlib import ExitStack

import numpy as np
import concourse.bass as bass
from concourse import mybir

F32 = mybir.dt.float32
F32R = mybir.dt.float32r
I32 = mybir.dt.int32
ALU = mybir.AluOpType
ACT = mybir.ActivationFunctionType
AX = mybir.AxisListType

P = 128
B, T, C = 4, 256, 128
NT = B * T // P
KEYS = 64
H, D = 16, 8
EPS = 1e-5
BIG = 1e30

E0, K0, HID0, CAP0 = 64, 6, 64, 48
SH0 = 256
E1, D1 = 16, 64
E2, K2, HID2 = 8, 2, 512
CAP2 = int(T / E2 * 1.25)
HK3, D3, R3 = 4, 64, 4
M3 = 3
FMIN = float(np.finfo(np.float32).min)

PACKS = {
    "first": [("x", NT * C), ("ctxT", B * KEYS), ("wq0", C), ("wkv0", 2 * C), ("rows0", 5 * C), ("ident", P),
              ("headmask", H), ("gain", 8)],
    "attn": [("wp0", C), ("router0", E0), ("ebias0", E0), ("earlier", P), ("half64", E0), ("ctx2", B * 2 * KEYS),
             ("wq2", C), ("wk2", C), ("wv2", C), ("wo2", C), ("wq4", C), ("wk4", C), ("wv4", C), ("wo4", C),
             ("parity", 2)],
    "moe0a": [("w1_0", (E0 * HID0 + SH0))],
    "moe0b": [("w2_0", (E0 * HID0 + SH0) // P * C)],
    "mix": [("half32", E1), ("sim", E1), ("gates", E1), ("qk3", E1 * P), ("v3", E1 * D1), ("o3", E1 * D1 // P * C),
            ("causal", T)],
    "moe2": [("router2", E2), ("b1_2", E2 * HID2 // P), ("b2_2", E2), ("slots2", CAP2)],
}
GQA = [("wq6", HK3 // 2 * R3 * C), ("wk6", HK3 * D3), ("wv6", HK3 * 2 * D3), ("wo6", H * D3 // P * C)]
LATER = {"moe2a": ("w1_0", E2 * HID2), "moe2b": ("w2_0", E2 * HID2 // P * C)}
IPACK = [("mask", B * KEYS), ("wg", M3 * P), ("wu", M3 * P), ("wd", M3 * C)]


def spans(fields):
    at, out = 0, {}
    for name, n in fields:
        out[name] = (at, at + n)
        at += n
    return out, at


def flamingo_blocks(nc, packed, ints, out):
    ctx = ExitStack()
    with ctx:
        def sb(name, shape, dt=F32):
            return ctx.enter_context(nc.sbuf_tensor(name, shape, dt))

        where, ctx_in = {}, {}
        for pk, fields in PACKS.items():
            sp, n = spans(fields)
            t = sb("in_" + pk, [P, n])
            ctx_in[pk] = t
            for name, (a, z) in sp.items():
                where[name] = t[:, a:z]
        for name, (a, z) in spans(GQA)[0].items():
            o = spans(PACKS["mix"])[0]["qk3"][0]
            where[name] = ctx_in["mix"][:, o + a:o + z]
        sp, n = spans(IPACK)
        ipk = sb("in_ints", [P, n], I32)
        fpk = ipk[:].bitcast(F32)
        for name, (a, z) in sp.items():
            where[name] = fpk[:, a:z]

        def w(name):
            return where[name]

        X = w("x").rearrange("p (t c) -> p t c", c=C)
        ident = w("ident")
        row0 = w("rows0").rearrange("p (k c) -> p k c", c=C)
        hm = w("headmask")
        ones = sb("ones", [P, P])
        half_neg = sb("half_neg", [P, E1])

        st = sb("ln_stats", [P, NT, 6])
        mv = sb("ln_mean_var", [P, NT, 2])
        vareps = sb("ln_var_eps", [P, NT])
        rstd = sb("ln_rstd", [P, NT])
        hN = sb("ln_h", [P, NT, C])
        hT = sb("hT", [P, B * T])

        att = sb("attention", [P, 3 * B * T])
        qT, oT = att[:, 0:B * T], att[:, 2 * B * T:]
        O = att[:, B * T:2 * B * T].rearrange("p (t c) -> p t c", c=C)
        gain = sb("tanh_gain", [P, 8])

        kk = sb("k_soft", [P, 2, C])
        vv = sb("v_ones", [P, 2, C + 1])
        kvb = sb("kv_blocks", [P, B, C + H])
        red = sb("red", [P, 2, 2 * H])
        red2 = sb("red2", [P, 2, 2 * H])

        kT = sb("kT", [P, 2, B * KEYS])
        kblk = {2: sb("kblk2", [P, B, H * KEYS]), 4: sb("kblk4", [P, B, H * KEYS])}
        v18 = {2: sb("v18_2", [P, B, H * (D + 1)]), 4: sb("v18_4", [P, B, H * (D + 1)])}
        A6 = kblk[2]
        VO6 = kblk[4][:].rearrange("p b (k c) -> p b k c", c=C)
        kT6 = kT
        S = sb("scores", [P, 6, 512])
        PT = sb("probsT", [P, 4, 512])
        smax = sb("smax", [P, 2, H // 2])
        ssum = sb("ssum", [P, 2, H // 2])
        rden = sb("rden", [P, 2, H])

        sc = sb("scores_r", [P, 4, E0])
        topin = sb("topin", [P, 4, 2 + E0])
        rep = sb("replaced", [P, 4, 2 + E0])
        top8 = sb("top8", [P, NT, 8])
        sel = sb("chosen", [P, NT, E0])
        wts = sb("weights", [P, 4, E0])
        rs = sb("rsum", [P, NT, 1])
        GG = sb("gates_tok", [P, 4, 2 * E0])
        gT = sb("gateT", [P, B * T], F32R)
        gT3 = gT[0:64, :]

        rows32 = sb("rows32", [64, E1], F32R)
        pair16 = sb("pair16", [64, E1 * D1], F32R)
        simn = sb("sim_n", [P, E1])
        simss = sb("sim_sumsq", [P, E1])
        siminv = sb("sim_inv", [P, E1])
        simsq = sb("sim_sq", [P, E1])
        sgate = sb("sgate", [P, E1])
        ss = sb("sumsq", [P, NT])
        rn = sb("rnorm", [P, NT])
        lg = sb("logits16", [P, NT, E1])
        on = sb("active16", [P, NT, E1])
        fb = sb("fallback16", [P, NT, E1])
        topin2 = sb("topin16", [P, NT, 6 + E1])
        rep2 = sb("replaced16", [P, NT, 6 + E1])
        cnt = sb("count16", [P, NT, 1])
        G16 = sb("gates16", [P, NT, 64])

        REGION = 5800
        with nc.sbuf_tensor("spread64", [P, E0 * HID0], F32R) as early:
            spread64 = early
        region = sb("region", [P, REGION])

        def carve(at, *shape):
            n = int(np.prod(shape))
            a = region[:, at:at + n]
            if len(shape) > 1:
                names = "abc"[:len(shape)]
                a = a.rearrange("p (" + " ".join(names) + ") -> p " + " ".join(names), **dict(zip(names, shape)))
            return a, at + n

        H1, at = carve(E0 * HID0, 2, 512)
        Hg = PT[:, 0:3, :]
        accS = S[:, 0:2, :]

        xeT = S[:, 0:4, :]
        mixT = PT
        qT3, at = carve(0, B, T)
        kT3, at = carve(at, B, T)
        v3d, at = carve(at, B, 2, 2 * D1)
        S3, at = carve(at, 4, T)
        PT3, at = carve(at, 2, T)
        aT3, at = carve(at, B, T)
        m3, at = carve(at, 4)
        s3, at = carve(at, 4)
        junk, at = carve(at, C)

        SL = E2 * CAP2
        D5, at = carve(0, NT, SL)
        PT5 = att[:].rearrange("p (t n) -> p t n", t=NT)
        Y5 = D5[:].rearrange("p t n -> p (t n)")[:, 0:B * 3 * C].rearrange("p (b n) -> p b n", b=B)
        XS5, at = carve(at, E2, B * CAP2)
        YT5, at = carve(at, B, SL)
        H5, at = carve(at, 4, B * CAP2)
        Dw5 = S[:].rearrange("p k n -> p (k n)")[:, 0:NT * SL].rearrange("p (t n) -> p t n", t=NT)
        vT6 = PT[:]
        sg7, at = carve(0, 3, T)
        H7, at = carve(at, 2, M3, T)

        PS = ctx.enter_context(nc.psum_tensor("banks", [P, 8, 512], F32))

        def sem(name):
            return ctx.enter_context(nc.semaphore(name))

        load = {pk: sem("load_" + pk) for pk in list(PACKS) + list(LATER) + ["gqa"]}
        load_ints = sem("load_ints")
        stored = sem("stored")
        names = """consts half_set gain_set spread_set rows_set ints_cast dve_step pool_step
            ln_var ln_rstd ln_h ln_T hT out_ready resid
            k0_mm k0_sub k0_exp k0_soft kv0_mm kvb_set q0_mm q0_sub q0_exp q0_soft q0T_mm q0T_set kvo_mm
            kT_mm kT_set kblk_set v_mm v18_set sim_sq sim_mm sim_ss sim_pw sim_set sg_exp
            o_tok pv_out oT_mm oT_set q_mm q_set sc_mm sc_sub sc_exp sc_sum sc_norm PT_mm PT_set pv_mm
            r1_mm r1_exp sel_set pos_mm gg_set ggT_mm gT_set mA mG h1 hg hg_used acc_evac
            ss_set ss_pw l3_mm l3_sub l3_exp g3_set g3T_mm g3T_set bc_mm xe_set xe_used qkv_set
            s3_mm s3_sub s3_exp s3_norm PT3_mm PT3_set a3_mm a3_set bp_mm mix_set mix_used
            r5_mm r5_sub r5_exp sel5 pos5 d5_set dw5_set xs_mm xs_set pt5_mm pt5_set h5_mm h5_set h5_used
            y5_mm yt_set y5T_mm y5_set kT6_mm kT6_set vT6_mm vT6_set A6_mm A6_set vo_mm vo_set
            gu_mm silu7 h7_set""".split()
        sig = {n: sem(n) for n in names}

        block = ctx.enter_context(nc.Block())

        HALF = 512
        STEPS1 = (E0 * HID0 + SH0) // P
        GATED1 = E0 * HID0 // P
        ATT = [0, 2, 4]
        KV0 = [3, 4, 5, 7]
        FIN = 4
        UNITS = 2 * NT
        UBASE = {2: 0, 4: UNITS, 6: 2 * UNITS}
        UBANK = {2: [4, 5, 6, 7], 4: [4, 5, 6, 7], 6: [2, 3, 4, 5, 6, 7]}
        LAG = {2: 2, 4: 2, 6: 4}
        SCALE = {2: D ** -0.5, 4: D ** -0.5, 6: D3 ** -0.5}
        OUT = {0: 0, 1: B, 2: 2 * B, 4: 3 * B, 5: 4 * B, 7: 5 * B}
        GRP = [(0, 3), (3, 6), (6, 8)]

        def heads(ap, d=D):
            return ap.rearrange("p (h d) -> p h d", d=d)

        def bank(k):
            return PS[:, k, :]

        def ubank(s, u):
            return UBANK[s][u % len(UBANK[s])]

        @block.sync
        def _(sp):
            for pk in ["first", "attn", "moe0a", "moe0b", "mix", "moe2"]:
                sp.dma_start(ctx_in[pk][:], packed[pk]).then_inc(load[pk], 16)
            sp.dma_start(ipk[:], ints).then_inc(load_ints, 16)
            sp.wait_ge(sig["hg_used"], 2 * STEPS1)
            for pk, (name, n) in LATER.items():
                sp.dma_start(w(name)[:, 0:n], packed[pk]).then_inc(load[pk], 16)
            sp.wait_ge(sig["mix_used"], B * E1 // 4)
            o, n = spans(PACKS["mix"])[0]["qk3"][0], spans(GQA)[1]
            sp.dma_start(ctx_in["mix"][:, o:o + n], packed["gqa"]).then_inc(load["gqa"], 16)
            for b in range(B):
                sp.wait_ge(sig["resid"], 7 * B + b + 1)
                sp.dma_start(out[:, 2 * b * C:(2 * b + 2) * C],
                             w("x")[:, 2 * b * C:(2 * b + 2) * C]).then_inc(stored, 16)
            sp.wait_ge(stored, 16 * B)

        @block.gpsimd
        def _(pool):
            tt = nc.gpsimd.tensor_tensor
            nc.gpsimd.memset(half_neg[:], -0.5).then_inc(sig["half_set"], 1)
            pool.wait_ge(sig["half_set"], 1)

            def rsqrt(s, batches=range(B)):
                for b in batches:
                    n = s * B + b
                    pool.wait_ge(sig["ln_var"], n + 1)
                    t = slice(2 * b, 2 * b + 2)
                    tt(rstd[:, t], vareps[:, t], half_neg[:, 0:2], ALU.pow).then_inc(sig["ln_rstd"], 1)

            def key_blocks(s):
                k = s // 4
                pool.wait_ge(sig["kT_set"], 1)
                for b in range(B):
                    a = kT[:, k, b * KEYS:(b + 1) * KEYS].unsqueeze(1).broadcast_to([P, H, KEYS])
                    tt(heads(kblk[s][:, b, :], KEYS), a, hm.unsqueeze(2).broadcast_to([P, H, KEYS]), ALU.mult)\
                        .then_inc(sig["kblk_set"], 1)

            rsqrt(0)
            pool.wait_ge(load["attn"], 16)
            nc.gpsimd.tensor_copy(spread64[:].rearrange("p (e d) -> p e d", d=HID0),
                                  w("half64").unsqueeze(2).broadcast_to([P, E0, HID0])).then_inc(sig["spread_set"], 1)
            key_blocks(2)
            rsqrt(1)
            pool.wait_ge(sig["sim_ss"], 1)
            tt(siminv[:], simss[:], half_neg[:], ALU.pow).then_inc(sig["sim_pw"], 1)
            key_blocks(4)
            pool.wait_ge(load_ints, 16)
            nc.gpsimd.tensor_copy(fpk, ipk[:]).then_inc(sig["pool_step"], 1)
            pool.wait_ge(sig["pool_step"], 1)
            a = B * KEYS
            nc.gpsimd.tensor_scalar(fpk[:, a:], fpk[:, a:], 1.0 / 127.0, None, ALU.mult)
            nc.gpsimd.tensor_scalar(fpk[:, 0:a], fpk[:, 0:a], -1.0, 1.0, ALU.mult, ALU.add)\
                .then_inc(sig["pool_step"], 1)
            pool.wait_ge(sig["pool_step"], 2)
            nc.gpsimd.tensor_scalar(fpk[:, 0:a], fpk[:, 0:a], FMIN, None, ALU.mult).then_inc(sig["ints_cast"], 1)
            rsqrt(2)
            rsqrt(3)
            pool.wait_ge(sig["ss_set"], 1)
            tt(rn[:], ss[:], half_neg[:, 0:NT], ALU.pow).then_inc(sig["ss_pw"], 1)
            rsqrt(4)
            rsqrt(5)
            rsqrt(6)
            for u in range(UNITS):
                if u % 4 == 0 and u >= 8:
                    rsqrt(7, [u // 4 - 2])
                pool.wait_ge(sig["sc_sum"], u + 1)
                tt(heads(S[:, u % 6, :], KEYS), heads(S[:, u % 6, :], KEYS),
                   ssum[:, u % 2, :].unsqueeze(2).broadcast_to([P, H // 2, KEYS]), ALU.mult)\
                    .then_inc(sig["sc_norm"], 1)
            rsqrt(7, [B - 2, B - 1])

        @block.tensor
        def _(pe):
            mm, tr = nc.tensor.matmul, nc.tensor.transpose

            def h(b, j=None):
                a = 2 * b * P
                return hT[:, a:a + 2 * P] if j is None else hT[:, a + j * P:a + (j + 1) * P]

            def ln_T(s, b):
                n = s * B + b
                pe.wait_ge(sig["ln_h"], 2 * n + 2)
                if b >= 2:
                    pe.wait_ge(sig["hT"], n - 1)
                for j in range(2):
                    m = tr(bank(6 + b % 2)[:, j * P:(j + 1) * P], hN[:, 2 * b + j, :], ident)
                m.then_inc(sig["ln_T"], 1)

            def got_hT(s, b):
                pe.wait_ge(sig["hT"], s * B + b + 1)

            def out_free(s, b):
                n = s * B + b
                if n >= 2:
                    pe.wait_ge(sig["resid"], n - 1)

            def setup_kv0():
                pe.wait_ge(load["first"], 16)
                pe.wait_ge(sig["consts"], 1)
                for j in range(2):
                    o = bank(6 + j)[:, 0:2 * C]
                    mm(o, ones[0:1, :], row0[0:1, 1:3, :], start=True, stop=False)
                    mm(o, w("ctxT")[:, j * P:(j + 1) * P], w("wkv0"), start=False, stop=True).then_inc(sig["k0_mm"], 1)
                for b in range(B):
                    pe.wait_ge(sig["k0_soft"], b // 2 + 1)
                    r = slice((b % 2) * KEYS, (b % 2 + 1) * KEYS)
                    mm(bank(KV0[b])[:, 0:C + 1], kk[r, b // 2, :], vv[r, b // 2, :], start=True, stop=True)\
                        .then_inc(sig["kv0_mm"], 1)

            def attn0():
                for b in range(B):
                    ln_T(0, b)
                    got_hT(0, b)
                    if b == 0:
                        pe.wait_ge(sig["kvb_set"], B)
                    if b >= 2:
                        pe.wait_ge(sig["q0_sub"], b - 1)
                    for j in range(2):
                        o = bank(2 + b % 2)[:, j * C:(j + 1) * C]
                        mm(o, ones[0:1, :], row0[0:1, 0, :], start=True, stop=False)
                        m = mm(o, h(b, j), w("wq0"), start=False, stop=True)
                    m.then_inc(sig["q0_mm"], 1)
                pe.wait_ge(load["attn"], 16)
                for k, s in enumerate((2, 4)):
                    m = mm(bank(4)[:, k * 256:(k + 1) * 256], w(f"wk{s}"), w("ctxT"), start=True, stop=True)
                m.then_inc(sig["kT_mm"], 1)
                for b in range(B):
                    m = mm(bank(5)[:, b * C:(b + 1) * C], w("ctx2")[:, b * P:(b + 1) * P], w("wv2"),
                           start=True, stop=True)
                m.then_inc(sig["v_mm"], 1)
                for i in range(B + 3):
                    if i < B:
                        b = i
                        pe.wait_ge(sig["q0_soft"], b + 1)
                        pe.wait_ge(sig["hT"], B) if b < 2 else pe.wait_ge(sig["q0T_set"], b - 1)
                        for j in range(2):
                            m = tr(bank(6 + b % 2)[:, j * P:(j + 1) * P], O[:, 2 * b + j, :], ident)
                        m.then_inc(sig["q0T_mm"], 1)
                    if 1 <= i <= B:
                        b = i - 1
                        pe.wait_ge(sig["q0T_set"], b + 1)
                        if b >= 2:
                            pe.wait_ge(sig["o_tok"], b - 1)
                        else:
                            pe.wait_ge(sig["q0_sub"], B)
                        for j in range(2):
                            m = mm(bank(2 + b % 2)[:, j * (C + H):(j + 1) * (C + H)],
                                   qT[:, (2 * b + j) * P:(2 * b + j + 1) * P], kvb[:, b, :], start=True, stop=True)
                        m.then_inc(sig["kvo_mm"], 1)
                    if 2 <= i <= B + 1:
                        o_transpose(0, i - 2, 4)
                    if i >= 3:
                        o_project(0, i - 3, w("wp0"), row0[0:1, 3, :])

            def o_transpose(s, b, first):
                k = ATT.index(s) * B + b
                if s == 0:
                    pe.wait_ge(sig["o_tok"], b + 1)
                else:
                    pe.wait_ge(sig["pv_out"], (s // 4) * NT + 2 * b + 2)
                if (s, b) == (0, 0):
                    pe.wait_ge(sig["kT_set"], 1)
                if (s, b) == (0, 1):
                    pe.wait_ge(sig["v18_set"], B)
                if b >= 2:
                    pe.wait_ge(sig["oT_set"], k - 1)
                for j in range(2):
                    m = tr(bank(first + b % 2)[:, j * P:(j + 1) * P], O[:, 2 * b + j, :], ident)
                m.then_inc(sig["oT_mm"], 1)

            def o_project(s, b, wo, bias=None):
                k = ATT.index(s) * B + b
                pe.wait_ge(sig["oT_set"], k + 1)
                out_free(s, b)
                for j in range(2):
                    o = bank(b % 2)[:, j * C:(j + 1) * C]
                    if bias is not None:
                        mm(o, ones[0:1, :], bias, start=True, stop=False)
                    m = mm(o, oT[:, (2 * b + j) * P:(2 * b + j + 1) * P], wo, start=bias is None, stop=True)
                m.then_inc(sig["out_ready"], 1)

            def router1():
                for b in range(B):
                    ln_T(1, b)
                for hf in range(2):
                    for b in (2 * hf, 2 * hf + 1):
                        got_hT(1, b)
                        pe.wait_ge(sig["o_tok"], B)
                        for j in range(2):
                            i = 2 * (b % 2) + j
                            m = mm(bank(2 + hf)[:, i * E0:(i + 1) * E0], h(b, j), w("router0"), start=True, stop=True)
                    m.then_inc(sig["r1_mm"], 1)
                pe.wait_ge(sig["oT_set"], B)
                for b in range(B):
                    m = mm(bank(5)[:, b * C:(b + 1) * C], w("ctx2")[:, b * P:(b + 1) * P], w("wv4"),
                           start=True, stop=True)
                m.then_inc(sig["v_mm"], 1)
                for hf in range(2):
                    pe.wait_ge(sig["sel_set"], hf + 1)
                    for j in range(4):
                        i = 4 * hf + j
                        o = bank(2 + hf)[:, 256 + j * E0:256 + (j + 1) * E0]
                        for k in range(i):
                            mm(o, ones[:], sel[:, k, :], start=(k == 0), stop=False)
                        m = mm(o, w("earlier"), sel[:, i, :], start=(i == 0), stop=True)
                    m.then_inc(sig["pos_mm"], 1)
                    pe.wait_ge(sig["gg_set"], hf + 1)
                    for j in range(4):
                        m = tr(bank(6 + hf)[:, j * P:(j + 1) * P], GG[:, j, :], ident)
                    m.then_inc(sig["ggT_mm"], 1)
                pe.wait_ge(sig["sim_sq"], 1)
                mm(bank(4)[:, 0:E1], ones[:], simsq[:], start=True, stop=True).then_inc(sig["sim_mm"], 1)

            def experts1():
                w1 = w("w1_0").rearrange("p (m k) -> p m k", k=P)
                w2 = w("w2_0").rearrange("p (m k) -> p m k", k=C)
                for pk in ("moe0a", "moe0b"):
                    pe.wait_ge(load[pk], 16)
                pe.wait_ge(sig["spread_set"], 1)
                pe.wait_ge(sig["sim_ss"], 1)
                pe.wait_ge(sig["v18_set"], 2 * B)
                pe.wait_ge(sig["gT_set"], 2)

                def finish(hf):
                    pe.wait_ge(sig["acc_evac"], hf + 1)
                    pe.wait_ge(sig["resid"], B)
                    for j in range(4):
                        m = tr(bank(hf)[:, j * P:(j + 1) * P], accS[:, hf, j * P:(j + 1) * P], ident)
                    m.then_inc(sig["out_ready"], 2)

                for i in range(2 * STEPS1 + 2):
                    if i < 2 * STEPS1:
                        hf, m = divmod(i, STEPS1)
                        t = slice(hf * HALF, (hf + 1) * HALF)
                        if i >= 2:
                            pe.wait_ge(sig["h1"], i - 1)
                        mm(bank(6 + i % 2), w1[:, m, :], hT[:, t], start=True, stop=True).then_inc(sig["mA"], 1)
                        if m < GATED1:
                            if i >= 2:
                                pe.wait_ge(sig["hg"], i - 1)
                            mm(bank(4 + i % 2), spread64[:, m * P:(m + 1) * P], gT[:, t], start=True, stop=True)\
                                .then_inc(sig["mG"], 1)
                    if i >= 2:
                        hf, m = divmod(i - 2, STEPS1)
                        pe.wait_ge(sig["hg"], i - 1)
                        mm(bank(2 + hf), w2[:, m, :], Hg[:, (i - 2) % 3, :], start=(m == 0), stop=(m == STEPS1 - 1))\
                            .then_inc(sig["hg_used"], 1)
                    if i == STEPS1 + 2 + FIN:
                        finish(0)
                finish(1)

            def unit_scores(s, u):
                v = UBASE[s] + u
                t, k = divmod(u, 2)
                n = len(UBANK[s])
                if u >= n:
                    pe.wait_ge(sig["PT_set"], v - n + 1)
                lh = hT[:, t * P:(t + 1) * P] if s == 6 else qT[:, t * P:(t + 1) * P]
                mat = A6 if s == 6 else kblk[s]
                mm(bank(ubank(s, u)), lh, mat[:, t // 2, k * 512:(k + 1) * 512], start=True, stop=True)\
                    .then_inc(sig["sc_mm"], 1)

            def unit_transpose(s, u):
                v = UBASE[s] + u
                pe.wait_ge(sig["sc_norm"], u + 1) if s == 6 else pe.wait_ge(sig["sc_exp"], v + 1)
                for i in range(4):
                    m = tr(bank(ubank(s, u))[:, i * P:(i + 1) * P], S[:, u % 6, i * P:(i + 1) * P], ident)
                m.then_inc(sig["PT_mm"], 1)

            def attention(s):
                k = s // 4
                for i in range(B + 1):
                    if i < B:
                        ln_T(s, i)
                    if i >= 1:
                        b = i - 1
                        got_hT(s, b)
                        if b < 2:
                            pe.wait_ge(sig["acc_evac"], 2) if s == 2 else pe.wait_ge(sig["a3_set"], B)
                        else:
                            pe.wait_ge(sig["q_set"], k * B + b - 1)
                        mm(bank(2 + b % 2)[:, 0:256], w(f"wq{s}"), h(b), start=True, stop=True).then_inc(sig["q_mm"], 1)
                pe.wait_ge(sig["q_set"], (k + 1) * B)
                lag = LAG[s]
                for i in range(UNITS + lag + 1):
                    if i < UNITS:
                        if i % 4 == 0:
                            pe.wait_ge(sig["kblk_set"], k * B + i // 4 + 1)
                        unit_scores(s, i)
                    if lag <= i < UNITS + lag:
                        unit_transpose(s, i - lag)
                    if i >= lag + 1:
                        u = i - lag - 1
                        t, q = divmod(u, 2)
                        pe.wait_ge(sig["PT_set"], UBASE[s] + u + 1)
                        if q == 0 and t >= 2:
                            pe.wait_ge(sig["pv_out"], k * NT + t - 1)
                        for c in range(4):
                            a = (4 * q + c) * 18
                            m = mm(bank(2 + t % 2)[:, a:a + 18], PT[:, u % 4, c * P:(c + 1) * P],
                                   v18[s][:, t // 2, a:a + 18], start=True, stop=True)
                        m.then_inc(sig["pv_mm"], 1)
                for i in range(B + 1):
                    if i < B:
                        o_transpose(s, i, 4)
                    if i >= 1:
                        o_project(s, i - 1, w(f"wo{s}"))

            def mixture3():
                pe.wait_ge(load["mix"], 16)
                pe.wait_ge(sig["sim_set"], 1)
                for i in range(B + 1):
                    if i < B:
                        ln_T(3, i)
                    if i >= 1:
                        b = i - 1
                        got_hT(3, b)
                        if b == 0:
                            pe.wait_ge(sig["pv_out"], NT)
                        for j in range(2):
                            t = 2 * b + j
                            m = mm(bank(2)[:, t * E1:(t + 1) * E1], h(b, j), simn[:], start=True, stop=True)
                m.then_inc(sig["l3_mm"], 1)
                pe.wait_ge(sig["g3_set"], 1)
                pe.wait_ge(sig["oT_set"], 2 * B)
                for t in range(NT):
                    m = tr(bank(4 + t // 4)[0:64, (t % 4) * P:(t % 4 + 1) * P], G16[:, t, :], ident)
                    if t % 4 == 3:
                        m.then_inc(sig["g3T_mm"], 1)
                n = E1 // 2
                for i in range(B * n + 2):
                    if i < B * n:
                        b, k = divmod(i, n)
                        pe.wait_ge(sig["g3T_set"], 2) if i < 2 else pe.wait_ge(sig["xe_set"], i - 1)
                        for q in range(2):
                            m = mm(bank(4 + i % 2)[:, q * T:(q + 1) * T],
                                   rows32[:, 2 * k + q:2 * k + q + 1].broadcast_to([64, P]),
                                   gT3[:, b * T:(b + 1) * T], start=True, stop=True)
                        m.then_inc(sig["bc_mm"], 1)
                    if i >= 2:
                        v = i - 2
                        b, k = divmod(v, n)
                        pe.wait_ge(sig["xe_set"], v + 1)
                        if k == 0 and b >= 2:
                            pe.wait_ge(sig["qkv_set"], 4 * (b - 1))
                        for q in range(2):
                            e = 2 * k + q
                            xe = xeT[:, v % 4, q * T:(q + 1) * T]
                            mm(bank(2 + b % 2)[:, 0:T], w("qk3")[:, e * P:(e + 1) * P], xe, start=(e == 0),
                               stop=(e == E1 - 1))
                            for j in range(2):
                                m = mm(bank(6 + b % 2)[:, j * D1:(j + 1) * D1], xe[:, j * P:(j + 1) * P],
                                       w("v3")[:, e * D1:(e + 1) * D1], start=(e == 0 and j == 0),
                                       stop=(e == E1 - 1), skip_group_check=True)
                        m.then_inc(sig["xe_used"], 1)
                for i in range(NT + 3):
                    if i < NT:
                        b, j = divmod(i, 2)
                        keys = (j + 1) * P
                        pe.wait_ge(sig["qkv_set"], 4 * B)
                        if i >= 2:
                            pe.wait_ge(sig["s3_sub"], i - 1)
                        mm(bank(4 + i % 2)[:, 0:keys], qT3[0:D1, b, j * P:(j + 1) * P], kT3[0:D1, b, 0:keys],
                           start=True, stop=True).then_inc(sig["s3_mm"], 1)
                    if 2 <= i < NT + 2:
                        t = i - 2
                        j = t % 2
                        pe.wait_ge(sig["s3_norm"], t + 1)
                        if t >= 2:
                            pe.wait_ge(sig["PT3_set"], t - 1)
                        for k in range(j + 1):
                            m = tr(bank(6 + t % 2)[:, k * P:(k + 1) * P], S3[:, t % 4, k * P:(k + 1) * P], ident)
                        m.then_inc(sig["PT3_mm"], 1)
                    if i >= 3:
                        t = i - 3
                        b, j = divmod(t, 2)
                        pe.wait_ge(sig["PT3_set"], t + 1)
                        if j == 0 and b >= 2:
                            pe.wait_ge(sig["a3_set"], b - 1)
                        for k in range(j + 1):
                            m = mm(bank(2 + b % 2)[:, j * P:(j + 1) * P], v3d[:, b, k, :],
                                   PT3[:, t % 2, k * P:(k + 1) * P], start=(k == 0), stop=(k == j))
                        m.then_inc(sig["a3_mm"], 1)
                n = E1 // 4
                for i in range(B * n + 2):
                    if i < B * n:
                        b, k = divmod(i, n)
                        pe.wait_ge(sig["s3_sub"], NT) if i < 2 else pe.wait_ge(sig["mix_set"], i - 1)
                        for q in range(2):
                            p = 2 * k + q
                            m = mm(bank(4 + i % 2)[:, q * T:(q + 1) * T], pair16[:, p * P:(p + 1) * P],
                                   gT3[:, b * T:(b + 1) * T], start=True, stop=True)
                        m.then_inc(sig["bp_mm"], 1)
                    if i >= 2:
                        v = i - 2
                        b, k = divmod(v, n)
                        pe.wait_ge(sig["mix_set"], v + 1)
                        if k == 0:
                            out_free(3, b)
                        for q in range(2):
                            p = 2 * k + q
                            for j in range(2):
                                m = mm(bank(b % 2)[:, j * C:(j + 1) * C],
                                       mixT[:, v % 4, q * T + j * P:q * T + (j + 1) * P],
                                       w("o3")[:, p * C:(p + 1) * C], start=(p == 0 and j == 0),
                                       stop=(p == E1 // 2 - 1), skip_group_check=True)
                        m.then_inc(sig["mix_used"], 1)

            def experts5():
                pe.wait_ge(load["moe2"], 16)
                for i in range(B + 1):
                    if i < B:
                        ln_T(5, i)
                    if i >= 1:
                        b = i - 1
                        got_hT(5, b)
                        if b == 0:
                            pe.wait_ge(sig["pv_out"], 2 * NT)
                        for j in range(2):
                            t = 2 * b + j
                            o = bank(2)[:, t * E2:(t + 1) * E2]
                            mm(o, ones[0:1, :], row0[0:1, 4, 0:E2], start=True, stop=False)
                            m = mm(o, h(b, j), w("router2"), start=False, stop=True)
                m.then_inc(sig["r5_mm"], 1)
                setup6()
                pe.wait_ge(sig["sel5"], 1)
                for t in range(NT):
                    o = bank(2)[:, 256 + t * E2:256 + (t + 1) * E2]
                    if t % 2:
                        mm(o, ones[:], sel[:, t - 1, 0:E2], start=True, stop=False)
                    m = mm(o, w("earlier"), sel[:, t, 0:E2], start=(t % 2 == 0), stop=True)
                m.then_inc(sig["pos5"], 1)
                for b in range(B):
                    pe.wait_ge(sig["d5_set"], 2 * b + 2)
                    pe.wait_ge(sig["A6_set"], H // 2) if b < 2 else pe.wait_ge(sig["xs_set"], b - 1)
                    for j in range(2):
                        t = 2 * b + j
                        m = mm(bank(4 + b % 2)[:, 0:SL], hN[:, t, :], D5[:, t, :], start=(j == 0), stop=(j == 1))
                    m.then_inc(sig["xs_mm"], 1)
                for t in range(NT):
                    pe.wait_ge(sig["dw5_set"], t + 1)
                    pe.wait_ge(sig["vo_set"], B * HK3) if t < 2 else pe.wait_ge(sig["pt5_set"], t - 1)
                    for g, (a, z) in enumerate(GRP):
                        m = tr(bank(6 + t % 2)[0:(z - a) * CAP2, g * P:(g + 1) * P],
                               Dw5[:, t, a * CAP2:z * CAP2], ident)
                    m.then_inc(sig["pt5_mm"], 1)
                w1 = w("w1_0")[:, 0:E2 * HID2].rearrange("p (m k) -> p m k", k=P)
                w2 = w("w2_0")[:, 0:E2 * HID2].rearrange("p (m k) -> p m k", k=C)
                n = HID2 // P
                N = B * CAP2
                for pk in ("moe2a", "moe2b"):
                    pe.wait_ge(load[pk], 16)
                for i in range(E2 * n + 2):
                    if i < E2 * n:
                        e = i // n
                        pe.wait_ge(sig["xs_set"], B) if i < 2 else pe.wait_ge(sig["h5_set"], i - 1)
                        mm(bank(4 + i % 2)[:, 0:N], w1[:, i, :], XS5[:, e, :], start=True, stop=True)\
                            .then_inc(sig["h5_mm"], 1)
                    if i >= 2:
                        v = i - 2
                        e, k = divmod(v, n)
                        pe.wait_ge(sig["h5_set"], v + 1)
                        if k == 0:
                            pe.wait_ge(sig["d5_set"], NT) if e < 2 else pe.wait_ge(sig["yt_set"], e - 1)
                        m = mm(bank(2 + e % 2)[:, 0:N], w2[:, v, :], H5[:, v % 4, :], start=(k == 0),
                               stop=(k == n - 1)).then_inc(sig["h5_used"], 1)
                pe.wait_ge(sig["yt_set"], E2)
                for i in range(B + 1):
                    if i < B:
                        b = i
                        pe.wait_ge(sig["pt5_set"], NT) if b < 2 else pe.wait_ge(sig["y5_set"], b - 1)
                        for g, (a, z) in enumerate(GRP):
                            m = tr(bank(6 + b % 2)[0:(z - a) * CAP2, g * C:(g + 1) * C],
                                   YT5[:, b, a * CAP2:z * CAP2], ident)
                        m.then_inc(sig["y5T_mm"], 1)
                    if i >= 1:
                        b = i - 1
                        pe.wait_ge(sig["y5_set"], b + 1)
                        out_free(5, b)
                        for j in range(2):
                            for g, (a, z) in enumerate(GRP):
                                r = slice(0, (z - a) * CAP2)
                                m = mm(bank(b % 2)[:, j * C:(j + 1) * C], PT5[r, 2 * b + j, g * P:(g + 1) * P],
                                       Y5[r, b, g * C:(g + 1) * C], start=(g == 0), stop=(g == 2))
                        m.then_inc(sig["out_ready"], 1)

            def setup6():
                pe.wait_ge(load["gqa"], 16)
                pe.wait_ge(sig["oT_set"], 3 * B)
                for k in range(2):
                    m = mm(bank(4)[:, k * 256:(k + 1) * 256], w("wk6")[:, k * P:(k + 1) * P], w("ctxT"),
                           start=True, stop=True)
                m.then_inc(sig["kT6_mm"], 1)
                pe.wait_ge(sig["hT"], 6 * B)
                for g in range(HK3):
                    if g >= 2:
                        pe.wait_ge(sig["vT6_set"], g - 1)
                    mm(bank(6 + g % 2), w("wv6")[:, g * P:(g + 1) * P], w("ctx2"), start=True, stop=True)\
                        .then_inc(sig["vT6_mm"], 1)
                pe.wait_ge(sig["kT6_set"], 1)
                for hh in range(H // 2):
                    if hh >= 2:
                        pe.wait_ge(sig["A6_set"], hh - 1)
                    for i in range(2):
                        q = 2 * hh + i
                        g, r = q // R3, q % R3
                        G, gp = g // 2, g % 2
                        rr = slice(gp * D3, (gp + 1) * D3)
                        a = (G * R3 + r) * C
                        m = mm(bank(4 + hh % 2)[:, i * 256:(i + 1) * 256], w("wq6")[rr, a:a + C], kT6[rr, G, :],
                               start=True, stop=True)
                    m.then_inc(sig["A6_mm"], 1)
                pe.wait_ge(sig["vT6_set"], HK3)
                for n in range(B * HK3):
                    b, g = divmod(n, HK3)
                    if n >= 2:
                        pe.wait_ge(sig["vo_set"], n - 1)
                    mm(bank(6 + n % 2)[:, 0:256], vT6[:, g, b * P:(b + 1) * P],
                       w("wo6")[:, 2 * g * C:(2 * g + 2) * C], start=True, stop=True).then_inc(sig["vo_mm"], 1)

            def attention6():
                for b in range(B):
                    ln_T(6, b)
                pe.wait_ge(sig["hT"], 7 * B)
                pe.wait_ge(sig["yt_set"], E2)
                lag = LAG[6]
                for i in range(UNITS + lag + 1):
                    if i < UNITS:
                        unit_scores(6, i)
                    if lag <= i < UNITS + lag:
                        unit_transpose(6, i - lag)
                    if i >= lag + 1:
                        u = i - lag - 1
                        t, q = divmod(u, 2)
                        b, j = divmod(t, 2)
                        pe.wait_ge(sig["PT_set"], UBASE[6] + u + 1)
                        if j == 0 and q == 0:
                            out_free(6, b)
                        for c in range(4):
                            m = mm(bank(b % 2)[:, j * C:(j + 1) * C], PT[:, u % 4, c * P:(c + 1) * P],
                                   VO6[:, b, 4 * q + c, :], start=(q == 0 and c == 0), stop=(q == 1 and c == 3))
                        m.then_inc(sig["pv_mm"], 1)

            def mlp7():
                pe.wait_ge(sig["ints_cast"], 1)
                for b in range(B):
                    ln_T(7, b)
                for i in range(B * M3 + M3):
                    if i < B * M3:
                        b, m = divmod(i, M3)
                        got_hT(7, b)
                        if i >= 4:
                            pe.wait_ge(sig["h7_set"], i - 3)
                        k = 2 + i % 4
                        mm(bank(k)[:, 0:T], w("wg")[:, m * P:(m + 1) * P], h(b), start=True, stop=True)
                        mm(bank(k)[:, T:2 * T], w("wu")[:, m * P:(m + 1) * P], h(b), start=True, stop=True)\
                            .then_inc(sig["gu_mm"], 1)
                    if i >= M3 and i % M3 == M3 - 1:
                        b = i // M3 - 1
                        pe.wait_ge(sig["h7_set"], M3 * (b + 1))
                        out_free(7, b)
                        for j in range(2):
                            for m in range(M3):
                                q = mm(bank(b % 2)[:, j * C:(j + 1) * C], H7[:, b % 2, m, j * P:(j + 1) * P],
                                       w("wd")[:, m * C:(m + 1) * C], start=(m == 0), stop=(m == M3 - 1))
                        q.then_inc(sig["out_ready"], 1)

            setup_kv0()
            attn0()
            router1()
            experts1()
            attention(2)
            mixture3()
            attention(4)
            experts5()
            attention6()
            mlp7()

        @block.scalar
        def _(act):
            A, copy = nc.scalar.activation, nc.scalar.copy

            def ln_out(s):
                for b in range(B):
                    act.wait_ge(sig["ln_T"], s * B + b + 1)
                    copy(hT[:, b * 256:(b + 1) * 256], PS[:, 6 + b % 2, 0:256]).then_inc(sig["hT"], 1)

            def o_out(s, b, first=4):
                k = ATT.index(s) * B + b
                act.wait_ge(sig["oT_mm"], k + 1)
                copy(oT[:, b * 256:(b + 1) * 256], PS[:, first + b % 2, 0:256]).then_inc(sig["oT_set"], 1)

            def unit_out(s, u):
                v = UBASE[s] + u
                act.wait_ge(sig["PT_mm"], v + 1)
                if u >= 4:
                    act.wait_ge(sig["pv_mm"], v - 3)
                copy(PT[:, u % 4, :], PS[:, ubank(s, u), :]).then_inc(sig["PT_set"], 1)

            def units(s):
                lag = LAG[s]
                for i in range(UNITS + lag):
                    if i >= lag:
                        unit_out(s, i - lag)
                    if i < UNITS:
                        act.wait_ge(sig["sc_sub"], UBASE[s] + i + 1)
                        A(S[:, i % 6, :], S[:, i % 6, :], ACT.Exp, scale=1.0 if s == 4 else SCALE[s])\
                            .then_inc(sig["sc_exp"], 1)

            act.wait_ge(load["first"], 16)
            A(gain[:], w("gain"), ACT.Tanh).then_inc(sig["gain_set"], 1)
            for j in range(2):
                act.wait_ge(sig["k0_sub"], j + 1)
                A(kk[:, j, :], kk[:, j, :], ACT.Exp).then_inc(sig["k0_exp"], 1)
            for i in range(B + 1):
                if i < B:
                    act.wait_ge(sig["ln_T"], i + 1)
                    copy(hT[:, i * 256:(i + 1) * 256], PS[:, 6 + i % 2, 0:256]).then_inc(sig["hT"], 1)
                if i >= 1:
                    b = i - 1
                    act.wait_ge(sig["q0_sub"], b + 1)
                    A(O[:, 2 * b:2 * b + 2, :], O[:, 2 * b:2 * b + 2, :], ACT.Exp).then_inc(sig["q0_exp"], 1)
            act.wait_ge(sig["kT_mm"], 1)
            copy(kT[:], PS[:, 4, :].rearrange("p (k n) -> p k n", k=2)).then_inc(sig["kT_set"], 1)
            for i in range(B + 2):
                if i < B:
                    act.wait_ge(sig["q0T_mm"], i + 1)
                    copy(qT[:, i * 256:(i + 1) * 256], PS[:, 6 + i % 2, 0:256]).then_inc(sig["q0T_set"], 1)
                if i >= 2:
                    o_out(0, i - 2)
            ln_out(1)
            for hf in range(2):
                act.wait_ge(sig["r1_mm"], hf + 1)
                if hf:
                    act.wait_ge(sig["gg_set"], 1)
                A(sc[:], PS[:, 2 + hf, 0:4 * E0].rearrange("p (j e) -> p j e", j=4), ACT.Exp, scale=-1.0)\
                    .then_inc(sig["r1_exp"], 1)
            act.wait_ge(load["mix"], 16)
            A(sgate[:], w("gates"), ACT.Exp, scale=-1.0).then_inc(sig["sg_exp"], 1)
            for i in range(2 * STEPS1):
                hf, m = divmod(i, STEPS1)
                act.wait_ge(sig["mA"], i + 1)
                if i >= 2:
                    act.wait_ge(sig["hg"], i - 1)
                A(H1[:, i % 2, :], PS[:, 6 + i % 2, :], ACT.Gelu_apprx_tanh).then_inc(sig["h1"], 1)
                if i == STEPS1 + 1 or i == 2 * STEPS1 - 1:
                    hf = 0 if i == STEPS1 + 1 else 1
                    act.wait_ge(sig["hg_used"], (hf + 1) * STEPS1)
                    copy(accS[:, hf, :], PS[:, 2 + hf, :]).then_inc(sig["acc_evac"], 1)

            def attention(s):
                k = s // 4
                for i in range(B + 2):
                    if i < B:
                        n = s * B + i
                        act.wait_ge(sig["ln_T"], n + 1)
                        copy(hT[:, i * 256:(i + 1) * 256], PS[:, 6 + i % 2, 0:256]).then_inc(sig["hT"], 1)
                    if i >= 2:
                        b = i - 2
                        act.wait_ge(sig["q_mm"], k * B + b + 1)
                        copy(qT[:, b * 256:(b + 1) * 256], PS[:, 2 + b % 2, 0:256]).then_inc(sig["q_set"], 1)
                units(s)
                for b in range(B):
                    o_out(s, b)

            attention(2)
            ln_out(3)
            act.wait_ge(sig["l3_sub"], 1)
            A(lg[:], lg[:], ACT.Exp).then_inc(sig["l3_exp"], 1)
            for b in range(B):
                act.wait_ge(sig["xe_used"], (b + 1) * E1 // 2)
                copy(qT3[0:D1, b, :], PS[0:D1, 2 + b % 2, 0:T]).then_inc(sig["qkv_set"], 1)
                copy(kT3[0:D1, b, :], PS[D1:2 * D1, 2 + b % 2, 0:T]).then_inc(sig["qkv_set"], 1)
                v = PS[:, 6 + b % 2, 0:2 * D1].rearrange("p (j d) -> p j d", j=2)
                copy(v3d[:, b, :, 0:D1], v).then_inc(sig["qkv_set"], 1)
                copy(v3d[:, b, :, D1:2 * D1], v).then_inc(sig["qkv_set"], 1)
            for i in range(NT + 2):
                if i >= 2:
                    t = i - 2
                    j = t % 2
                    act.wait_ge(sig["PT3_mm"], t + 1)
                    if t >= 2:
                        act.wait_ge(sig["a3_mm"], t - 1)
                    copy(PT3[:, t % 2, 0:(j + 1) * P], PS[:, 6 + t % 2, 0:(j + 1) * P]).then_inc(sig["PT3_set"], 1)
                if i < NT:
                    ks = (i % 2 + 1) * P
                    act.wait_ge(sig["s3_sub"], i + 1)
                    A(S3[:, i % 4, 0:ks], S3[:, i % 4, 0:ks], ACT.Exp, scale=D1 ** -0.5,
                      accum_out=s3[:, i % 4:i % 4 + 1]).then_inc(sig["s3_exp"], 1)
            attention(4)
            ln_out(5)
            act.wait_ge(sig["r5_sub"], 1)
            A(lg[:, :, 0:E2], lg[:, :, 0:E2], ACT.Exp).then_inc(sig["r5_exp"], 1)
            act.wait_ge(sig["kT6_mm"], 1)
            copy(kT6[:], PS[:, 4, :].rearrange("p (k n) -> p k n", k=2)).then_inc(sig["kT6_set"], 1)
            for hh in range(H // 2):
                act.wait_ge(sig["A6_mm"], hh + 1)
                for i in range(2):
                    m = copy(A6[:, :, (2 * hh + i) * KEYS:(2 * hh + i + 1) * KEYS],
                             PS[:, 4 + hh % 2, i * 256:(i + 1) * 256].rearrange("p (b k) -> p b k", b=B))
                m.then_inc(sig["A6_set"], 1)
            for n in range(B * HK3):
                act.wait_ge(sig["vo_mm"], n + 1)
                g = n % HK3
                copy(VO6[:, n // HK3, 2 * g:2 * g + 2, :],
                     PS[:, 6 + n % 2, 0:256].rearrange("p (k c) -> p k c", k=2)).then_inc(sig["vo_set"], 1)
            for b in range(B):
                act.wait_ge(sig["xs_mm"], b + 1)
                copy(XS5[:, :, b * CAP2:(b + 1) * CAP2],
                     PS[:, 4 + b % 2, 0:SL].rearrange("p (e s) -> p e s", e=E2)).then_inc(sig["xs_set"], 1)
            for t in range(NT):
                act.wait_ge(sig["pt5_mm"], t + 1)
                copy(PT5[0:120, t, 0:2 * P], PS[0:120, 6 + t % 2, 0:2 * P])
                copy(PT5[0:80, t, 2 * P:3 * P], PS[0:80, 6 + t % 2, 2 * P:3 * P]).then_inc(sig["pt5_set"], 1)
            n = HID2 // P
            for i in range(E2 * n + 3):
                if i < E2 * n:
                    act.wait_ge(sig["h5_mm"], i + 1)
                    if i >= 4:
                        act.wait_ge(sig["h5_used"], i - 3)
                    A(H5[:, i % 4, :], PS[:, 4 + i % 2, 0:B * CAP2], ACT.Relu, bias=w("b1_2")[:, i:i + 1])\
                        .then_inc(sig["h5_set"], 1)
                if i >= 3 and (i - 3) % n == n - 1:
                    e = (i - 3) // n
                    act.wait_ge(sig["h5_used"], (e + 1) * n)
                    A(YT5[:, :, e * CAP2:(e + 1) * CAP2],
                      PS[:, 2 + e % 2, 0:B * CAP2].rearrange("p (b s) -> p b s", b=B), ACT.Identity,
                      bias=w("b2_2")[:, e:e + 1]).then_inc(sig["yt_set"], 1)
            for b in range(B):
                act.wait_ge(sig["y5T_mm"], b + 1)
                copy(Y5[0:120, b, 0:2 * C], PS[0:120, 6 + b % 2, 0:2 * C])
                copy(Y5[0:80, b, 2 * C:3 * C], PS[0:80, 6 + b % 2, 2 * C:3 * C]).then_inc(sig["y5_set"], 1)
            ln_out(6)
            units(6)
            ln_out(7)
            for i in range(B * M3):
                act.wait_ge(sig["gu_mm"], i + 1)
                if i >= 3:
                    act.wait_ge(sig["h7_set"], i - 2)
                A(sg7[:, i % 3, :], PS[:, 2 + i % 4, 0:T], ACT.Silu).then_inc(sig["silu7"], 1)

        @block.vector
        def _(dve):
            tt, ts, stt = nc.vector.tensor_tensor, nc.vector.tensor_scalar, nc.vector.scalar_tensor_tensor
            cp, red_, rcp = nc.vector.tensor_copy, nc.vector.tensor_reduce, nc.vector.reciprocal
            chain = [0]

            def link(ins):
                chain[0] += 1
                ins.then_inc(sig["dve_step"], 1)
                dve.wait_ge(sig["dve_step"], chain[0])

            def over(a, k):
                return a.unsqueeze(len(a.shape)).broadcast_to(list(a.shape) + [k])

            def ln_stats(s, b):
                for j in range(2):
                    m = nc.vector.bn_stats(st[:, 2 * b + j, :], X[:, 2 * b + j, :])
                link(m)
                for j in range(2):
                    m = nc.vector.bn_aggr(mv[:, 2 * b + j, :], st[:, 2 * b + j, :])
                link(m)
                ts(vareps[:, 2 * b:2 * b + 2], mv[:, 2 * b:2 * b + 2, 1], EPS, None, ALU.add)\
                    .then_inc(sig["ln_var"], 1)

            def ln_norm(s, b):
                n = s * B + b
                dve.wait_ge(sig["ln_rstd"], n + 1)
                if s:
                    dve.wait_ge(sig["ln_T"], n - B + 1)
                for j in range(2):
                    t = 2 * b + j
                    ts(hN[:, t, :], X[:, t, :], mv[:, t, 0:1], rstd[:, t:t + 1], ALU.subtract, ALU.mult)\
                        .then_inc(sig["ln_h"], 1)
                if s == 3:
                    dve.wait_ge(sig["ln_h"], 2 * n + 2)
                    for j in range(2):
                        t = 2 * b + j
                        link(nc.vector.tensor_tensor_reduce(junk, hN[:, t, :], hN[:, t, :], 1.0, 0.0, ALU.mult,
                                                            ALU.add, ss[:, t:t + 1]))

            def residual(s, b, o=None, ready=None):
                if (s, b) == (0, 0):
                    dve.wait_ge(sig["gain_set"], 1)
                if ready is None:
                    dve.wait_ge(sig["out_ready"], OUT[s] + b + 1)
                else:
                    dve.wait_ge(sig[ready[0]], ready[1])
                x = w("x")[:, 2 * b * C:(2 * b + 2) * C]
                k = s // 2 + (0 if s % 2 == 0 else 4)
                stt(x, PS[:, b % 2, 0:2 * C] if o is None else o, gain[:, k:k + 1], x, ALU.mult, ALU.add)\
                    .then_inc(sig["resid"], 1)
                if s < 7:
                    dve.wait_ge(sig["resid"], s * B + b + 1)
                    ln_stats(s + 1, b)

            def residuals(s, ready=None):
                for i in range(B + 1):
                    if i < B:
                        residual(s, i, ready=None if ready is None else ready(i))
                    if i >= 1 and s < 7:
                        ln_norm(s + 1, i - 1)

            def setup_kv0():
                for j in range(2):
                    dve.wait_ge(sig["k0_mm"], j + 1)
                    kps = heads(PS[:, 6 + j, 0:C])
                    link(red_(red[:, j, 0:H], kps, AX.X, ALU.max))
                    cp(vv[:, j, 0:C], PS[:, 6 + j, C:2 * C])
                    tt(heads(kk[:, j, :]), kps, over(red[:, j, 0:H], D), ALU.subtract).then_inc(sig["k0_sub"], 1)
                for j in range(2):
                    dve.wait_ge(sig["k0_exp"], j + 1)
                    kv = heads(kk[:, j, :])
                    link(red_(red[:, j, 0:H], kv, AX.X, ALU.add))
                    link(rcp(red2[:, j, 0:H], red[:, j, 0:H]))
                    tt(kv, kv, over(red2[:, j, 0:H], D), ALU.mult).then_inc(sig["k0_soft"], 1)
                for b in range(B):
                    dve.wait_ge(sig["kv0_mm"], b + 1)
                    tt(heads(kvb[:, b, 0:C]), heads(PS[:, KV0[b], 0:C]), over(hm, D), ALU.mult)
                    ts(kvb[:, b, C:C + H], hm, PS[:, KV0[b], C:C + 1], None, ALU.mult).then_inc(sig["kvb_set"], 1)

            def values18(s):
                k = s // 4
                dve.wait_ge(sig["v_mm"], k + 1)
                for b in range(B):
                    o = v18[s][:, b, :].rearrange("p (k j d) -> p k j d", j=2, d=D + 1)
                    i = PS[:, 5, b * C:(b + 1) * C].rearrange("p (k j d) -> p k j d", j=2, d=D)
                    for j in range(2):
                        ts(o[:, :, j, 0:D], i[:, :, j, :], w("parity")[:, j:j + 1], None, ALU.mult)
                        m = ts(o[:, :, j, D], ones[:, 0:H // 2], w("parity")[:, j:j + 1], None, ALU.mult)
                    m.then_inc(sig["v18_set"], 1)

            def attn0():
                for i in range(B + 1):
                    if i < B:
                        b = i
                        dve.wait_ge(sig["q0_mm"], b + 1)
                        qps = heads(PS[:, 2 + b % 2, 0:256])
                        link(red_(red[:, b % 2, :], qps, AX.X, ALU.max))
                        tt(O[:, 2 * b:2 * b + 2, :].rearrange("p j (h d) -> p (j h) d", d=D), qps,
                           over(red[:, b % 2, :], D), ALU.subtract).then_inc(sig["q0_sub"], 1)
                    if i >= 1:
                        b = i - 1
                        q = O[:, 2 * b:2 * b + 2, :].rearrange("p j (h d) -> p (j h) d", d=D)
                        dve.wait_ge(sig["q0_exp"], b + 1)
                        link(red_(red2[:, b % 2, :], q, AX.X, ALU.add))
                        link(rcp(red2[:, b % 2, :], red2[:, b % 2, :]))
                        tt(q, q, over(red2[:, b % 2, :], D), ALU.mult).then_inc(sig["q0_soft"], 1)
                dve.wait_ge(sig["q0_soft"], B)
                values18(2)
                for b in range(B):
                    dve.wait_ge(sig["kvo_mm"], b + 1)
                    kvo = PS[:, 2 + b % 2, 0:2 * (C + H)].rearrange("p (j n) -> p j n", j=2)
                    r = red2[:, b % 2, :].rearrange("p (j h) -> p j h", j=2)
                    link(rcp(r, kvo[:, :, C:C + H]))
                    for j in range(2):
                        m = tt(heads(accS[:, 0, j * C:(j + 1) * C]), heads(kvo[:, j, 0:C]), over(r[:, j, :], D), ALU.mult)
                    link(m)
                    o = O[:, 2 * b:2 * b + 2, :].rearrange("p j c -> p (j c)")
                    tt(o, o, accS[:, 0, 0:2 * C], ALU.add).then_inc(sig["o_tok"], 1)
                    dve.wait_ge(sig["o_tok"], b + 1)
                residuals(0)

            def router1():
                for hf in range(2):
                    dve.wait_ge(sig["r1_exp"], hf + 1)
                    tiles = slice(4 * hf, 4 * hf + 4)
                    link(ts(sc[:], sc[:], 1.0, None, ALU.add))
                    link(rcp(sc[:], sc[:]))
                    link(tt(topin[:, :, 2:], sc[:], w("ebias0").unsqueeze(1).broadcast_to([P, 4, E0]), ALU.add))
                    for j in range(4):
                        m = nc.vector.max(top8[:, j, :], topin[:, j, :])
                    link(m)
                    for j in range(4):
                        m = nc.vector.match_replace(rep[:, j, :], top8[:, j, :], topin[:, j, :], -BIG)
                    link(m)
                    ts(sel[:, tiles, :], rep[:, :, 2:], -BIG, None, ALU.is_equal).then_inc(sig["sel_set"], 1)
                    dve.wait_ge(sig["sel_set"], hf + 1)
                    r = rs[:, 0:4, :]
                    link(tt(wts[:], sc[:], sel[:, tiles, :], ALU.mult))
                    link(red_(r, wts[:], AX.X, ALU.add))
                    link(ts(r, r, 1e-20, None, ALU.add))
                    link(rcp(r, r))
                    link(tt(wts[:], wts[:], r.broadcast_to([P, 4, E0]), ALU.mult))
                    dve.wait_ge(sig["pos_mm"], hf + 1)
                    if hf:
                        dve.wait_ge(sig["ggT_mm"], hf)
                    g = GG[:].rearrange("p j (k e) -> p j k e", k=2)
                    pos = PS[:, 2 + hf, 256:512].rearrange("p (j e) -> p j e", j=4)
                    link(stt(g[:, :, 0, :], pos, float(CAP0), wts[:], ALU.is_lt, ALU.mult))
                    cp(g[:, :, 1, :], g[:, :, 0, :]).then_inc(sig["gg_set"], 1)
                    if hf == 0:
                        values18(4)
                    dve.wait_ge(sig["ggT_mm"], hf + 1)
                    g = gT[:, hf * HALF:(hf + 1) * HALF]
                    link(cp(g, PS[:, 6 + hf, :]))
                    tt(g[64:128, :], PS[64:128, 6 + hf, :], g[64:128, :].bitcast(F32), ALU.subtract)\
                        .then_inc(sig["gT_set"], 1)
                    dve.wait_ge(sig["gT_set"], hf + 1)

            def setup_mix():
                dve.wait_ge(load["mix"], 16)
                tt(simsq[:], w("sim"), w("sim"), ALU.mult).then_inc(sig["sim_sq"], 1)
                cp(rows32[:], w("half32")[0:64, :])
                cp(pair16[:].rearrange("p (e d) -> p e d", d=D1), over(w("half32")[0:64, :], D1))
                dve.wait_ge(sig["sim_mm"], 1)
                ts(simss[:], PS[:, 4, 0:E1], 1e-24, None, ALU.max).then_inc(sig["sim_ss"], 1)
                dve.wait_ge(sig["sg_exp"], 1)
                link(ts(sgate[:], sgate[:], 1.0, None, ALU.add))
                link(rcp(sgate[:], sgate[:]))
                dve.wait_ge(sig["sim_pw"], 1)
                tt(simn[:], w("sim"), siminv[:], ALU.mult).then_inc(sig["sim_set"], 1)

            def experts1():
                for i in range(2 * STEPS1):
                    m = i % STEPS1
                    dve.wait_ge(sig["h1"], i + 1)
                    if i >= 3:
                        dve.wait_ge(sig["hg_used"], i - 2)
                    if m < GATED1:
                        dve.wait_ge(sig["mG"], i // STEPS1 * GATED1 + m + 1)
                        tt(Hg[:, i % 3, :], H1[:, i % 2, :], PS[:, 4 + i % 2, :], ALU.mult).then_inc(sig["hg"], 1)
                    else:
                        cp(Hg[:, i % 3, :], H1[:, i % 2, :]).then_inc(sig["hg"], 1)
                    if i == STEPS1 + 3 + FIN:
                        half_end(0)
                half_end(1)

            def half_end(hf):
                for j in range(2):
                    b = 2 * hf + j
                    residual(1, b, PS[:, hf, j * 256:(j + 1) * 256], ("out_ready", OUT[1] + 2 * hf + 2))
                for j in range(2):
                    ln_norm(2, 2 * hf + j)

            def normalise(s, t):
                k = s // 4
                dve.wait_ge(sig["pv_mm"], UBASE[s] + 2 * t + 2)
                pv = heads(PS[:, 2 + t % 2, 0:H * (D + 1)], D + 1)
                link(rcp(rden[:, t % 2, :], pv[:, :, D]))
                tt(heads(O[:, t, :]), pv[:, :, 0:D], over(rden[:, t % 2, :], D), ALU.mult).then_inc(sig["pv_out"], 1)

            def unit_front(s, u):
                v = UBASE[s] + u
                t, q = divmod(u, 2)
                dve.wait_ge(sig["sc_mm"], v + 1)
                if u >= 6:
                    dve.wait_ge(sig["PT_mm"], v - 5)
                i, o = heads(PS[:, ubank(s, u), :], KEYS), heads(S[:, u % 6, :], KEYS)
                if s == 4:
                    e = w("mask")[:, t // 2 * KEYS:(t // 2 + 1) * KEYS].unsqueeze(1).broadcast_to([P, H // 2, KEYS])
                    link(stt(o, i, SCALE[4], e, ALU.mult, ALU.add))
                    i = o
                link(red_(smax[:, u % 2, :], i, AX.X, ALU.max))
                tt(o, i, over(smax[:, u % 2, :], KEYS), ALU.subtract).then_inc(sig["sc_sub"], 1)

            def attention(s):
                if s == 4:
                    dve.wait_ge(sig["ints_cast"], 1)
                lag = LAG[s] + 3
                for i in range(UNITS + lag):
                    if i < UNITS:
                        unit_front(s, i)
                    if i >= lag and (i - lag) % 2:
                        normalise(s, (i - lag) // 2)
                residuals(s)

            def logits3():
                link(ts(ss[:], ss[:], 1e-24, None, ALU.max))
                ts(ss[:], ss[:], 1.0, None, ALU.mult).then_inc(sig["ss_set"], 1)
                dve.wait_ge(sig["l3_mm"], 1)
                dve.wait_ge(sig["ss_pw"], 1)
                l = PS[:, 2, 0:NT * E1].rearrange("p (t e) -> p t e", t=NT)
                link(tt(lg[:], l, over(rn[:], E1), ALU.mult))
                link(tt(lg[:], lg[:], sgate[:].unsqueeze(1).broadcast_to([P, NT, E1]), ALU.subtract))
                link(cp(topin2[:, :, 6:], lg[:]))
                for t in range(NT):
                    m = nc.vector.max(top8[:, t, :], topin2[:, t, :])
                ts(on[:], lg[:], 0.0, None, ALU.is_gt)
                link(m)
                for t in range(NT):
                    m = nc.vector.match_replace(rep2[:, t, :], top8[:, t, :], topin2[:, t, :], -BIG)
                link(red_(cnt[:], lg[:], AX.X, ALU.max))
                link(ts(fb[:], rep2[:, :, 6:], -BIG, None, ALU.is_equal))
                link(ts(cnt[:], cnt[:], 0.0, None, ALU.is_le))
                link(tt(fb[:], fb[:], cnt[:].broadcast_to([P, NT, E1]), ALU.mult))
                link(tt(on[:], on[:], fb[:], ALU.max))
                link(ts(lg[:], lg[:], 0.0, None, ALU.max))
                link(red_(cnt[:], lg[:], AX.X, ALU.max))
                tt(lg[:], lg[:], cnt[:].broadcast_to([P, NT, E1]), ALU.subtract).then_inc(sig["l3_sub"], 1)
                dve.wait_ge(sig["l3_exp"], 1)
                link(tt(lg[:], lg[:], on[:], ALU.mult))
                link(red_(cnt[:], lg[:], AX.X, ALU.add))
                link(rcp(cnt[:], cnt[:]))
                for k in range(2):
                    m = tt(G16[:, :, 32 * k:32 * k + E1], lg[:], cnt[:].broadcast_to([P, NT, E1]), ALU.mult)
                m.then_inc(sig["g3_set"], 1)

            def mixture3():
                logits3()
                for k in range(2):
                    dve.wait_ge(sig["g3T_mm"], k + 1)
                    g = gT3[:, k * 512:(k + 1) * 512]
                    link(cp(g, PS[0:64, 4 + k, :]))
                    tt(g[32:64, :], PS[32:64, 4 + k, :], g[32:64, :].bitcast(F32), ALU.subtract)\
                        .then_inc(sig["g3T_set"], 1)
                for i in range(B * E1 // 2):
                    b = i // (E1 // 2)
                    dve.wait_ge(sig["bc_mm"], i + 1)
                    if i >= 4:
                        dve.wait_ge(sig["xe_used"], i - 3)
                    hb = hT[:, b * T:(b + 1) * T].unsqueeze(1).broadcast_to([P, 2, T])
                    tt(heads(xeT[:, i % 4, :], T), heads(PS[:, 4 + i % 2, :], T), hb, ALU.mult)\
                        .then_inc(sig["xe_set"], 1)
                for i in range(NT + 1):
                    if i < NT:
                        j = i % 2
                        ks = (j + 1) * P
                        x = S3[:, i % 4, 0:ks]
                        dve.wait_ge(sig["s3_mm"], i + 1)
                        if i >= 4:
                            dve.wait_ge(sig["PT3_mm"], i - 3)
                        a = P if j == 0 else 0
                        link(tt(x, PS[:, 4 + i % 2, 0:ks], w("causal")[:, a:a + ks], ALU.add))
                        link(red_(m3[:, i % 4:i % 4 + 1], x, AX.X, ALU.max))
                        ts(x, x, m3[:, i % 4:i % 4 + 1], None, ALU.subtract).then_inc(sig["s3_sub"], 1)
                    if i >= 1:
                        t = i - 1
                        ks = (t % 2 + 1) * P
                        dve.wait_ge(sig["s3_exp"], t + 1)
                        link(rcp(m3[:, t % 4:t % 4 + 1], s3[:, t % 4:t % 4 + 1]))
                        ts(S3[:, t % 4, 0:ks], S3[:, t % 4, 0:ks], m3[:, t % 4:t % 4 + 1], None, ALU.mult)\
                            .then_inc(sig["s3_norm"], 1)
                for b in range(B):
                    dve.wait_ge(sig["a3_mm"], 2 * b + 2)
                    cp(aT3[:, b, :], PS[:, 2 + b % 2, 0:T]).then_inc(sig["a3_set"], 1)
                dve.wait_ge(sig["a3_set"], B)
                n = E1 // 4

                for i in range(B * n + n):
                    if i < B * n:
                        b = i // n
                        dve.wait_ge(sig["bp_mm"], i + 1)
                        if i >= 4:
                            dve.wait_ge(sig["mix_used"], i - 3)
                        ab = aT3[:, b, :].unsqueeze(1).broadcast_to([P, 2, T])
                        tt(heads(mixT[:, i % 4, :], T), heads(PS[:, 4 + i % 2, :], T), ab, ALU.mult)\
                            .then_inc(sig["mix_set"], 1)
                    if i >= n and (i + 1) % n == 0:
                        b = i // n - 1
                        residual(3, b, ready=("mix_used", (b + 1) * n))
                        if b:
                            ln_norm(4, b - 1)
                ln_norm(4, B - 1)

            def router5():
                dve.wait_ge(sig["r5_mm"], 1)
                l8 = lg[:, :, 0:E2]
                lps = PS[:, 2, 0:NT * E2].rearrange("p (t e) -> p t e", t=NT)
                link(red_(rs[:], lps, AX.X, ALU.max))
                tt(l8, lps, rs[:].broadcast_to([P, NT, E2]), ALU.subtract).then_inc(sig["r5_sub"], 1)
                dve.wait_ge(sig["r5_exp"], 1)
                link(red_(rs[:], l8, AX.X, ALU.add))
                link(rcp(rs[:], rs[:]))
                link(tt(l8, l8, rs[:].broadcast_to([P, NT, E2]), ALU.mult))
                link(cp(topin2[:, :, 6:6 + E2], l8))
                for t in range(NT):
                    m = nc.vector.max(top8[:, t, :], topin2[:, t, 0:6 + E2])
                link(m)
                for t in range(NT):
                    m = nc.vector.match_replace(rep2[:, t, 0:6 + E2], top8[:, t, :], topin2[:, t, 0:6 + E2], -BIG)
                link(m)
                ts(sel[:, :, 0:E2], rep2[:, :, 6:6 + E2], -BIG, None, ALU.is_equal).then_inc(sig["sel5"], 1)
                for g in range(HK3):
                    dve.wait_ge(sig["vT6_mm"], g + 1)
                    o = vT6[:, g, :].rearrange("p (b j k) -> p b j k", j=2, k=KEYS)
                    i = PS[:, 6 + g % 2, :].rearrange("p (b j k) -> p b j k", j=2, k=KEYS)
                    for j in range(2):
                        m = ts(o[:, :, j, :], i[:, :, j, :], w("parity")[:, j:j + 1], None, ALU.mult)
                    m.then_inc(sig["vT6_set"], 1)
                dve.wait_ge(sig["pos5"], 1)
                dve.wait_ge(sig["sel5"], 1)
                pos = PS[:, 2, 256:256 + NT * E2].rearrange("p (t e) -> p t e", t=NT)
                link(stt(fb[:, :, 0:E2], sel[:, :, 0:E2], -1000.0, pos, ALU.mult, ALU.add))
                for t in range(NT):
                    tt(heads(D5[:, t, :], CAP2), over(fb[:, t, 0:E2], CAP2),
                       w("slots2").unsqueeze(1).broadcast_to([P, E2, CAP2]), ALU.is_equal).then_inc(sig["d5_set"], 1)
                for t in range(NT):
                    if t == 0:
                        dve.wait_ge(sig["d5_set"], NT)
                    tt(heads(Dw5[:, t, :], CAP2), heads(D5[:, t, :], CAP2), over(lg[:, t, 0:E2], CAP2), ALU.mult)\
                        .then_inc(sig["dw5_set"], 1)

            def attention6():
                lag = 2
                for i in range(UNITS + LAG[6] + 3):
                    if i < UNITS:
                        unit_front(6, i)
                    if lag <= i < UNITS + lag:
                        u = i - lag
                        dve.wait_ge(sig["sc_exp"], UBASE[6] + u + 1)
                        if u >= 2:
                            dve.wait_ge(sig["sc_norm"], u - 1)
                        link(red_(rden[:, u % 2, 0:H // 2], heads(S[:, u % 6, :], KEYS), AX.X, ALU.add))
                        rcp(ssum[:, u % 2, :], rden[:, u % 2, 0:H // 2]).then_inc(sig["sc_sum"], 1)
                    b = i - LAG[6] - 5
                    if b >= 0 and b % 4 == 0:
                        residual(6, b // 4, ready=("pv_mm", UBASE[6] + b + 4))
                        if b:
                            ln_norm(7, b // 4 - 1)
                ln_norm(7, B - 1)

            def mlp7():
                for i in range(B * M3 + M3):
                    if i < B * M3:
                        b, m = divmod(i, M3)
                        dve.wait_ge(sig["silu7"], i + 1)
                        if m == 0 and b >= 2:
                            dve.wait_ge(sig["out_ready"], OUT[7] + b - 1)
                        tt(H7[:, b % 2, m, :], sg7[:, i % 3, :], PS[:, 2 + i % 4, T:2 * T], ALU.mult)\
                            .then_inc(sig["h7_set"], 1)
                    if i >= M3 and i % M3 == M3 - 1:
                        b = i // M3 - 1
                        residual(7, b, ready=("out_ready", OUT[7] + b + 1))

            nc.vector.memset(ones[:], 1.0)
            nc.vector.memset(vv[:, :, C:C + 1], 1.0)
            nc.vector.memset(topin[:, :, 0:2], BIG)
            nc.vector.memset(topin2[:, :, 0:6], BIG)
            nc.vector.memset(G16[:], 0.0).then_inc(sig["consts"], 1)
            dve.wait_ge(sig["consts"], 1)
            dve.wait_ge(load["first"], 16)
            ln_stats(0, 0)
            ln_stats(0, 1)
            ln_norm(0, 0)
            setup_kv0()
            for b in range(1, B):
                if b + 1 < B:
                    ln_stats(0, b + 1)
                ln_norm(0, b)
            attn0()
            router1()
            setup_mix()
            experts1()
            attention(2)
            mixture3()
            attention(4)
            router5()
            residuals(5)
            attention6()
            mlp7()


def layout(i):
    f = {k: np.asarray(v) for k, v in i.items()}

    def rows(a, n=P):
        return np.broadcast_to(a.reshape(1, -1), (n, a.size))

    def tiles(a):
        return a.reshape(-1, P, a.shape[-1]).transpose(1, 0, 2).reshape(P, -1)

    def first_rows(parts):
        a = np.zeros((P, len(parts) * C), np.float32)
        for k, v in enumerate(parts):
            a[0, k * C:k * C + v.size] = v
        return a

    p = np.arange(P)
    ctx = f["ctx_1024"].reshape(B * KEYS, C).T
    ctx2 = np.repeat(ctx.reshape(C, B, 1, KEYS), 2, axis=2).reshape(C, -1)
    half32 = ((p[:, None] % 32 == np.arange(E1)) & (p[:, None] < 64)).astype(np.float32)
    cols = np.arange(T)
    wq6 = f["L3_xattn_Wq"].reshape(2, 2, R3, D3, C).transpose(1, 3, 0, 2, 4).reshape(P, -1)
    qk3 = np.concatenate([f["L1_ffn_q_proj"], f["L1_ffn_k_proj"]], axis=2)
    a = {
        "x": tiles(f["x"].reshape(B * T, C)), "ctxT": ctx, "ctx2": ctx2,
        "wq0": f["L0_xattn_Wq"].T, "wkv0": np.concatenate([f["L0_xattn_Wk"].T, f["L0_xattn_Wv"].T], axis=1),
        "wp0": f["L0_xattn_Wp"].T,
        "rows0": first_rows([f["L0_xattn_bq"], f["L0_xattn_bk"], f["L0_xattn_bv"], f["L0_xattn_bp"], f["L2_ffn_br"]]),
        "ident": np.eye(P, dtype=np.float32), "headmask": (p[:, None] // D == np.arange(H)).astype(np.float32),
        "gain": np.concatenate([rows(f["g_xattn"]), rows(f["g_ffn"])], axis=1),
        "router0": f["L0_ffn_router_weight"].T, "ebias0": rows(f["L0_ffn_expert_bias"]),
        "earlier": (p[:, None] < p).astype(np.float32), "half64": (p[:, None] % E0 == np.arange(E0)).astype(np.float32),
        "wq2": f["L1_xattn_w_q"].T, "wk2": f["L1_xattn_w_k"].T, "wv2": f["L1_xattn_w_v"].T, "wo2": f["L1_xattn_w_o"].T,
        "wq4": f["L2_xattn_Wq"], "wk4": f["L2_xattn_Wk"], "wv4": f["L2_xattn_Wv"], "wo4": f["L2_xattn_Wo"],
        "parity": (p[:, None] // KEYS == np.arange(2)).astype(np.float32),
        "w1_0": np.concatenate([f["L0_ffn_w1"].transpose(1, 0, 2).reshape(C, -1), f["L0_ffn_sw1"].T], axis=1),
        "w2_0": np.concatenate([tiles(f["L0_ffn_w2"].reshape(-1, C)), tiles(f["L0_ffn_sw2"].T)], axis=1),
        "half32": half32, "sim": f["L1_ffn_sim_matrix"], "gates": rows(f["L1_ffn_gates"]),
        "qk3": qk3.transpose(1, 0, 2).reshape(C, -1), "v3": f["L1_ffn_v_proj"].transpose(1, 0, 2).reshape(C, -1),
        "o3": tiles(f["L1_ffn_o_proj"].reshape(-1, C)),
        "causal": np.where(cols[None, :] <= P + p[:, None], 0.0, -BIG).astype(np.float32),
        "router2": f["L2_ffn_Wr"], "b1_2": f["L2_ffn_b1"].reshape(-1, P).T, "b2_2": f["L2_ffn_b2"].T,
        "slots2": rows(np.arange(CAP2, dtype=np.float32) - 1000),
        "moe2a": f["L2_ffn_W1"].transpose(1, 0, 2).reshape(C, -1), "moe2b": tiles(f["L2_ffn_W2"].reshape(-1, C)),
        "wq6": wq6, "wk6": f["L3_xattn_Wk"].T,
        "wv6": np.repeat(f["L3_xattn_Wv"].T.reshape(C, HK3, 1, D3), 2, axis=2).reshape(C, -1),
        "wo6": tiles(f["L3_xattn_Wo"].T),
        "mask": rows(f["mask_BxS2_ik0"]), "wg": f["L3_ffn_w_gate"].T, "wu": f["L3_ffn_w_up"].T,
        "wd": tiles(f["L3_ffn_w_down"].T),
    }
    packs = {"p_" + k: np.ascontiguousarray(np.concatenate([a[n] for n, _ in v], axis=1)) for k, v in PACKS.items()}
    for k in LATER:
        packs["p_" + k] = np.ascontiguousarray(a[k])
    packs["p_gqa"] = np.ascontiguousarray(np.concatenate([a[n] for n, _ in GQA], axis=1))
    packs["p_ints"] = np.ascontiguousarray(np.concatenate([a[n] for n, _ in IPACK], axis=1))
    return packs


def kernel(**inputs):
    import concourse.bacc as bacc
    from concourse.bass_utils import run_bass_kernel_spmd

    nc = bacc.Bacc("TRN2", target_bir_lowering=False, num_devices=1)
    arrays = layout(inputs)
    aps = {k: nc.dram_tensor(k, a.shape, mybir.dt.from_np(a.dtype), kind="ExternalInput").ap()
           for k, a in arrays.items()}
    out = nc.dram_tensor("out", (P, NT * C), F32, kind="ExternalOutput").ap()
    flamingo_blocks(nc, {k[2:]: v for k, v in aps.items()}, aps["p_ints"], out)
    r = run_bass_kernel_spmd(nc, [arrays], core_ids=[0])
    y = r.results[0]["out"]
    return y.reshape(P, NT, C).transpose(1, 0, 2).reshape(B, T, C)
```

```python
from contextlib import ExitStack

import numpy as np
import concourse.bass as bass
from concourse import mybir

F32 = mybir.dt.float32
F32R = mybir.dt.float32r
I32 = mybir.dt.int32
ALU = mybir.AluOpType
ACT = mybir.ActivationFunctionType
AX = mybir.AxisListType

P = 128
B, T, C = 4, 256, 128
NT = B * T // P
KEYS = 64
H, D = 16, 8
EPS = 1e-5
BIG = 1e30

E0, K0, HID0, CAP0 = 64, 6, 64, 48
SH0 = 256
E1, D1 = 16, 64
E2, K2, HID2 = 8, 2, 512
CAP2 = int(T / E2 * 1.25)
HK3, D3, R3 = 4, 64, 4
M3 = 3
FMIN = float(np.finfo(np.float32).min)

PACKS = {
    "first": [("x", NT * C), ("ctxT", B * KEYS), ("wq0", C), ("wkv0", 2 * C), ("rows0", 5 * C), ("ident", P),
              ("headmask", H), ("gain", 8)],
    "attn": [("wp0", C), ("router0", E0), ("ebias0", E0), ("earlier", P), ("half64", E0), ("ctx2", B * 2 * KEYS),
             ("wq2", C), ("wk2", C), ("wv2", C), ("wo2", C), ("wq4", C), ("wk4", C), ("wv4", C), ("wo4", C),
             ("parity", 2)],
    "moe0a": [("w1_0", (E0 * HID0 + SH0))],
    "moe0b": [("w2_0", (E0 * HID0 + SH0) // P * C)],
    "mix": [("half32", E1), ("sim", E1), ("gates", E1), ("causal", T)],
    "moe2": [("router2", E2), ("b1_2", E2 * HID2 // P), ("b2_2", E2), ("slots2", CAP2)],
}
MIXW = [("qkv3", (E1 * 3 + 1) * D1), ("o3", E1 * D1 // P * C)]
GQA = [("wq6", HK3 // 2 * R3 * C), ("wk6", HK3 * D3), ("wv6", HK3 * 2 * D3), ("wo6", H * D3 // P * C)]
LATER = {"moe2a": ("w1_0", E2 * HID2), "moe2b": ("w2_0", E2 * HID2 // P * C)}
IPACK = [("mask", B * KEYS), ("wg", M3 * P), ("wu", M3 * P), ("wd", M3 * C)]


def spans(fields):
    at, out = 0, {}
    for name, n in fields:
        out[name] = (at, at + n)
        at += n
    return out, at


def flamingo_blocks(nc, packed, ints, out):
    ctx = ExitStack()
    with ctx:
        def sb(name, shape, dt=F32):
            return ctx.enter_context(nc.sbuf_tensor(name, shape, dt))

        def twice(name, shape):
            with nc.sbuf_tensor("rounded_" + name, shape, F32R) as rounded:
                pass
            return sb(name, shape), rounded

        where, ctx_in, low = {}, {}, {}
        for pk, fields in PACKS.items():
            sp, n = spans(fields)
            if pk in ("moe0a", "moe0b"):
                t, low[pk] = twice("in_" + pk, [P, n])
            else:
                t = sb("in_" + pk, [P, n])
            ctx_in[pk] = t[:]
            for name, (a, z) in sp.items():
                where[name] = ctx_in[pk][:, a:z]
        w2place, w2hi = twice("w2_high", [P, E0 * HID0 + SH0])
        for fields in (MIXW, GQA):
            for name, (a, z) in spans(fields)[0].items():
                where[name] = w2place[:, a:z]
        sp, n = spans(IPACK)
        ipk = sb("in_ints", [P, n], I32)
        fpk = ipk[:].bitcast(F32)
        for name, (a, z) in sp.items():
            where[name] = fpk[:, a:z]

        def w(name):
            return where[name]

        X = w("x").rearrange("p (t c) -> p t c", c=C)
        ident = w("ident")
        row0 = w("rows0").rearrange("p (k c) -> p k c", c=C)
        hm = w("headmask")
        ones = sb("ones", [P, P])
        half_neg = sb("half_neg", [P, E1])

        st = sb("ln_stats", [P, NT, 6])
        mv = sb("ln_mean_var", [P, NT, 2])
        vareps = sb("ln_var_eps", [P, NT])
        rstd = sb("ln_rstd", [P, NT])
        hN = sb("ln_h", [P, NT, C])
        hT = sb("hT", [P, B * T])

        att, att_r = twice("attention", [P, 3 * B * T])
        qT, oT = att[:, 0:B * T], att[:, 2 * B * T:]
        O = att[:, B * T:2 * B * T].rearrange("p (t c) -> p t c", c=C)
        gain = sb("tanh_gain", [P, 8])

        kk = sb("k_soft", [P, 2, C])
        vv = sb("v_ones", [P, 2, C + 1])
        kvb = sb("kv_blocks", [P, B, C + H])
        red = sb("red", [P, 2, 2 * H])
        red2 = sb("red2", [P, 2, 2 * H])

        kT = sb("kT", [P, 2, B * KEYS])
        w1place, w1hi = twice("w1_high", [P, E0 * HID0 + SH0])
        kblk4 = w1place[:, 0:B * H * KEYS].rearrange("p (b n) -> p b n", b=B)
        kblk = {2: sb("kblk2", [P, B, H * KEYS]), 4: kblk4}
        v18 = {2: sb("v18_2", [P, B, H * (D + 1)]), 4: sb("v18_4", [P, B, H * (D + 1)])}
        A6 = kblk[2]
        VO6 = kblk4.rearrange("p b (k c) -> p b k c", c=C)
        kT6 = kT
        S, S_r = twice("scores", [P, 6, 512])
        PT, PT_r = twice("probsT", [P, 4, 512])
        smax = sb("smax", [P, 2, H // 2])
        ssum = sb("ssum", [P, 2, H // 2])
        rden = sb("rden", [P, 2, H])

        sc = sb("scores_r", [P, NT, E0])
        topin = sb("topin", [P, 4, 2 + E0])
        rep = sb("replaced", [P, 4, 2 + E0])
        top8 = sb("top8", [P, NT, 8])
        sel = sb("chosen", [P, NT, E0])
        wts = sb("weights", [P, 4, E0])
        rs = sb("rsum", [P, NT, 1])
        GG = sb("gates_tok", [P, 4, 2 * E0])
        gT = sb("gateT", [P, B * T], F32R)
        gT3 = gT[0:64, :]

        rows32 = sb("rows32", [64, E1], F32R)
        pair16 = sb("pair16", [64, E1 * D1], F32R)
        simn = sb("sim_n", [P, E1])
        simss = sb("sim_sumsq", [P, E1])
        siminv = sb("sim_inv", [P, E1])
        simsq = sb("sim_sq", [P, E1])
        sgate = sb("sgate", [P, E1])
        ss = sb("sumsq", [P, NT])
        rn = sb("rnorm", [P, NT])
        lg = sb("logits16", [P, NT, E1])
        on = sb("active16", [P, NT, E1])
        fb = sb("fallback16", [P, NT, E1])
        topin2 = sb("topin16", [P, NT, 6 + E1])
        rep2 = sb("replaced16", [P, NT, 6 + E1])
        cnt = sb("count16", [P, NT, 1])
        G16 = sb("gates16", [P, NT, 64])

        REGION = 5800
        with nc.sbuf_tensor("spread64", [P, E0 * HID0], F32R) as early:
            spread64 = early
        region = sb("region", [P, REGION])

        def carve(at, *shape):
            n = int(np.prod(shape))
            a = region[:, at:at + n]
            if len(shape) > 1:
                names = "abc"[:len(shape)]
                a = a.rearrange("p (" + " ".join(names) + ") -> p " + " ".join(names), **dict(zip(names, shape)))
            return a, at + n

        H1, at = carve(E0 * HID0, 2, 512)
        Hg = S[:, 2:4, :]
        Hhi = [PT_r[:, k, :] for k in range(3)]
        Hlo = [PT_r[:, 3, :], S_r[:, 4, :], S_r[:, 5, :]]
        hThi, hTlo = att_r[:, 0:B * T], att_r[:, B * T:2 * B * T]
        accS = S[:, 0:2, :]

        XE = Hg
        qkv3hi, qkv3lo = w1hi[:, 0:E1 * 3 * D1 + D1], w2hi[:, 0:E1 * 3 * D1 + D1]
        vT3 = qT
        mixT = PT
        qT3, at = carve(0, B, T)
        kT3, at = carve(at, B, T)
        v3d, at = carve(at, B, 2, 2 * D1)
        S3, at = carve(at, 4, T)
        PT3, at = carve(at, 2, T)
        aT3, at = carve(at, B, T)
        m3, at = carve(at, 4)
        s3, at = carve(at, 4)
        junk, at = carve(at, C)

        SL = E2 * CAP2
        D5, at = carve(0, NT, SL)
        PT5 = att[:].rearrange("p (t n) -> p t n", t=NT)
        Y5 = D5[:].rearrange("p t n -> p (t n)")[:, 0:B * 3 * C].rearrange("p (b n) -> p b n", b=B)
        XS5, at = carve(at, E2, B * CAP2)
        YT5, at = carve(at, B, SL)
        H5, at = carve(at, 4, B * CAP2)
        Dw5 = S[:].rearrange("p k n -> p (k n)")[:, 0:NT * SL].rearrange("p (t n) -> p t n", t=NT)
        vT6 = PT[:]
        sg7, at = carve(0, 3, T)
        H7, at = carve(at, 2, M3, T)

        PS = ctx.enter_context(nc.psum_tensor("banks", [P, 8, 512], F32))

        def sem(name):
            return ctx.enter_context(nc.semaphore(name))

        load = {pk: sem("load_" + pk) for pk in list(PACKS) + list(LATER) + ["mixw", "gqa"]}
        load_ints = sem("load_ints")
        stored = sem("stored")
        names = """consts half_set gain_set spread_set rows_set ints_cast dve_step pool_step
            ln_var ln_rstd ln_h ln_T hT hT_hi hT_lo w_hi w_lo h_hi h_lo out_ready resid
            k0_mm k0_sub k0_exp k0_soft kv0_mm kvb_set q0_mm q0_sub q0_exp q0_soft q0T_mm q0T_set kvo_mm
            kT_mm kT_set kblk_set v_mm v18_set sim_sq sim_mm sim_ss sim_pw sim_set sg_exp
            o_tok pv_out oT_mm oT_set q_mm q_set sc_mm sc_sub sc_exp sc_sum sc_norm PT_mm PT_set pv_mm
            r1_mm r1_exp sel_set pos_mm gg_set ggT_mm gT_set mA mG h1 hg hg_used acc_evac
            ss_set ss_pw l3_mm l3_sub l3_exp g3_set g3T_mm g3T_set bc_mm xe_set xe_hi xe_lo xe_used w3_hi w3_lo qk_set vT_set v3_mm v3_set
            s3_mm s3_sub s3_exp s3_norm PT3_mm PT3_set a3_mm a3_set bp_mm mix_set mix_used
            r5_mm r5_sub r5_exp sel5 pos5 d5_set dw5_set xs_mm xs_set pt5_mm pt5_set h5_mm h5_set h5_used
            y5_mm yt_set y5T_mm y5_set kT6_mm kT6_set vT6_mm vT6_set A6_mm A6_set vo_mm vo_set
            gu_mm silu7 h7_set""".split()
        sig = {n: sem(n) for n in names}

        block = ctx.enter_context(nc.Block())

        HALF = 512
        STEPS1 = (E0 * HID0 + SH0) // P
        GATED1 = E0 * HID0 // P
        ATT = [0, 2, 4]
        KV0 = [3, 4, 5, 7]
        CUT1 = [0, 9, 18, 27, STEPS1]
        UNITS = 2 * NT
        MAIN, SIDE = slice(0, 2 * P), slice(2 * P, 4 * P)
        TURN_O, TURN_P, TURN_R, TURN_N, TURN_T = 10, 12, 12, 13, 15
        STEPS24 = UNITS - 4 + TURN_T + 1
        GT1 = [6, 1]
        UNITS3 = 2 * E1
        SETUP6, AT6 = 19, [20, 21, 23, 24, 25]
        EARLY7 = [17, 19, 20]
        LBANK = 7
        GATES5 = 8
        SIM1 = 20
        LAG1 = 3
        FIN = 4
        UBASE = {2: 0, 4: UNITS, 6: 2 * UNITS}
        UBANK = {2: [4, 5, 6, 7], 4: [4, 5, 6, 7], 6: [2, 3, 4, 5, 6, 7]}
        LAG = {2: 2, 4: 2, 6: 4}
        SCALE = {2: D ** -0.5, 4: D ** -0.5, 6: D3 ** -0.5}
        OUT = {0: 0, 1: B, 2: 2 * B, 4: 3 * B, 5: 4 * B, 7: 5 * B}
        GRP = [(0, 3), (3, 6), (6, 8)]

        def heads(ap, d=D):
            return ap.rearrange("p (h d) -> p h d", d=d)

        def bank(k):
            return PS[:, k, :]

        def due(i, turn):
            b, rest = divmod(i - turn, 4)
            return b if rest == 0 and 0 <= b < B else None

        def turn_bank(s, b):
            return {0: 6, 0.5: 4, 1: 6}.get(s, 0) + b % 2

        def bank7(n):
            return 6 + n % 2 if n < 2 * M3 else 2 + (n - 2 * M3) % 4

        def obank(s, b):
            return {1: b // 2, 3: b, 5: b}.get(s, b % 2)

        def ubank(s, u):
            return UBANK[s][u % len(UBANK[s])]

        @block.sync
        def _(sp):
            for pk in ["first", "attn", "moe0a", "moe0b", "mix", "moe2"]:
                sp.dma_start(ctx_in[pk], packed[pk]).then_inc(load[pk], 16)
            sp.dma_start(ipk[:], ints).then_inc(load_ints, 16)
            sp.wait_ge(sig["hg_used"], 2 * STEPS1)
            n = spans(MIXW)[1]
            sp.dma_start(w2place[:, 0:n], packed["mixw"]).then_inc(load["mixw"], 16)
            for pk, (name, n) in LATER.items():
                sp.dma_start(w(name)[:, 0:n], packed[pk]).then_inc(load[pk], 16)
            sp.wait_ge(sig["mix_used"], B * E1 // 4)
            n = spans(GQA)[1]
            sp.dma_start(w2place[:, 0:n], packed["gqa"]).then_inc(load["gqa"], 16)
            for b in range(B):
                sp.wait_ge(sig["resid"], 7 * B + b + 1)
                sp.dma_start(out[:, 2 * b * C:(2 * b + 2) * C],
                             w("x")[:, 2 * b * C:(2 * b + 2) * C]).then_inc(stored, 16)
            sp.wait_ge(stored, 16 * B)

        @block.gpsimd
        def _(pool):
            tt = nc.gpsimd.tensor_tensor
            nc.gpsimd.memset(half_neg[:], -0.5).then_inc(sig["half_set"], 1)
            pool.wait_ge(sig["half_set"], 1)

            def rsqrt(s, batches=range(B)):
                for b in batches:
                    n = s * B + b
                    pool.wait_ge(sig["ln_var"], n + 1)
                    t = slice(2 * b, 2 * b + 2)
                    tt(rstd[:, t], vareps[:, t], half_neg[:, 0:2], ALU.pow).then_inc(sig["ln_rstd"], 1)

            def key_blocks(s):
                k = s // 4
                pool.wait_ge(sig["kT_set"], 1)
                for b in range(B):
                    a = kT[:, k, b * KEYS:(b + 1) * KEYS].unsqueeze(1).broadcast_to([P, H, KEYS])
                    tt(heads(kblk[s][:, b, :], KEYS), a, hm.unsqueeze(2).broadcast_to([P, H, KEYS]), ALU.mult)\
                        .then_inc(sig["kblk_set"], 1)

            def cast_ints():
                pool.wait_ge(load_ints, 16)
                nc.gpsimd.tensor_copy(fpk, ipk[:]).then_inc(sig["pool_step"], 1)
                pool.wait_ge(sig["pool_step"], 1)
                a = B * KEYS
                nc.gpsimd.tensor_scalar(fpk[:, a:], fpk[:, a:], 1.0 / 127.0, None, ALU.mult)
                nc.gpsimd.tensor_scalar(fpk[:, 0:a], fpk[:, 0:a], -1.0, 1.0, ALU.mult, ALU.add)\
                    .then_inc(sig["pool_step"], 1)
                pool.wait_ge(sig["pool_step"], 2)
                nc.gpsimd.tensor_scalar(fpk[:, 0:a], fpk[:, 0:a], FMIN, None, ALU.mult).then_inc(sig["ints_cast"], 1)

            def low_weights(k):
                a = slice(CUT1[k] * P, CUT1[k + 1] * P)
                for j, (pk, hi) in enumerate((("moe0a", w1hi), ("moe0b", w2hi))):
                    pool.wait_ge(sig["w_hi"], 2 * k + j + 1)
                    tt(low[pk][:, a], ctx_in[pk][:, a], hi[:, a].bitcast(F32), ALU.subtract).then_inc(sig["w_lo"], 1)

            rsqrt(0)
            key_blocks(2)
            low_weights(0)
            rsqrt(1)
            for b in range(B):
                pool.wait_ge(sig["hT"], B + b + 1)
                a = slice(b * T, (b + 1) * T)
                tt(hTlo[:, a], hT[:, a], hThi[:, a].bitcast(F32), ALU.subtract).then_inc(sig["hT_lo"], 1)
            for k in (1, 2, 3):
                low_weights(k)
            for i in range(2 * STEPS1):
                pool.wait_ge(sig["h_hi"], i + 1)
                if i >= 3:
                    pool.wait_ge(sig["hg_used"], i - 2)
                tt(Hlo[i % 3], Hg[:, i % 2, :], Hhi[i % 3].bitcast(F32), ALU.subtract).then_inc(sig["h_lo"], 1)
                if i in (STEPS1 + 5 + FIN, STEPS1 + 6 + FIN):
                    rsqrt(2, [i - STEPS1 - 5 - FIN])
            rsqrt(2, [2, 3])
            pool.wait_ge(sig["sim_ss"], 1)
            tt(siminv[:], simss[:], half_neg[:], ALU.pow).then_inc(sig["sim_pw"], 1)
            pool.wait_ge(sig["w3_hi"], 1)
            tt(qkv3lo, w("qkv3"), qkv3hi.bitcast(F32), ALU.subtract).then_inc(sig["w3_lo"], 1)
            rsqrt(3)
            pool.wait_ge(sig["ss_set"], 1)
            tt(rn[:], ss[:], half_neg[:, 0:NT], ALU.pow).then_inc(sig["ss_pw"], 1)
            for i in range(UNITS3):
                pool.wait_ge(sig["xe_hi"], i + 1)
                if i >= 3:
                    pool.wait_ge(sig["xe_used"], i - 2)
                tt(Hlo[i % 3], XE[:, i % 2, :], Hhi[i % 3].bitcast(F32), ALU.subtract).then_inc(sig["xe_lo"], 1)
            pool.wait_ge(sig["xe_used"], UNITS3)
            key_blocks(4)
            cast_ints()
            rsqrt(4)
            rsqrt(5)
            rsqrt(6)
            for u in range(UNITS):
                if u % 4 == 0 and u >= 8:
                    rsqrt(7, [u // 4 - 2])
                pool.wait_ge(sig["sc_sum"], u + 1)
                tt(heads(S[:, u % 6, :], KEYS), heads(S[:, u % 6, :], KEYS),
                   ssum[:, u % 2, :].unsqueeze(2).broadcast_to([P, H // 2, KEYS]), ALU.mult)\
                    .then_inc(sig["sc_norm"], 1)
            rsqrt(7, [B - 2, B - 1])

        @block.tensor
        def _(pe):
            mm, tr = nc.tensor.matmul, nc.tensor.transpose

            def h(b, j=None):
                a = 2 * b * P
                return hT[:, a:a + 2 * P] if j is None else hT[:, a + j * P:a + (j + 1) * P]

            def side_free(s, b):
                n, q = (s * B + b + 2, s) if b < 2 else ((s + 1) * B + b - 2, s + 1)
                pe.wait_ge(sig["hT"], n + 1)
                if q in (2, 4):
                    pe.wait_ge(sig["q_set"], q // 4 * B + (b + 2) % 4 + 1)

            def ln_T(s, b):
                n = s * B + b
                pe.wait_ge(sig["ln_h"], 2 * n + 2)
                if b >= 2:
                    pe.wait_ge(sig["hT"], n - 1)
                    if s in (2, 4):
                        pe.wait_ge(sig["q_set"], s // 4 * B + b - 1)
                elif s == 1:
                    pe.wait_ge(sig["q0T_set"], B)
                for j in range(2):
                    m = tr(bank(turn_bank(s, b))[:, SIDE][:, j * P:(j + 1) * P], hN[:, 2 * b + j, :], ident)
                m.then_inc(sig["ln_T"], 1)

            def logits(s, b):
                got_hT(s, b)
                if b == 0:
                    pe.wait_ge(sig["PT_set"], UBASE[s - 1] + UNITS)
                    pe.wait_ge(sig["sim_set"], 1) if s == 3 else pe.wait_ge(load["moe2"], 16)
                for j in range(2):
                    t = 2 * b + j
                    if s == 3:
                        m = mm(bank(LBANK)[:, t * E1:(t + 1) * E1], h(b, j), simn[:], start=True, stop=True)
                    else:
                        o = bank(LBANK)[:, t * E2:(t + 1) * E2]
                        mm(o, ones[0:1, :], row0[0:1, 4, 0:E2], start=True, stop=False)
                        m = mm(o, h(b, j), w("router2"), start=False, stop=True)
                return m

            def queries(s, b):
                got_hT(s, b)
                mm(bank(b % 2)[:, MAIN], w(f"wq{s}"), h(b), start=True, stop=True).then_inc(sig["q_mm"], 1)

            def got_hT(s, b):
                pe.wait_ge(sig["hT"], s * B + b + 1)

            def setup_kv0():
                pe.wait_ge(load["first"], 16)
                pe.wait_ge(sig["consts"], 1)
                for j in range(2):
                    o = bank(6 + j)[:, 0:2 * C]
                    mm(o, ones[0:1, :], row0[0:1, 1:3, :], start=True, stop=False)
                    mm(o, w("ctxT")[:, j * P:(j + 1) * P], w("wkv0"), start=False, stop=True).then_inc(sig["k0_mm"], 1)
                for b in range(B):
                    pe.wait_ge(sig["k0_soft"], b // 2 + 1)
                    r = slice((b % 2) * KEYS, (b % 2 + 1) * KEYS)
                    mm(bank(KV0[b])[:, 0:C + 1], kk[r, b // 2, :], vv[r, b // 2, :], start=True, stop=True)\
                        .then_inc(sig["kv0_mm"], 1)

            def attn0():
                for b in range(B):
                    ln_T(0, b)
                    got_hT(0, b)
                    if b == 0:
                        pe.wait_ge(sig["kvb_set"], B)
                    if b >= 2:
                        pe.wait_ge(sig["q0_sub"], b - 1)
                    for j in range(2):
                        o = bank(2 + b % 2)[:, j * C:(j + 1) * C]
                        mm(o, ones[0:1, :], row0[0:1, 0, :], start=True, stop=False)
                        m = mm(o, h(b, j), w("wq0"), start=False, stop=True)
                    m.then_inc(sig["q0_mm"], 1)
                pe.wait_ge(load["attn"], 16)
                for k, s in enumerate((2, 4)):
                    m = mm(bank(4)[:, k * 256:(k + 1) * 256], w(f"wk{s}"), w("ctxT"), start=True, stop=True)
                m.then_inc(sig["kT_mm"], 1)
                for b in range(B):
                    m = mm(bank(5)[:, b * C:(b + 1) * C], w("ctx2")[:, b * P:(b + 1) * P], w("wv2"),
                           start=True, stop=True)
                m.then_inc(sig["v_mm"], 1)
                for i in range(B + 3):
                    if i < B:
                        b = i
                        pe.wait_ge(sig["q0_soft"], b + 1)
                        if b >= 2:
                            pe.wait_ge(sig["q0T_set"], b - 1)
                        for j in range(2):
                            m = tr(bank(6 + b % 2)[:, j * P:(j + 1) * P], O[:, 2 * b + j, :], ident)
                        m.then_inc(sig["q0T_mm"], 1)
                    if 1 <= i <= B:
                        b = i - 1
                        pe.wait_ge(sig["q0T_set"], b + 1)
                        if b >= 2:
                            pe.wait_ge(sig["o_tok"], b - 1)
                        else:
                            pe.wait_ge(sig["q0_sub"], B)
                        for j in range(2):
                            m = mm(bank(2 + b % 2)[:, j * (C + H):(j + 1) * (C + H)],
                                   qT[:, (2 * b + j) * P:(2 * b + j + 1) * P], kvb[:, b, :], start=True, stop=True)
                        m.then_inc(sig["kvo_mm"], 1)
                    if 2 <= i <= B + 1:
                        o_transpose(0, i - 2)
                    if 3 <= i <= B + 2:
                        o_project(0, i - 3, w("wp0"), row0[0:1, 3, :])
                for b in range(B):
                    ln_T(1, b)

            def o_transpose(s, b):
                if s == 0:
                    pe.wait_ge(sig["o_tok"], b + 1)
                    if b == 0:
                        pe.wait_ge(sig["kT_set"], 1)
                    if b == 1:
                        pe.wait_ge(sig["v18_set"], B)
                    if b >= 2:
                        pe.wait_ge(sig["oT_set"], b - 1)
                else:
                    pe.wait_ge(sig["pv_out"], (s // 4) * NT + 2 * b + 2)
                    side_free(s, b)
                for j in range(2):
                    m = tr(bank(turn_bank(s + 0.5, b))[:, SIDE][:, j * P:(j + 1) * P], O[:, 2 * b + j, :], ident)
                m.then_inc(sig["oT_mm"], 1)

            def o_project(s, b, wo, bias=None):
                pe.wait_ge(sig["oT_set"], ATT.index(s) * B + b + 1)
                if s == 0 and b >= 2:
                    pe.wait_ge(sig["resid"], b - 1)
                for j in range(2):
                    o = bank(b % 2)[:, j * C:(j + 1) * C]
                    if bias is not None:
                        mm(o, ones[0:1, :], bias, start=True, stop=False)
                    m = mm(o, oT[:, (2 * b + j) * P:(2 * b + j + 1) * P], wo, start=bias is None, stop=True)
                m.then_inc(sig["out_ready"], 1)

            def router1():
                for hf in range(2):
                    for b in (2 * hf, 2 * hf + 1):
                        got_hT(1, b)
                        pe.wait_ge(sig["o_tok"], B)
                        for j in range(2):
                            i = 2 * (b % 2) + j
                            m = mm(bank(2 + hf)[:, i * E0:(i + 1) * E0], h(b, j), w("router0"), start=True, stop=True)
                    m.then_inc(sig["r1_mm"], 1)
                for hf in range(2):
                    pe.wait_ge(sig["sel_set"], hf + 1)
                    for j in range(4):
                        i = 4 * hf + j
                        o = bank(2 + hf)[:, 256 + j * E0:256 + (j + 1) * E0]
                        for k in range(i):
                            mm(o, ones[:], sel[:, k, :], start=(k == 0), stop=False)
                        m = mm(o, w("earlier"), sel[:, i, :], start=(i == 0), stop=True)
                    m.then_inc(sig["pos_mm"], 1)
                gates_transpose(0)

            def gates_transpose(hf):
                pe.wait_ge(sig["gg_set"], hf + 1)
                pe.wait_ge(sig["resid"], B)
                for j in range(4):
                    m = tr(bank(GT1[hf])[:, j * P:(j + 1) * P], GG[:, j, :], ident)
                m.then_inc(sig["ggT_mm"], 1)

            def experts1():
                w1 = [a.rearrange("p (m k) -> p m k", k=P) for a in (w1hi[:], low["moe0a"][:])]
                w2 = [a.rearrange("p (m k) -> p m k", k=C) for a in (w2hi[:], low["moe0b"][:])]
                pe.wait_ge(sig["spread_set"], len(CUT1) - 1)
                pe.wait_ge(sig["oT_set"], B)
                pe.wait_ge(sig["gT_set"], 1)

                def finish(hf):
                    pe.wait_ge(sig["acc_evac"], hf + 1)
                    pe.wait_ge(sig["v18_set"], 2 * B)
                    pe.wait_ge(sig["sim_ss"], 1)
                    if hf:
                        pe.wait_ge(sig["q_set"], 2)
                    for j in range(4):
                        m = tr(bank(hf)[:, j * P:(j + 1) * P], accS[:, hf, j * P:(j + 1) * P], ident)
                    m.then_inc(sig["out_ready"], 2)

                def three(o, wts_, m, hi, lo, first, last):
                    mm(o, wts_[0][:, m, :], hi, start=first, stop=False)
                    mm(o, wts_[0][:, m, :], lo, start=False, stop=False)
                    return mm(o, wts_[1][:, m, :], hi, start=False, stop=last)

                for i in range(2 * STEPS1 + LAG1):
                    if i < 2 * STEPS1:
                        hf, m = divmod(i, STEPS1)
                        t = slice(hf * HALF, (hf + 1) * HALF)
                        if i in CUT1[:-1]:
                            pe.wait_ge(sig["w_lo"], 2 * CUT1.index(i) + 2)
                        if m == 0:
                            pe.wait_ge(sig["hT_lo"], 2 * hf + 2)
                            pe.wait_ge(sig["gT_set"], hf + 1)
                        if i == 4:
                            gates_transpose(1)
                        if i == 8:
                            pe.wait_ge(sig["resid"], B)
                            for b in range(B):
                                q = mm(bank(0)[:, b * C:(b + 1) * C], w("ctx2")[:, b * P:(b + 1) * P], w("wv4"),
                                       start=True, stop=True)
                            q.then_inc(sig["v_mm"], 1)
                        if i == SIM1 - 4:
                            pe.wait_ge(sig["sim_sq"], 1)
                            pe.wait_ge(sig["gT_set"], 2)
                            mm(bank(1)[:, 0:E1], ones[:], simsq[:], start=True, stop=True).then_inc(sig["sim_mm"], 1)
                        if i >= 2:
                            pe.wait_ge(sig["h1"], i - 1)
                        three(bank(6 + i % 2), w1, m, hThi[:, t], hTlo[:, t], True, True).then_inc(sig["mA"], 1)
                        if m < GATED1:
                            if i >= 2:
                                pe.wait_ge(sig["hg"], i - 1)
                            mm(bank(4 + i % 2), spread64[:, m * P:(m + 1) * P], gT[:, t], start=True, stop=True)\
                                .then_inc(sig["mG"], 1)
                    if i >= LAG1:
                        v = i - LAG1
                        hf, m = divmod(v, STEPS1)
                        pe.wait_ge(sig["h_lo"], v + 1)
                        three(bank(2 + hf), w2, m, Hhi[v % 3], Hlo[v % 3], m == 0, m == STEPS1 - 1)\
                            .then_inc(sig["hg_used"], 1)
                    if i == STEPS1 + LAG1 + FIN:
                        finish(0)
                    if i in (STEPS1 + LAG1 + FIN + 7, STEPS1 + LAG1 + FIN + 8):
                        ln_T(2, i - STEPS1 - LAG1 - FIN - 7)
                    if i in (STEPS1 + LAG1 + FIN + 10, STEPS1 + LAG1 + FIN + 11):
                        queries(2, i - STEPS1 - LAG1 - FIN - 10)
                finish(1)

            def unit_scores(s, u):
                v = UBASE[s] + u
                t, k = divmod(u, 2)
                n = len(UBANK[s])
                if u >= n:
                    pe.wait_ge(sig["PT_set"], v - n + 1)
                lh = hT[:, t * P:(t + 1) * P] if s == 6 else qT[:, t * P:(t + 1) * P]
                mat = A6 if s == 6 else kblk[s]
                mm(bank(ubank(s, u)), lh, mat[:, t // 2, k * 512:(k + 1) * 512], start=True, stop=True)\
                    .then_inc(sig["sc_mm"], 1)

            def unit_transpose(s, u):
                v = UBASE[s] + u
                pe.wait_ge(sig["sc_norm"], u + 1) if s == 6 else pe.wait_ge(sig["sc_exp"], v + 1)
                for i in range(4):
                    m = tr(bank(ubank(s, u))[:, i * P:(i + 1) * P], S[:, u % 6, i * P:(i + 1) * P], ident)
                m.then_inc(sig["PT_mm"], 1)

            def attention(s):
                k = s // 4
                lag = LAG[s]
                for i in range(STEPS24):
                    if s == 2 and i in (4, 5):
                        ln_T(2, i - 2)
                    if s == 2 and i in (6, 7):
                        queries(2, i - 4)
                    if i < UNITS:
                        if i % 4 == 0:
                            pe.wait_ge(sig["kblk_set"], k * B + i // 4 + 1)
                            pe.wait_ge(sig["q_set"], k * B + i // 4 + 1)
                        unit_scores(s, i)
                    if lag <= i < UNITS + lag:
                        unit_transpose(s, i - lag)
                    if lag + 1 <= i < UNITS + lag + 1:
                        u = i - lag - 1
                        t, q = divmod(u, 2)
                        pe.wait_ge(sig["PT_set"], UBASE[s] + u + 1)
                        if u == 0:
                            pe.wait_ge(sig["acc_evac"], 2) if s == 2 else pe.wait_ge(sig["resid"], 4 * B)
                        if q == 0 and t >= 2:
                            pe.wait_ge(sig["pv_out"], k * NT + t - 1)
                        for c in range(4):
                            a = (4 * q + c) * 18
                            m = mm(bank(2 + t % 2)[:, a:a + 18], PT[:, u % 4, c * P:(c + 1) * P],
                                   v18[s][:, t // 2, a:a + 18], start=True, stop=True)
                        m.then_inc(sig["pv_mm"], 1)
                    if due(i, TURN_T) is not None:
                        ln_T(s + 1, due(i, TURN_T))
                    if i == UNITS + lag + 3:
                        logits(s + 1, 0)
                        logits(s + 1, 1)
                    if due(i, TURN_T + 2) == 2:
                        logits(s + 1, 2)
                    if due(i, TURN_O) is not None:
                        o_transpose(s, due(i, TURN_O))
                    if due(i, TURN_P) is not None:
                        o_project(s, due(i, TURN_P), w(f"wo{s}"))
                    if s == 4 and i == SETUP6:
                        keys6()
                    if s == 4 and i in AT6:
                        queries_keys6(AT6.index(i))

            def values3(p):
                pe.wait_ge(sig["vT_set"], p + 1)
                for j in range(4):
                    a = p * HALF + j * P
                    m = tr(bank(p)[:, j * D1:(j + 1) * D1], vT3[0:D1, a:a + P], ident[0:D1, 0:D1])
                m.then_inc(sig["v3_mm"], 1)

            def mixture3():
                pe.wait_ge(load["mixw"], 16)
                logits(3, B - 1).then_inc(sig["l3_mm"], 1)
                pe.wait_ge(sig["g3_set"], 1)
                pe.wait_ge(sig["oT_set"], 2 * B)
                for t in range(NT):
                    m = tr(bank(4 + t // 4)[0:64, (t % 4) * P:(t % 4 + 1) * P], G16[:, t, :], ident)
                    if t % 4 == 3:
                        m.then_inc(sig["g3T_mm"], 1)
                pe.wait_ge(sig["w3_lo"], 1)
                for i in range(UNITS3 + LAG1):
                    if i < UNITS3:
                        p, e = divmod(i, E1)
                        pe.wait_ge(sig["g3T_set"], 2) if i < 2 else pe.wait_ge(sig["xe_set"], i - 1)
                        mm(bank(4 + i % 2), rows32[:, e:e + 1].broadcast_to([64, P]), gT3[:, p * HALF:(p + 1) * HALF],
                           start=True, stop=True).then_inc(sig["bc_mm"], 1)
                    if i >= LAG1:
                        v = i - LAG1
                        p, e = divmod(v, E1)
                        pe.wait_ge(sig["xe_lo"], v + 1)
                        for o, a in ((bank(2 + p), e * 3 * D1), (bank(6 + p), e * 3 * D1 + 2 * D1)):
                            a = slice(a, a + P)
                            mm(o, qkv3hi[:, a], Hhi[v % 3], start=(e == 0), stop=False)
                            mm(o, qkv3hi[:, a], Hlo[v % 3], start=False, stop=False)
                            m = mm(o, qkv3lo[:, a], Hhi[v % 3], start=False, stop=(e == E1 - 1))
                        m.then_inc(sig["xe_used"], 1)
                        if v == E1 + 8:
                            values3(0)
                values3(1)
                for i in range(NT + 3):
                    if i < NT:
                        b, j = divmod(i, 2)
                        keys = (j + 1) * P
                        pe.wait_ge(sig["qk_set"], b // 2 + 1)
                        pe.wait_ge(sig["xe_set"], UNITS3)
                        if i >= 2:
                            pe.wait_ge(sig["s3_sub"], i - 1)
                        mm(bank(4 + i % 2)[:, 0:keys], qT3[0:D1, b, j * P:(j + 1) * P], kT3[0:D1, b, 0:keys],
                           start=True, stop=True).then_inc(sig["s3_mm"], 1)
                    if 2 <= i < NT + 2:
                        t = i - 2
                        j = t % 2
                        pe.wait_ge(sig["s3_norm"], t + 1)
                        if t >= 2:
                            pe.wait_ge(sig["PT3_set"], t - 1)
                        else:
                            pe.wait_ge(sig["vT_set"], 2)
                        for k in range(j + 1):
                            m = tr(bank(6 + t % 2)[:, k * P:(k + 1) * P], S3[:, t % 4, k * P:(k + 1) * P], ident)
                        m.then_inc(sig["PT3_mm"], 1)
                    if i >= 3:
                        t = i - 3
                        b, j = divmod(t, 2)
                        pe.wait_ge(sig["PT3_set"], t + 1)
                        pe.wait_ge(sig["v3_set"], b // 2 + 1)
                        if j == 0 and b < 2:
                            pe.wait_ge(sig["qk_set"], 2)
                        if j == 0 and b >= 2:
                            pe.wait_ge(sig["a3_set"], b - 1)
                        for k in range(j + 1):
                            m = mm(bank(2 + b % 2)[:, j * P:(j + 1) * P], v3d[:, b, k, :],
                                   PT3[:, t % 2, k * P:(k + 1) * P], start=(k == 0), stop=(k == j))
                        m.then_inc(sig["a3_mm"], 1)
                n = E1 // 4
                for i in range(B * n + 10):
                    b = due(i, 11)
                    if b is not None:
                        ln_T(4, b)
                    b = due(i, 13)
                    if b is not None:
                        queries(4, b)
                    if i < B * n:
                        b, k = divmod(i, n)
                        pe.wait_ge(sig["s3_sub"], NT) if i < 2 else pe.wait_ge(sig["mix_set"], i - 1)
                        for q in range(2):
                            p = 2 * k + q
                            m = mm(bank(4 + i % 2)[:, q * T:(q + 1) * T], pair16[:, p * P:(p + 1) * P],
                                   gT3[:, b * T:(b + 1) * T], start=True, stop=True)
                        m.then_inc(sig["bp_mm"], 1)
                    if 2 <= i < B * n + 2:
                        v = i - 2
                        b, k = divmod(v, n)
                        pe.wait_ge(sig["mix_set"], v + 1)
                        if k == 0:
                            if b < 2:
                                side_free(3, b)
                            pe.wait_ge(sig["a3_set"], B)
                        for q in range(2):
                            p = 2 * k + q
                            for j in range(2):
                                m = mm(bank(b)[:, j * C:(j + 1) * C],
                                       mixT[:, v % 4, q * T + j * P:q * T + (j + 1) * P],
                                       w("o3")[:, p * C:(p + 1) * C], start=(p == 0 and j == 0),
                                       stop=(p == E1 // 2 - 1), skip_group_check=True)
                        m.then_inc(sig["mix_used"], 1)

            def experts5():
                pe.wait_ge(load["moe2"], 16)
                logits(5, B - 1).then_inc(sig["r5_mm"], 1)
                for hh in range(len(AT6), H // 2):
                    queries_keys6(hh)
                setup6()
                for b in range(B):
                    pe.wait_ge(sig["d5_set"], 2 * b + 2)
                    if b == 0:
                        pe.wait_ge(sig["vo_set"], B * HK3)
                    for j in range(2):
                        t = 2 * b + j
                        m = mm(bank(4 + b)[:, 0:SL], hN[:, t, :], D5[:, t, :], start=(j == 0), stop=(j == 1))
                    m.then_inc(sig["xs_mm"], 1)

                def gates5(t):
                    pe.wait_ge(sig["dw5_set"], t + 1)
                    if t >= 2:
                        pe.wait_ge(sig["pt5_set"], t - 1)
                    for g, (a, z) in enumerate(GRP):
                        m = tr(bank(6 + t % 2)[0:(z - a) * CAP2, g * P:(g + 1) * P],
                               Dw5[:, t, a * CAP2:z * CAP2], ident)
                    m.then_inc(sig["pt5_mm"], 1)

                w1 = w("w1_0")[:, 0:E2 * HID2].rearrange("p (m k) -> p m k", k=P)
                w2 = w("w2_0")[:, 0:E2 * HID2].rearrange("p (m k) -> p m k", k=C)
                n = HID2 // P
                N = B * CAP2
                for pk in ("moe2a", "moe2b"):
                    pe.wait_ge(load[pk], 16)
                for i in range(E2 * n + 2):
                    if i < E2 * n:
                        e = i // n
                        pe.wait_ge(sig["xs_set"], B) if i < 2 else pe.wait_ge(sig["h5_set"], i - 1)
                        mm(bank(4 + i % 2)[:, 0:N], w1[:, i, :], XS5[:, e, :], start=True, stop=True)\
                            .then_inc(sig["h5_mm"], 1)
                    if i >= 2:
                        v = i - 2
                        e, k = divmod(v, n)
                        pe.wait_ge(sig["h5_set"], v + 1)
                        if k == 0:
                            pe.wait_ge(sig["d5_set"], NT) if e < 2 else pe.wait_ge(sig["yt_set"], e - 1)
                        mm(bank(2 + e % 2)[:, 0:N], w2[:, v, :], H5[:, v % 4, :], start=(k == 0),
                           stop=(k == n - 1)).then_inc(sig["h5_used"], 1)
                    if i >= GATES5 and i % 2 == 0 and i < GATES5 + 2 * NT:
                        gates5((i - GATES5) // 2)
                pe.wait_ge(sig["yt_set"], E2)
                for i in range(B + 1):
                    if i < B:
                        b = i
                        pe.wait_ge(sig["pt5_set"], NT) if b < 2 else pe.wait_ge(sig["y5_set"], b - 1)
                        for g, (a, z) in enumerate(GRP):
                            m = tr(bank(6 + b % 2)[0:(z - a) * CAP2, g * C:(g + 1) * C],
                                   YT5[:, b, a * CAP2:z * CAP2], ident)
                        m.then_inc(sig["y5T_mm"], 1)
                    if i >= 1:
                        b = i - 1
                        pe.wait_ge(sig["y5_set"], b + 1)
                        for j in range(2):
                            for g, (a, z) in enumerate(GRP):
                                r = slice(0, (z - a) * CAP2)
                                m = mm(bank(b)[:, j * C:(j + 1) * C], PT5[r, 2 * b + j, g * P:(g + 1) * P],
                                       Y5[r, b, g * C:(g + 1) * C], start=(g == 0), stop=(g == 2))
                        m.then_inc(sig["out_ready"], 1)

            def keys6():
                pe.wait_ge(load["gqa"], 16)
                for k in range(2):
                    m = mm(bank(4)[:, k * 256:(k + 1) * 256], w("wk6")[:, k * P:(k + 1) * P], w("ctxT"),
                           start=True, stop=True)
                m.then_inc(sig["kT6_mm"], 1)

            def queries_keys6(hh):
                pe.wait_ge(sig["kT6_set"], 1)
                if hh >= 2:
                    pe.wait_ge(sig["A6_set"], hh - 1)
                for i in range(2):
                    q = 2 * hh + i
                    g, r = q // R3, q % R3
                    G, gp = g // 2, g % 2
                    rr = slice(gp * D3, (gp + 1) * D3)
                    a = (G * R3 + r) * C
                    m = mm(bank(4 + hh % 2)[:, i * 256:(i + 1) * 256], w("wq6")[rr, a:a + C], kT6[rr, G, :],
                           start=True, stop=True)
                m.then_inc(sig["A6_mm"], 1)

            def setup6():
                for g in range(HK3):
                    if g >= 2:
                        pe.wait_ge(sig["vT6_set"], g - 1)
                    if g == 1:
                        pe.wait_ge(sig["r5_sub"], 1)
                    mm(bank(6 + g % 2), w("wv6")[:, g * P:(g + 1) * P], w("ctx2"), start=True, stop=True)\
                        .then_inc(sig["vT6_mm"], 1)
                pe.wait_ge(sig["sel5"], 1)
                for t in range(NT):
                    o = bank(2)[:, 256 + t * E2:256 + (t + 1) * E2]
                    if t % 2:
                        mm(o, ones[:], sel[:, t - 1, 0:E2], start=True, stop=False)
                    m = mm(o, w("earlier"), sel[:, t, 0:E2], start=(t % 2 == 0), stop=True)
                m.then_inc(sig["pos5"], 1)
                pe.wait_ge(sig["vT6_set"], HK3)
                for n in range(B * HK3):
                    b, g = divmod(n, HK3)
                    if n < 2:
                        pe.wait_ge(sig["A6_set"], H // 2)
                    if n >= 4:
                        pe.wait_ge(sig["vo_set"], n - 3)
                    mm(bank(4 + n % 4)[:, 0:256], vT6[:, g, b * P:(b + 1) * P],
                       w("wo6")[:, 2 * g * C:(2 * g + 2) * C], start=True, stop=True).then_inc(sig["vo_mm"], 1)

            def attention6():
                for b in range(B):
                    ln_T(6, b)
                lag = LAG[6]
                for i in range(UNITS + lag + 1):
                    b = due(i, LAG[6] + 8)
                    if b is not None:
                        ln_T(7, b)
                    if i < UNITS:
                        if i % 4 == 0:
                            got_hT(6, i // 4)
                        unit_scores(6, i)
                    if lag <= i < UNITS + lag:
                        unit_transpose(6, i - lag)
                    if i >= lag + 1:
                        u = i - lag - 1
                        t, q = divmod(u, 2)
                        b, j = divmod(t, 2)
                        pe.wait_ge(sig["PT_set"], UBASE[6] + u + 1)
                        if j == 0 and q == 0:
                            side_free(6, b)
                        for c in range(4):
                            m = mm(bank(b % 2)[:, j * C:(j + 1) * C], PT[:, u % 4, c * P:(c + 1) * P],
                                   VO6[:, b, 4 * q + c, :], start=(q == 0 and c == 0), stop=(q == 1 and c == 3))
                        m.then_inc(sig["pv_mm"], 1)
                    if i in EARLY7:
                        gate_up7(2 * EARLY7.index(i))
                        gate_up7(2 * EARLY7.index(i) + 1)

            def gate_up7(n):
                b, m = divmod(n, M3)
                if n == 0:
                    pe.wait_ge(sig["ints_cast"], 1)
                    pe.wait_ge(sig["PT_set"], UBASE[6] + 12)
                got_hT(7, b)
                if 2 <= n < 2 * M3:
                    pe.wait_ge(sig["h7_set"], n - 1)
                if n == 2 * M3:
                    pe.wait_ge(sig["PT_set"], UBASE[6] + UNITS)
                if n >= 2 * M3 + 4:
                    pe.wait_ge(sig["h7_set"], n - 3)
                k = bank7(n)
                mm(bank(k)[:, 0:T], w("wg")[:, m * P:(m + 1) * P], h(b), start=True, stop=True)
                mm(bank(k)[:, T:2 * T], w("wu")[:, m * P:(m + 1) * P], h(b), start=True, stop=True)\
                    .then_inc(sig["gu_mm"], 1)

            def down7(b):
                pe.wait_ge(sig["h7_set"], M3 * (b + 1))
                if b < 2:
                    side_free(7, b)
                else:
                    pe.wait_ge(sig["resid"], 7 * B + b - 1)
                for j in range(2):
                    for m in range(M3):
                        q = mm(bank(b % 2)[:, j * C:(j + 1) * C], H7[:, b % 2, m, j * P:(j + 1) * P],
                               w("wd")[:, m * C:(m + 1) * C], start=(m == 0), stop=(m == M3 - 1))
                q.then_inc(sig["out_ready"], 1)

            def mlp7():
                for n in range(2 * M3, 3 * M3):
                    gate_up7(n)
                down7(0)
                ln_T(7, B - 1)
                down7(1)
                for n in range(3 * M3, B * M3):
                    gate_up7(n)
                down7(2)
                down7(3)

            setup_kv0()
            attn0()
            router1()
            experts1()
            attention(2)
            mixture3()
            attention(4)
            experts5()
            attention6()
            mlp7()

        @block.scalar
        def _(act):
            A, copy = nc.scalar.activation, nc.scalar.copy

            def ln_out(s, b):
                act.wait_ge(sig["ln_T"], s * B + b + 1)
                if s == 1:
                    copy(hThi[:, b * 256:(b + 1) * 256], PS[:, turn_bank(s, b), SIDE]).then_inc(sig["hT_hi"], 1)
                copy(hT[:, b * 256:(b + 1) * 256], PS[:, turn_bank(s, b), SIDE]).then_inc(sig["hT"], 1)

            def q_out(s, b):
                act.wait_ge(sig["q_mm"], s // 4 * B + b + 1)
                copy(qT[:, b * 256:(b + 1) * 256], PS[:, b % 2, MAIN]).then_inc(sig["q_set"], 1)

            def o_out(s, b):
                act.wait_ge(sig["oT_mm"], ATT.index(s) * B + b + 1)
                copy(oT[:, b * 256:(b + 1) * 256], PS[:, turn_bank(s + 0.5, b), SIDE]).then_inc(sig["oT_set"], 1)

            def unit_out(s, u):
                v = UBASE[s] + u
                act.wait_ge(sig["PT_mm"], v + 1)
                if u >= 4:
                    act.wait_ge(sig["pv_mm"], v - 3)
                copy(PT[:, u % 4, :], PS[:, ubank(s, u), :]).then_inc(sig["PT_set"], 1)

            def a6_out(hh):
                act.wait_ge(sig["A6_mm"], hh + 1)
                for q in range(2):
                    m = copy(A6[:, :, (2 * hh + q) * KEYS:(2 * hh + q + 1) * KEYS],
                             PS[:, 4 + hh % 2, q * 256:(q + 1) * 256].rearrange("p (b k) -> p b k", b=B))
                m.then_inc(sig["A6_set"], 1)

            def silu7(n):
                act.wait_ge(sig["gu_mm"], n + 1)
                if n >= 3:
                    act.wait_ge(sig["h7_set"], n - 2)
                A(sg7[:, n % 3, :], PS[:, bank7(n), 0:T], ACT.Silu).then_inc(sig["silu7"], 1)

            def units(s):
                lag = LAG[s]
                for i in range(STEPS24 if s < 6 else UNITS + lag + 1):
                    if s == 2 and i in (4, 5):
                        ln_out(2, i - 2)
                    if s == 2 and i in (6, 7):
                        q_out(2, i - 4)
                    if lag <= i < UNITS + lag:
                        unit_out(s, i - lag)
                    if s < 6 and due(i, TURN_T) is not None:
                        ln_out(s + 1, due(i, TURN_T))
                    if s < 6 and due(i, TURN_O) is not None:
                        o_out(s, due(i, TURN_O))
                    if s == 4 and i == SETUP6:
                        act.wait_ge(sig["kT6_mm"], 1)
                        copy(kT6[:], PS[:, 4, :].rearrange("p (k n) -> p k n", k=2)).then_inc(sig["kT6_set"], 1)
                    if s == 4 and i in AT6:
                        a6_out(AT6.index(i))
                    if s == 6 and due(i, lag + 8) is not None:
                        ln_out(7, due(i, lag + 8))
                    if s == 2 and i == 8:
                        act.wait_ge(load["mixw"], 16)
                        copy(qkv3hi, w("qkv3")).then_inc(sig["w3_hi"], 1)
                    if s == 6 and i > UNITS + 1:
                        silu7(2 * (i - UNITS - 2))
                        silu7(2 * (i - UNITS - 2) + 1)
                    if i < UNITS:
                        act.wait_ge(sig["sc_sub"], UBASE[s] + i + 1)
                        A(S[:, i % 6, :], S[:, i % 6, :], ACT.Exp, scale=1.0 if s == 4 else SCALE[s])\
                            .then_inc(sig["sc_exp"], 1)

            def spread(k):
                a = E0 // 4
                if k == 0:
                    act.wait_ge(load["attn"], 16)
                copy(spread64[:].rearrange("p (e d) -> p e d", d=HID0)[:, k * a:(k + 1) * a, :],
                     w("half64")[:, k * a:(k + 1) * a].unsqueeze(2).broadcast_to([P, a, HID0]))\
                    .then_inc(sig["spread_set"], 1)

            def high_weights(k, j):
                pk, hi = (("moe0a", w1hi), ("moe0b", w2hi))[j]
                if k == 0:
                    act.wait_ge(load[pk], 16)
                a = slice(CUT1[k] * P, CUT1[k + 1] * P)
                copy(hi[:, a], ctx_in[pk][:, a]).then_inc(sig["w_hi"], 1)

            act.wait_ge(load["first"], 16)
            A(gain[:], w("gain"), ACT.Tanh).then_inc(sig["gain_set"], 1)
            for j in range(2):
                act.wait_ge(sig["k0_sub"], j + 1)
                A(kk[:, j, :], kk[:, j, :], ACT.Exp).then_inc(sig["k0_exp"], 1)
            for i in range(B + 1):
                if i < B:
                    ln_out(0, i)
                if i >= 1:
                    b = i - 1
                    act.wait_ge(sig["q0_sub"], b + 1)
                    A(O[:, 2 * b:2 * b + 2, :], O[:, 2 * b:2 * b + 2, :], ACT.Exp).then_inc(sig["q0_exp"], 1)
                    spread(b)
            act.wait_ge(sig["kT_mm"], 1)
            copy(kT[:], PS[:, 4, :].rearrange("p (k n) -> p k n", k=2)).then_inc(sig["kT_set"], 1)
            high_weights(0, 0)
            for i in range(B + 2):
                if i < B:
                    act.wait_ge(sig["q0T_mm"], i + 1)
                    copy(qT[:, i * 256:(i + 1) * 256], PS[:, 6 + i % 2, 0:256]).then_inc(sig["q0T_set"], 1)
                if i >= 2:
                    o_out(0, i - 2)
                if i < 5:
                    high_weights((i + 1) // 2, (i + 1) % 2)
            for b in range(B):
                ln_out(1, b)
            high_weights(3, 0)
            high_weights(3, 1)
            for hf in range(2):
                act.wait_ge(sig["r1_mm"], hf + 1)
                A(sc[:, 4 * hf:4 * hf + 4, :], PS[:, 2 + hf, 0:4 * E0].rearrange("p (j e) -> p j e", j=4), ACT.Exp,
                  scale=-1.0).then_inc(sig["r1_exp"], 1)
            act.wait_ge(load["mix"], 16)
            A(sgate[:], w("gates"), ACT.Exp, scale=-1.0).then_inc(sig["sg_exp"], 1)
            for i in range(2 * STEPS1 + 1):
                if i < 2 * STEPS1:
                    act.wait_ge(sig["mA"], i + 1)
                    if i >= 2:
                        act.wait_ge(sig["hg"], i - 1)
                    A(H1[:, i % 2, :], PS[:, 6 + i % 2, :], ACT.Gelu_apprx_tanh).then_inc(sig["h1"], 1)
                if i >= 1:
                    act.wait_ge(sig["hg"], i)
                    if i >= 4:
                        act.wait_ge(sig["hg_used"], i - 3)
                    copy(Hhi[(i - 1) % 3], Hg[:, (i - 1) % 2, :]).then_inc(sig["h_hi"], 1)
                if i in (STEPS1 + LAG1 + FIN + 7, STEPS1 + LAG1 + FIN + 8):
                    ln_out(2, i - STEPS1 - LAG1 - FIN - 7)
                if i in (STEPS1 + LAG1 + FIN + 10, STEPS1 + LAG1 + FIN + 11):
                    q_out(2, i - STEPS1 - LAG1 - FIN - 10)
                if i == STEPS1 + LAG1 or i == 2 * STEPS1:
                    hf = 0 if i == STEPS1 + LAG1 else 1
                    act.wait_ge(sig["hg_used"], (hf + 1) * STEPS1)
                    copy(accS[:, hf, :], PS[:, 2 + hf, :]).then_inc(sig["acc_evac"], 1)

            units(2)
            act.wait_ge(sig["l3_sub"], 1)
            A(lg[:], lg[:], ACT.Exp).then_inc(sig["l3_exp"], 1)
            for i in range(UNITS3 + LAG1 + 9):
                if i < UNITS3:
                    act.wait_ge(sig["xe_set"], i + 1)
                    if i >= 3:
                        act.wait_ge(sig["xe_used"], i - 2)
                    copy(Hhi[i % 3], XE[:, i % 2, :]).then_inc(sig["xe_hi"], 1)
                p, k = divmod(i - E1, E1)
                if p >= 0 and k == LAG1:
                    act.wait_ge(sig["xe_used"], (p + 1) * E1)
                    a = PS[:, 2 + p, :].rearrange("p (b t) -> p b t", b=2)
                    copy(vT3[0:D1, p * HALF:(p + 1) * HALF], PS[0:D1, 6 + p, :]).then_inc(sig["vT_set"], 1)
                    copy(qT3[0:D1, 2 * p:2 * p + 2, :], a[0:D1])
                    copy(kT3[0:D1, 2 * p:2 * p + 2, :], a[D1:2 * D1]).then_inc(sig["qk_set"], 1)
                if p >= 0 and k == LAG1 + 8:
                    act.wait_ge(sig["v3_mm"], p + 1)
                    a = PS[:, p, 0:4 * D1].rearrange("p (b j d) -> p b j d", b=2, j=2)
                    for q in range(2):
                        for b in range(2):
                            m = copy(v3d[:, 2 * p + b, :, q * D1:(q + 1) * D1], a[:, b])
                    m.then_inc(sig["v3_set"], 1)
            for i in range(NT + 2):
                if i >= 2:
                    t = i - 2
                    j = t % 2
                    act.wait_ge(sig["PT3_mm"], t + 1)
                    if t >= 2:
                        act.wait_ge(sig["a3_mm"], t - 1)
                    copy(PT3[:, t % 2, 0:(j + 1) * P], PS[:, 6 + t % 2, 0:(j + 1) * P]).then_inc(sig["PT3_set"], 1)
                if i < NT:
                    ks = (i % 2 + 1) * P
                    act.wait_ge(sig["s3_sub"], i + 1)
                    A(S3[:, i % 4, 0:ks], S3[:, i % 4, 0:ks], ACT.Exp, scale=D1 ** -0.5,
                      accum_out=s3[:, i % 4:i % 4 + 1]).then_inc(sig["s3_exp"], 1)
            for b in range(B):
                ln_out(4, b)
                q_out(4, b)
            units(4)
            act.wait_ge(sig["r5_sub"], 1)
            A(lg[:, :, 0:E2], lg[:, :, 0:E2], ACT.Exp).then_inc(sig["r5_exp"], 1)
            for hh in range(len(AT6), H // 2):
                a6_out(hh)
            for n in range(B * HK3):
                act.wait_ge(sig["vo_mm"], n + 1)
                g = n % HK3
                copy(VO6[:, n // HK3, 2 * g:2 * g + 2, :],
                     PS[:, 4 + n % 4, 0:256].rearrange("p (k c) -> p k c", k=2)).then_inc(sig["vo_set"], 1)
            for b in range(B):
                act.wait_ge(sig["xs_mm"], b + 1)
                copy(XS5[:, :, b * CAP2:(b + 1) * CAP2],
                     PS[:, 4 + b, 0:SL].rearrange("p (e s) -> p e s", e=E2)).then_inc(sig["xs_set"], 1)
            n = HID2 // P
            for i in range(E2 * n + 3):
                if i < E2 * n:
                    act.wait_ge(sig["h5_mm"], i + 1)
                    if i >= 4:
                        act.wait_ge(sig["h5_used"], i - 3)
                    A(H5[:, i % 4, :], PS[:, 4 + i % 2, 0:B * CAP2], ACT.Relu, bias=w("b1_2")[:, i:i + 1])\
                        .then_inc(sig["h5_set"], 1)
                if i > GATES5 and i % 2 == 1 and i < GATES5 + 2 * NT:
                    t = (i - GATES5) // 2
                    act.wait_ge(sig["pt5_mm"], t + 1)
                    copy(PT5[0:120, t, 0:2 * P], PS[0:120, 6 + t % 2, 0:2 * P])
                    copy(PT5[0:80, t, 2 * P:3 * P], PS[0:80, 6 + t % 2, 2 * P:3 * P]).then_inc(sig["pt5_set"], 1)
                if i >= 3 and (i - 3) % n == n - 1:
                    e = (i - 3) // n
                    act.wait_ge(sig["h5_used"], (e + 1) * n)
                    A(YT5[:, :, e * CAP2:(e + 1) * CAP2],
                      PS[:, 2 + e % 2, 0:B * CAP2].rearrange("p (b s) -> p b s", b=B), ACT.Identity,
                      bias=w("b2_2")[:, e:e + 1]).then_inc(sig["yt_set"], 1)
            for b in range(B):
                act.wait_ge(sig["y5T_mm"], b + 1)
                copy(Y5[0:120, b, 0:2 * C], PS[0:120, 6 + b % 2, 0:2 * C])
                copy(Y5[0:80, b, 2 * C:3 * C], PS[0:80, 6 + b % 2, 2 * C:3 * C]).then_inc(sig["y5_set"], 1)
            for b in range(B):
                ln_out(6, b)
            units(6)
            for n in range(2 * M3, 3 * M3):
                silu7(n)
            ln_out(7, B - 1)
            for n in range(3 * M3, B * M3):
                silu7(n)

        @block.vector
        def _(dve):
            tt, ts, stt = nc.vector.tensor_tensor, nc.vector.tensor_scalar, nc.vector.scalar_tensor_tensor
            cp, red_, rcp = nc.vector.tensor_copy, nc.vector.tensor_reduce, nc.vector.reciprocal
            chain = [0]

            def link(ins):
                chain[0] += 1
                ins.then_inc(sig["dve_step"], 1)
                dve.wait_ge(sig["dve_step"], chain[0])

            def over(a, k):
                return a.unsqueeze(len(a.shape)).broadcast_to(list(a.shape) + [k])

            def ln_stats(s, b):
                for j in range(2):
                    m = nc.vector.bn_stats(st[:, 2 * b + j, :], X[:, 2 * b + j, :])
                link(m)
                for j in range(2):
                    m = nc.vector.bn_aggr(mv[:, 2 * b + j, :], st[:, 2 * b + j, :])
                link(m)
                ts(vareps[:, 2 * b:2 * b + 2], mv[:, 2 * b:2 * b + 2, 1], EPS, None, ALU.add)\
                    .then_inc(sig["ln_var"], 1)

            def ln_norm(s, b):
                n = s * B + b
                dve.wait_ge(sig["ln_rstd"], n + 1)
                if s:
                    dve.wait_ge(sig["ln_T"], n - B + 1)
                for j in range(2):
                    t = 2 * b + j
                    ts(hN[:, t, :], X[:, t, :], mv[:, t, 0:1], rstd[:, t:t + 1], ALU.subtract, ALU.mult)\
                        .then_inc(sig["ln_h"], 1)
                if s == 3:
                    dve.wait_ge(sig["ln_h"], 2 * n + 2)
                    for j in range(2):
                        t = 2 * b + j
                        link(nc.vector.tensor_tensor_reduce(junk, hN[:, t, :], hN[:, t, :], 1.0, 0.0, ALU.mult,
                                                            ALU.add, ss[:, t:t + 1]))

            def residual(s, b, o=None, ready=None):
                if (s, b) == (0, 0):
                    dve.wait_ge(sig["gain_set"], 1)
                if ready is None:
                    dve.wait_ge(sig["out_ready"], OUT[s] + b + 1)
                else:
                    dve.wait_ge(sig[ready[0]], ready[1])
                x = w("x")[:, 2 * b * C:(2 * b + 2) * C]
                k = s // 2 + (0 if s % 2 == 0 else 4)
                stt(x, PS[:, obank(s, b), 0:2 * C] if o is None else o, gain[:, k:k + 1], x, ALU.mult, ALU.add)\
                    .then_inc(sig["resid"], 1)
                if s < 7:
                    dve.wait_ge(sig["resid"], s * B + b + 1)
                    ln_stats(s + 1, b)

            def residuals(s, ready=None):
                for i in range(B + 1):
                    if i < B:
                        residual(s, i, ready=None if ready is None else ready(i))
                    if i >= 1 and s < 7:
                        ln_norm(s + 1, i - 1)

            def setup_kv0():
                for j in range(2):
                    dve.wait_ge(sig["k0_mm"], j + 1)
                    kps = heads(PS[:, 6 + j, 0:C])
                    link(red_(red[:, j, 0:H], kps, AX.X, ALU.max))
                    cp(vv[:, j, 0:C], PS[:, 6 + j, C:2 * C])
                    tt(heads(kk[:, j, :]), kps, over(red[:, j, 0:H], D), ALU.subtract).then_inc(sig["k0_sub"], 1)
                for j in range(2):
                    dve.wait_ge(sig["k0_exp"], j + 1)
                    kv = heads(kk[:, j, :])
                    link(red_(red[:, j, 0:H], kv, AX.X, ALU.add))
                    link(rcp(red2[:, j, 0:H], red[:, j, 0:H]))
                    tt(kv, kv, over(red2[:, j, 0:H], D), ALU.mult).then_inc(sig["k0_soft"], 1)
                for b in range(B):
                    dve.wait_ge(sig["kv0_mm"], b + 1)
                    tt(heads(kvb[:, b, 0:C]), heads(PS[:, KV0[b], 0:C]), over(hm, D), ALU.mult)
                    ts(kvb[:, b, C:C + H], hm, PS[:, KV0[b], C:C + 1], None, ALU.mult).then_inc(sig["kvb_set"], 1)

            def values18(s):
                k = s // 4
                dve.wait_ge(sig["v_mm"], k + 1)
                for b in range(B):
                    o = v18[s][:, b, :].rearrange("p (k j d) -> p k j d", j=2, d=D + 1)
                    i = PS[:, 5 if s == 2 else 0, b * C:(b + 1) * C].rearrange("p (k j d) -> p k j d", j=2, d=D)
                    for j in range(2):
                        ts(o[:, :, j, 0:D], i[:, :, j, :], w("parity")[:, j:j + 1], None, ALU.mult)
                        m = ts(o[:, :, j, D], ones[:, 0:H // 2], w("parity")[:, j:j + 1], None, ALU.mult)
                    m.then_inc(sig["v18_set"], 1)

            def attn0():
                for i in range(B + 1):
                    if i < B:
                        b = i
                        dve.wait_ge(sig["q0_mm"], b + 1)
                        qps = heads(PS[:, 2 + b % 2, 0:256])
                        link(red_(red[:, b % 2, :], qps, AX.X, ALU.max))
                        tt(O[:, 2 * b:2 * b + 2, :].rearrange("p j (h d) -> p (j h) d", d=D), qps,
                           over(red[:, b % 2, :], D), ALU.subtract).then_inc(sig["q0_sub"], 1)
                    if i >= 1:
                        b = i - 1
                        q = O[:, 2 * b:2 * b + 2, :].rearrange("p j (h d) -> p (j h) d", d=D)
                        dve.wait_ge(sig["q0_exp"], b + 1)
                        link(red_(red2[:, b % 2, :], q, AX.X, ALU.add))
                        link(rcp(red2[:, b % 2, :], red2[:, b % 2, :]))
                        tt(q, q, over(red2[:, b % 2, :], D), ALU.mult).then_inc(sig["q0_soft"], 1)
                dve.wait_ge(sig["q0_soft"], B)
                values18(2)
                for b in range(B):
                    dve.wait_ge(sig["kvo_mm"], b + 1)
                    kvo = PS[:, 2 + b % 2, 0:2 * (C + H)].rearrange("p (j n) -> p j n", j=2)
                    r = red2[:, b % 2, :].rearrange("p (j h) -> p j h", j=2)
                    link(rcp(r, kvo[:, :, C:C + H]))
                    for j in range(2):
                        m = tt(heads(accS[:, 0, j * C:(j + 1) * C]), heads(kvo[:, j, 0:C]), over(r[:, j, :], D), ALU.mult)
                    link(m)
                    o = O[:, 2 * b:2 * b + 2, :].rearrange("p j c -> p (j c)")
                    tt(o, o, accS[:, 0, 0:2 * C], ALU.add).then_inc(sig["o_tok"], 1)
                    dve.wait_ge(sig["o_tok"], b + 1)
                residuals(0)

            def choose(hf):
                dve.wait_ge(sig["r1_exp"], hf + 1)
                tiles = slice(4 * hf, 4 * hf + 4)
                s_ = sc[:, tiles, :]
                link(ts(s_, s_, 1.0, None, ALU.add))
                link(rcp(s_, s_))
                link(tt(topin[:, :, 2:], s_, w("ebias0").unsqueeze(1).broadcast_to([P, 4, E0]), ALU.add))
                for j in range(4):
                    m = nc.vector.max(top8[:, j, :], topin[:, j, :])
                link(m)
                for j in range(4):
                    m = nc.vector.match_replace(rep[:, j, :], top8[:, j, :], topin[:, j, :], -BIG)
                link(m)
                ts(sel[:, tiles, :], rep[:, :, 2:], -BIG, None, ALU.is_equal).then_inc(sig["sel_set"], 1)
                dve.wait_ge(sig["sel_set"], hf + 1)

            def weigh(hf):
                tiles = slice(4 * hf, 4 * hf + 4)
                r = rs[:, 0:4, :]
                link(tt(wts[:], sc[:, tiles, :], sel[:, tiles, :], ALU.mult))
                link(red_(r, wts[:], AX.X, ALU.add))
                link(ts(r, r, 1e-20, None, ALU.add))
                link(rcp(r, r))
                link(tt(wts[:], wts[:], r.broadcast_to([P, 4, E0]), ALU.mult))
                dve.wait_ge(sig["pos_mm"], hf + 1)
                if hf:
                    dve.wait_ge(sig["ggT_mm"], hf)
                g = GG[:].rearrange("p j (k e) -> p j k e", k=2)
                pos = PS[:, 2 + hf, 256:512].rearrange("p (j e) -> p j e", j=4)
                link(stt(g[:, :, 0, :], pos, float(CAP0), wts[:], ALU.is_lt, ALU.mult))
                cp(g[:, :, 1, :], g[:, :, 0, :]).then_inc(sig["gg_set"], 1)

            def gates_out(hf):
                dve.wait_ge(sig["ggT_mm"], hf + 1)
                g = gT[:, hf * HALF:(hf + 1) * HALF]
                link(cp(g, PS[:, GT1[hf], :]))
                tt(g[64:128, :], PS[64:128, GT1[hf], :], g[64:128, :].bitcast(F32), ALU.subtract)\
                    .then_inc(sig["gT_set"], 1)

            def setup_mix():
                dve.wait_ge(load["mix"], 16)
                tt(simsq[:], w("sim"), w("sim"), ALU.mult).then_inc(sig["sim_sq"], 1)
                cp(rows32[:], w("half32")[0:64, :])

            def setup_mix_norms():
                dve.wait_ge(sig["sim_mm"], 1)
                ts(simss[:], PS[:, 1, 0:E1], 1e-24, None, ALU.max).then_inc(sig["sim_ss"], 1)
                dve.wait_ge(sig["sg_exp"], 1)
                link(ts(sgate[:], sgate[:], 1.0, None, ALU.add))
                link(rcp(sgate[:], sgate[:]))

            def setup_mix_end():
                dve.wait_ge(sig["sim_pw"], 1)
                tt(simn[:], w("sim"), siminv[:], ALU.mult).then_inc(sig["sim_set"], 1)
                cp(pair16[:].rearrange("p (e d) -> p e d", d=D1), over(w("half32")[0:64, :], D1))

            def experts1():
                for i in range(2 * STEPS1):
                    m = i % STEPS1
                    dve.wait_ge(sig["h1"], i + 1)
                    if i >= 2:
                        dve.wait_ge(sig["h_lo"], i - 1)
                    if m < GATED1:
                        dve.wait_ge(sig["mG"], i // STEPS1 * GATED1 + m + 1)
                        tt(Hg[:, i % 2, :], H1[:, i % 2, :], PS[:, 4 + i % 2, :], ALU.mult).then_inc(sig["hg"], 1)
                    else:
                        cp(Hg[:, i % 2, :], H1[:, i % 2, :]).then_inc(sig["hg"], 1)
                    if i == 1:
                        weigh(1)
                    if i == 5:
                        gates_out(1)
                    if i == 7:
                        setup_mix()
                    if i == 10:
                        values18(4)
                    if i == SIM1 - 3:
                        setup_mix_norms()
                    if i == STEPS1 + 4 + FIN:
                        half_out(0)
                    if i == STEPS1 + 5 + FIN:
                        half_out(1)
                    if i in (STEPS1 + 7 + FIN, STEPS1 + 8 + FIN):
                        ln_norm(2, i - STEPS1 - 7 - FIN)

            def half_out(b):
                residual(1, b, PS[:, b // 2, (b % 2) * 256:(b % 2 + 1) * 256], ("out_ready", OUT[1] + b // 2 * 2 + 2))

            def normalise(s, t):
                k = s // 4
                dve.wait_ge(sig["pv_mm"], UBASE[s] + 2 * t + 2)
                pv = heads(PS[:, 2 + t % 2, 0:H * (D + 1)], D + 1)
                link(rcp(rden[:, t % 2, :], pv[:, :, D]))
                tt(heads(O[:, t, :]), pv[:, :, 0:D], over(rden[:, t % 2, :], D), ALU.mult).then_inc(sig["pv_out"], 1)

            def unit_front(s, u):
                v = UBASE[s] + u
                t, q = divmod(u, 2)
                dve.wait_ge(sig["sc_mm"], v + 1)
                if u >= 6:
                    dve.wait_ge(sig["PT_mm"], v - 5)
                i, o = heads(PS[:, ubank(s, u), :], KEYS), heads(S[:, u % 6, :], KEYS)
                if s == 4:
                    e = w("mask")[:, t // 2 * KEYS:(t // 2 + 1) * KEYS].unsqueeze(1).broadcast_to([P, H // 2, KEYS])
                    link(stt(o, i, SCALE[4], e, ALU.mult, ALU.add))
                    i = o
                link(red_(smax[:, u % 2, :], i, AX.X, ALU.max))
                tt(o, i, over(smax[:, u % 2, :], KEYS), ALU.subtract).then_inc(sig["sc_sub"], 1)

            def attention(s):
                if s == 4:
                    dve.wait_ge(sig["ints_cast"], 1)
                lag = LAG[s] + 3
                for i in range(STEPS24):
                    if i < UNITS:
                        unit_front(s, i)
                    if s == 2 and i in (0, 1):
                        half_out(2 + i)
                    if s == 2 and i in (2, 3):
                        ln_norm(2, i)
                    if s == 2 and i == UNITS - 2:
                        setup_mix_end()
                    if lag <= i < UNITS + lag and (i - lag) % 2:
                        normalise(s, (i - lag) // 2)
                    if due(i, TURN_N) is not None:
                        ln_norm(s + 1, due(i, TURN_N))
                    if due(i, TURN_R) is not None:
                        residual(s, due(i, TURN_R))

            def logits3():
                link(ts(ss[:], ss[:], 1e-24, None, ALU.max))
                ts(ss[:], ss[:], 1.0, None, ALU.mult).then_inc(sig["ss_set"], 1)
                dve.wait_ge(sig["l3_mm"], 1)
                dve.wait_ge(sig["ss_pw"], 1)
                l = PS[:, LBANK, 0:NT * E1].rearrange("p (t e) -> p t e", t=NT)
                link(tt(lg[:], l, over(rn[:], E1), ALU.mult))
                link(tt(lg[:], lg[:], sgate[:].unsqueeze(1).broadcast_to([P, NT, E1]), ALU.subtract))
                link(cp(topin2[:, :, 6:], lg[:]))
                for t in range(NT):
                    m = nc.vector.max(top8[:, t, :], topin2[:, t, :])
                ts(on[:], lg[:], 0.0, None, ALU.is_gt)
                link(m)
                for t in range(NT):
                    m = nc.vector.match_replace(rep2[:, t, :], top8[:, t, :], topin2[:, t, :], -BIG)
                link(red_(cnt[:], lg[:], AX.X, ALU.max))
                link(ts(fb[:], rep2[:, :, 6:], -BIG, None, ALU.is_equal))
                link(ts(cnt[:], cnt[:], 0.0, None, ALU.is_le))
                link(tt(fb[:], fb[:], cnt[:].broadcast_to([P, NT, E1]), ALU.mult))
                link(tt(on[:], on[:], fb[:], ALU.max))
                link(ts(lg[:], lg[:], 0.0, None, ALU.max))
                link(red_(cnt[:], lg[:], AX.X, ALU.max))
                tt(lg[:], lg[:], cnt[:].broadcast_to([P, NT, E1]), ALU.subtract).then_inc(sig["l3_sub"], 1)
                dve.wait_ge(sig["l3_exp"], 1)
                link(tt(lg[:], lg[:], on[:], ALU.mult))
                link(red_(cnt[:], lg[:], AX.X, ALU.add))
                link(rcp(cnt[:], cnt[:]))
                for k in range(2):
                    m = tt(G16[:, :, 32 * k:32 * k + E1], lg[:], cnt[:].broadcast_to([P, NT, E1]), ALU.mult)
                m.then_inc(sig["g3_set"], 1)

            def mixture3():
                logits3()
                for k in range(2):
                    dve.wait_ge(sig["g3T_mm"], k + 1)
                    g = gT3[:, k * 512:(k + 1) * 512]
                    link(cp(g, PS[0:64, 4 + k, :]))
                    tt(g[32:64, :], PS[32:64, 4 + k, :], g[32:64, :].bitcast(F32), ALU.subtract)\
                        .then_inc(sig["g3T_set"], 1)
                for i in range(UNITS3):
                    p = i // E1
                    dve.wait_ge(sig["bc_mm"], i + 1)
                    if i >= 2:
                        dve.wait_ge(sig["xe_lo"], i - 1)
                    tt(XE[:, i % 2, :], PS[:, 4 + i % 2, :], hT[:, p * HALF:(p + 1) * HALF], ALU.mult)\
                        .then_inc(sig["xe_set"], 1)
                for i in range(NT + 1):
                    if i < NT:
                        j = i % 2
                        ks = (j + 1) * P
                        x = S3[:, i % 4, 0:ks]
                        dve.wait_ge(sig["s3_mm"], i + 1)
                        if i >= 4:
                            dve.wait_ge(sig["PT3_mm"], i - 3)
                        a = P if j == 0 else 0
                        link(tt(x, PS[:, 4 + i % 2, 0:ks], w("causal")[:, a:a + ks], ALU.add))
                        link(red_(m3[:, i % 4:i % 4 + 1], x, AX.X, ALU.max))
                        ts(x, x, m3[:, i % 4:i % 4 + 1], None, ALU.subtract).then_inc(sig["s3_sub"], 1)
                    if i >= 1:
                        t = i - 1
                        ks = (t % 2 + 1) * P
                        dve.wait_ge(sig["s3_exp"], t + 1)
                        link(rcp(m3[:, t % 4:t % 4 + 1], s3[:, t % 4:t % 4 + 1]))
                        ts(S3[:, t % 4, 0:ks], S3[:, t % 4, 0:ks], m3[:, t % 4:t % 4 + 1], None, ALU.mult)\
                            .then_inc(sig["s3_norm"], 1)
                for b in range(B):
                    dve.wait_ge(sig["a3_mm"], 2 * b + 2)
                    cp(aT3[:, b, :], PS[:, 2 + b % 2, 0:T]).then_inc(sig["a3_set"], 1)
                dve.wait_ge(sig["a3_set"], B)
                n = E1 // 4
                for i in range(B * n + 6):
                    if i < B * n:
                        b = i // n
                        dve.wait_ge(sig["bp_mm"], i + 1)
                        if i >= 4:
                            dve.wait_ge(sig["mix_used"], i - 3)
                        ab = aT3[:, b, :].unsqueeze(1).broadcast_to([P, 2, T])
                        tt(heads(mixT[:, i % 4, :], T), heads(PS[:, 4 + i % 2, :], T), ab, ALU.mult)\
                            .then_inc(sig["mix_set"], 1)
                    b = due(i, n + 3)
                    if b is not None:
                        residual(3, b, ready=("mix_used", (b + 1) * n))
                    b = due(i, n + 5)
                    if b is not None:
                        ln_norm(4, b)

            def router5():
                dve.wait_ge(sig["r5_mm"], 1)
                l8 = lg[:, :, 0:E2]
                lps = PS[:, LBANK, 0:NT * E2].rearrange("p (t e) -> p t e", t=NT)
                link(red_(rs[:], lps, AX.X, ALU.max))
                tt(l8, lps, rs[:].broadcast_to([P, NT, E2]), ALU.subtract).then_inc(sig["r5_sub"], 1)
                dve.wait_ge(sig["r5_exp"], 1)
                link(red_(rs[:], l8, AX.X, ALU.add))
                link(rcp(rs[:], rs[:]))
                link(tt(l8, l8, rs[:].broadcast_to([P, NT, E2]), ALU.mult))
                link(cp(topin2[:, :, 6:6 + E2], l8))
                for t in range(NT):
                    m = nc.vector.max(top8[:, t, :], topin2[:, t, 0:6 + E2])
                link(m)
                for t in range(NT):
                    m = nc.vector.match_replace(rep2[:, t, 0:6 + E2], top8[:, t, :], topin2[:, t, 0:6 + E2], -BIG)
                link(m)
                ts(sel[:, :, 0:E2], rep2[:, :, 6:6 + E2], -BIG, None, ALU.is_equal).then_inc(sig["sel5"], 1)
                for g in range(HK3):
                    dve.wait_ge(sig["vT6_mm"], g + 1)
                    o = vT6[:, g, :].rearrange("p (b j k) -> p b j k", j=2, k=KEYS)
                    i = PS[:, 6 + g % 2, :].rearrange("p (b j k) -> p b j k", j=2, k=KEYS)
                    for j in range(2):
                        m = ts(o[:, :, j, :], i[:, :, j, :], w("parity")[:, j:j + 1], None, ALU.mult)
                    m.then_inc(sig["vT6_set"], 1)
                dve.wait_ge(sig["pos5"], 1)
                dve.wait_ge(sig["sel5"], 1)
                pos = PS[:, 2, 256:256 + NT * E2].rearrange("p (t e) -> p t e", t=NT)
                link(stt(fb[:, :, 0:E2], sel[:, :, 0:E2], -1000.0, pos, ALU.mult, ALU.add))
                for t in range(NT):
                    tt(heads(D5[:, t, :], CAP2), over(fb[:, t, 0:E2], CAP2),
                       w("slots2").unsqueeze(1).broadcast_to([P, E2, CAP2]), ALU.is_equal).then_inc(sig["d5_set"], 1)
                for t in range(NT):
                    if t == 0:
                        dve.wait_ge(sig["d5_set"], NT)
                    tt(heads(Dw5[:, t, :], CAP2), heads(D5[:, t, :], CAP2), over(lg[:, t, 0:E2], CAP2), ALU.mult)\
                        .then_inc(sig["dw5_set"], 1)

            def attention6():
                lag = 2
                for i in range(UNITS + LAG[6] + 3):
                    if i < UNITS:
                        unit_front(6, i)
                    if lag <= i < UNITS + lag:
                        u = i - lag
                        dve.wait_ge(sig["sc_exp"], UBASE[6] + u + 1)
                        if u >= 2:
                            dve.wait_ge(sig["sc_norm"], u - 1)
                        link(red_(rden[:, u % 2, 0:H // 2], heads(S[:, u % 6, :], KEYS), AX.X, ALU.add))
                        rcp(ssum[:, u % 2, :], rden[:, u % 2, 0:H // 2]).then_inc(sig["sc_sum"], 1)
                    if UNITS + 3 <= i < UNITS + 6:
                        hidden7(2 * (i - UNITS - 3))
                        hidden7(2 * (i - UNITS - 3) + 1)
                    b = i - LAG[6] - 5
                    if b >= 0 and b % 4 == 0:
                        residual(6, b // 4, ready=("pv_mm", UBASE[6] + b + 4))
                    if b >= 1 and (b - 1) % 4 == 0:
                        ln_norm(7, (b - 1) // 4)

            def hidden7(n):
                b, m = divmod(n, M3)
                dve.wait_ge(sig["silu7"], n + 1)
                if m == 0 and b >= 2:
                    dve.wait_ge(sig["out_ready"], OUT[7] + b - 1)
                tt(H7[:, b % 2, m, :], sg7[:, n % 3, :], PS[:, bank7(n), T:2 * T], ALU.mult)\
                    .then_inc(sig["h7_set"], 1)

            def mlp7():
                for n in range(2 * M3, 3 * M3):
                    hidden7(n)
                residual(7, 0)
                residual(7, 1)
                for n in range(3 * M3, B * M3):
                    hidden7(n)
                residual(7, 2)
                residual(7, 3)

            nc.vector.memset(ones[:], 1.0)
            nc.vector.memset(vv[:, :, C:C + 1], 1.0)
            nc.vector.memset(topin[:, :, 0:2], BIG)
            nc.vector.memset(topin2[:, :, 0:6], BIG)
            nc.vector.memset(G16[:], 0.0).then_inc(sig["consts"], 1)
            dve.wait_ge(sig["consts"], 1)
            dve.wait_ge(load["first"], 16)
            ln_stats(0, 0)
            ln_stats(0, 1)
            ln_norm(0, 0)
            setup_kv0()
            for b in range(1, B):
                if b + 1 < B:
                    ln_stats(0, b + 1)
                ln_norm(0, b)
            attn0()
            choose(0)
            choose(1)
            weigh(0)
            gates_out(0)
            experts1()
            attention(2)
            mixture3()
            attention(4)
            router5()
            residuals(5)
            attention6()
            mlp7()


def layout(i):
    f = {k: np.asarray(v) for k, v in i.items()}

    def rows(a, n=P):
        return np.broadcast_to(a.reshape(1, -1), (n, a.size))

    def tiles(a):
        return a.reshape(-1, P, a.shape[-1]).transpose(1, 0, 2).reshape(P, -1)

    def first_rows(parts):
        a = np.zeros((P, len(parts) * C), np.float32)
        for k, v in enumerate(parts):
            a[0, k * C:k * C + v.size] = v
        return a

    p = np.arange(P)
    ctx = f["ctx_1024"].reshape(B * KEYS, C).T
    ctx2 = np.repeat(ctx.reshape(C, B, 1, KEYS), 2, axis=2).reshape(C, -1)
    half32 = ((p[:, None] % 32 == np.arange(E1)) & (p[:, None] < 64)).astype(np.float32)
    cols = np.arange(T)
    wq6 = f["L3_xattn_Wq"].reshape(2, 2, R3, D3, C).transpose(1, 3, 0, 2, 4).reshape(P, -1)
    qkv3 = np.concatenate([f["L1_ffn_q_proj"], f["L1_ffn_k_proj"], f["L1_ffn_v_proj"]], axis=2)
    a = {
        "x": tiles(f["x"].reshape(B * T, C)), "ctxT": ctx, "ctx2": ctx2,
        "wq0": f["L0_xattn_Wq"].T, "wkv0": np.concatenate([f["L0_xattn_Wk"].T, f["L0_xattn_Wv"].T], axis=1),
        "wp0": f["L0_xattn_Wp"].T,
        "rows0": first_rows([f["L0_xattn_bq"], f["L0_xattn_bk"], f["L0_xattn_bv"], f["L0_xattn_bp"], f["L2_ffn_br"]]),
        "ident": np.eye(P, dtype=np.float32), "headmask": (p[:, None] // D == np.arange(H)).astype(np.float32),
        "gain": np.concatenate([rows(f["g_xattn"]), rows(f["g_ffn"])], axis=1),
        "router0": f["L0_ffn_router_weight"].T, "ebias0": rows(f["L0_ffn_expert_bias"]),
        "earlier": (p[:, None] < p).astype(np.float32), "half64": (p[:, None] % E0 == np.arange(E0)).astype(np.float32),
        "wq2": f["L1_xattn_w_q"].T, "wk2": f["L1_xattn_w_k"].T, "wv2": f["L1_xattn_w_v"].T, "wo2": f["L1_xattn_w_o"].T,
        "wq4": f["L2_xattn_Wq"], "wk4": f["L2_xattn_Wk"], "wv4": f["L2_xattn_Wv"], "wo4": f["L2_xattn_Wo"],
        "parity": (p[:, None] // KEYS == np.arange(2)).astype(np.float32),
        "w1_0": np.concatenate([f["L0_ffn_w1"].transpose(1, 0, 2).reshape(C, -1), f["L0_ffn_sw1"].T], axis=1),
        "w2_0": np.concatenate([tiles(f["L0_ffn_w2"].reshape(-1, C)), tiles(f["L0_ffn_sw2"].T)], axis=1),
        "half32": half32, "sim": f["L1_ffn_sim_matrix"], "gates": rows(f["L1_ffn_gates"]),
        "qkv3": np.concatenate([qkv3.transpose(1, 0, 2).reshape(C, -1), qkv3[0, :, 0:D1]], axis=1),
        "o3": tiles(f["L1_ffn_o_proj"].reshape(-1, C)),
        "causal": np.where(cols[None, :] <= P + p[:, None], 0.0, -BIG).astype(np.float32),
        "router2": f["L2_ffn_Wr"], "b1_2": f["L2_ffn_b1"].reshape(-1, P).T, "b2_2": f["L2_ffn_b2"].T,
        "slots2": rows(np.arange(CAP2, dtype=np.float32) - 1000),
        "moe2a": f["L2_ffn_W1"].transpose(1, 0, 2).reshape(C, -1), "moe2b": tiles(f["L2_ffn_W2"].reshape(-1, C)),
        "wq6": wq6, "wk6": f["L3_xattn_Wk"].T,
        "wv6": np.repeat(f["L3_xattn_Wv"].T.reshape(C, HK3, 1, D3), 2, axis=2).reshape(C, -1),
        "wo6": tiles(f["L3_xattn_Wo"].T),
        "mask": rows(f["mask_BxS2_ik0"]), "wg": f["L3_ffn_w_gate"].T, "wu": f["L3_ffn_w_up"].T,
        "wd": tiles(f["L3_ffn_w_down"].T),
    }
    packs = {"p_" + k: np.ascontiguousarray(np.concatenate([a[n] for n, _ in v], axis=1)) for k, v in PACKS.items()}
    for k in LATER:
        packs["p_" + k] = np.ascontiguousarray(a[k])
    packs["p_mixw"] = np.ascontiguousarray(np.concatenate([a[n] for n, _ in MIXW], axis=1))
    packs["p_gqa"] = np.ascontiguousarray(np.concatenate([a[n] for n, _ in GQA], axis=1))
    packs["p_ints"] = np.ascontiguousarray(np.concatenate([a[n] for n, _ in IPACK], axis=1))
    return packs


def kernel(**inputs):
    import concourse.bacc as bacc
    from concourse.bass_utils import run_bass_kernel_spmd

    nc = bacc.Bacc("TRN2", target_bir_lowering=False, num_devices=1)
    arrays = layout(inputs)
    aps = {k: nc.dram_tensor(k, a.shape, mybir.dt.from_np(a.dtype), kind="ExternalInput").ap()
           for k, a in arrays.items()}
    out = nc.dram_tensor("out", (P, NT * C), F32, kind="ExternalOutput").ap()
    flamingo_blocks(nc, {k[2:]: v for k, v in aps.items()}, aps["p_ints"], out)
    r = run_bass_kernel_spmd(nc, [arrays], core_ids=[0])
    y = r.results[0]["out"]
    return y.reshape(P, NT, C).transpose(1, 0, 2).reshape(B, T, C)
```
